# Optimizing a Trainium2 kernel written in Bass

```python
import numpy as np
import jax
import jax.numpy as jnp

def _softmax(x, axis=-1):
    return jax.nn.softmax(x, axis=axis)

def _gelu(x):
    return jax.nn.gelu(x, approximate=True)

def _silu(x):
    return jax.nn.silu(x)

def _sigmoid(x):
    return jax.nn.sigmoid(x)

def _layernorm(x, axis=-1, eps=1e-05):
    m = jnp.mean(x, axis=axis, keepdims=True)
    v = jnp.var(x, axis=axis, keepdims=True)
    return (x - m) / jnp.sqrt(v + eps)

def _scatter_add(tgt, idx, src, axis=0):
    return tgt.at[idx].add(src)

def _segment_sum(src, seg, n):
    return jax.ops.segment_sum(src, seg, n)
kernel_name = 'mk_xattn_ffn_d1_seqx_r4_37f224'

def setup_inputs(seed: int=0):
    np.random.seed(seed)
    _w = jnp.asarray

    def _rec_inputs():
        import jax
        import jax.numpy as jnp
        _rk = jax.random.key(seed)
        x = 4.136e-05 + 0.9999 * jax.random.normal(jax.random.fold_in(_rk, 1), (4, 512, 512), jnp.float32)
        _lenS = 512 - jax.random.randint(jax.random.fold_in(_rk, 7), (4,), 0, max(1, 512 // 4) + 1, jnp.int32)
        _lenS2 = 512 - jax.random.randint(jax.random.fold_in(_rk, 8), (4,), 0, max(1, 512 // 4) + 1, jnp.int32)
        _ctx_1024P = jax.random.normal(jax.random.fold_in(_rk, 11), (4, 16, 256), jnp.float32)
        _ctx_1024c = jax.random.dirichlet(jax.random.fold_in(_rk, 511), 0.3 * jnp.ones((16,), jnp.float32), (4, 512))
        _ctx_1024t = jnp.einsum('bsk,bkd->bsd', _ctx_1024c, _ctx_1024P)
        _ctx_1024t = _ctx_1024t * jax.lax.rsqrt(jnp.mean(jnp.square(_ctx_1024t)) + 1e-12) * 0.953939
        ctx_1024 = -0.000292821 + 1.00034 * (_ctx_1024t + 0.3 * jax.random.normal(jax.random.fold_in(_rk, 611), (4, 512, 256), jnp.float32))
        return (x, ctx_1024)
    x, ctx_1024 = _rec_inputs()

    def _L0_xattn_setup():
        import jax, jax.numpy as jnp
        import numpy as np
        import math
        B, L, DM = (2, 512, 256)
        DS, DC, EXP = (16, 4, 2)
        DI = EXP * DM
        DR = math.ceil(DM / 16)
        DT_MIN, DT_MAX, DT_FLOOR = (0.001, 0.1, 0.0001)

        def _ssm_forward(hidden_states, z, in_proj_w, conv_w, conv_b, x_proj_w, dt_proj_w, dt_proj_b, A_log, D):
            b = hidden_states.shape[0]
            x = jnp.einsum('ed,bld->bel', in_proj_w, hidden_states)
            xp = jnp.pad(x, ((0, 0), (0, 0), (DC - 1, 0)))
            xc = jax.lax.conv_general_dilated(xp, conv_w[:, None, :], window_strides=(1,), padding='VALID', dimension_numbers=('NCH', 'OIH', 'NCH'), feature_group_count=DI)
            u = jax.nn.silu(xc + conv_b[None, :, None])
            x_dbl = jnp.einsum('ke,bel->bkl', x_proj_w, u)
            dt_lo = x_dbl[:, :DR]
            Bm = x_dbl[:, DR:DR + DS]
            Cm = x_dbl[:, DR + DS:]
            delta = jax.nn.softplus(jnp.einsum('er,brl->bel', dt_proj_w, dt_lo) + dt_proj_b[None, :, None])
            A = -jnp.exp(A_log)

            def step(state, xs):
                d_t, B_t, C_t, u_t = xs
                dA = jnp.exp(d_t[..., None] * A)
                state = state * dA + (d_t * u_t)[..., None] * B_t[:, None, :]
                y_t = jnp.einsum('ben,bn->be', state, C_t)
                return (state, y_t)
            xs = (jnp.moveaxis(delta, -1, 0), jnp.moveaxis(Bm, -1, 0), jnp.moveaxis(Cm, -1, 0), jnp.moveaxis(u, -1, 0))
            state0 = jnp.zeros((b, DI, DS), delta.dtype)
            _, ys = jax.lax.scan(step, state0, xs)
            y = jnp.moveaxis(ys, 0, -1)
            y = y + D[None, :, None] * u
            y = y * jax.nn.silu(z)
            return jnp.swapaxes(y, 1, 2)
        key = jax.random.key(seed)
        ks = jax.random.split(key, 8)
        hidden_states = jax.random.normal(ks[0], (B, L, DM), jnp.float32)
        z = jax.random.normal(ks[1], (B, DI, L), jnp.float32)
        in_proj_w = jax.random.normal(ks[2], (DI, DM), jnp.float32) * DM ** (-0.5)
        conv_w = jax.random.normal(ks[3], (DI, DC), jnp.float32) * DC ** (-0.5)
        conv_b = jnp.zeros((DI,), jnp.float32)
        x_proj_w = jax.random.normal(ks[4], (DR + 2 * DS, DI), jnp.float32) * DI ** (-0.5)
        dt_std = DR ** (-0.5)
        dt_proj_w = jax.random.uniform(ks[5], (DI, DR), jnp.float32, -dt_std, dt_std)
        dt = jnp.exp(jax.random.uniform(ks[6], (DI,), jnp.float32) * (math.log(DT_MAX) - math.log(DT_MIN)) + math.log(DT_MIN))
        dt = jnp.clip(dt, DT_FLOOR)
        dt_proj_b = dt + jnp.log(-jnp.expm1(-dt))
        A_log = jnp.log(jnp.broadcast_to(jnp.arange(1, DS + 1, dtype=jnp.float32), (DI, DS)))
        D = jnp.ones((DI,), jnp.float32)
        return dict(hidden_states=hidden_states, z=z, in_proj_w=in_proj_w, conv_w=conv_w, conv_b=conv_b, x_proj_w=x_proj_w, dt_proj_w=dt_proj_w, dt_proj_b=dt_proj_b, A_log=A_log, D=D)
    _L0_xattn_all = _L0_xattn_setup()
    _L0_xattn_in = {k: v for k, v in _L0_xattn_all.items() if k in ('in_proj_w', 'conv_w', 'conv_b', 'x_proj_w', 'dt_proj_w', 'dt_proj_b', 'A_log', 'D')}
    del _L0_xattn_all

    def _L0_ffn_setup():
        import jax, jax.numpy as jnp
        import numpy as np
        NUM_EXPERTS = 8
        TOP_K = 2
        EMB = 512
        MLP = 1024
        B, S = (4, 256)
        key = jax.random.key(seed)
        ks = jax.random.split(key, 5)
        scale_x = 1.0
        return {'x': jax.random.normal(ks[0], (B, S, EMB), dtype=jnp.float32), 'gate_kernel': jax.random.normal(ks[1], (EMB, NUM_EXPERTS), dtype=jnp.float32) / np.sqrt(EMB), 'w0_kernel': jax.random.normal(ks[2], (NUM_EXPERTS, EMB, MLP), dtype=jnp.float32) / np.sqrt(EMB), 'w1_kernel': jax.random.normal(ks[3], (NUM_EXPERTS, EMB, MLP), dtype=jnp.float32) / np.sqrt(EMB), 'wo_kernel': jax.random.normal(ks[4], (NUM_EXPERTS, MLP, EMB), dtype=jnp.float32) / np.sqrt(MLP)}
    _L0_ffn_all = _L0_ffn_setup()
    _L0_ffn_in = {k: v for k, v in _L0_ffn_all.items() if k in ('gate_kernel', 'w0_kernel', 'w1_kernel', 'wo_kernel')}
    del _L0_ffn_all
    return {'x': x, 'ctx_1024': ctx_1024, 'L0_xattn_in_proj_w': _L0_xattn_in['in_proj_w'], 'L0_xattn_conv_w': _L0_xattn_in['conv_w'], 'L0_xattn_conv_b': _L0_xattn_in['conv_b'], 'L0_xattn_x_proj_w': _L0_xattn_in['x_proj_w'], 'L0_xattn_dt_proj_w': _L0_xattn_in['dt_proj_w'], 'L0_xattn_dt_proj_b': _L0_xattn_in['dt_proj_b'], 'L0_xattn_A_log': _L0_xattn_in['A_log'], 'L0_xattn_D': _L0_xattn_in['D'], 'L0_ffn_gate_kernel': _L0_ffn_in['gate_kernel'], 'L0_ffn_w0_kernel': _L0_ffn_in['w0_kernel'], 'L0_ffn_w1_kernel': _L0_ffn_in['w1_kernel'], 'L0_ffn_wo_kernel': _L0_ffn_in['wo_kernel']}

def reference(x, ctx_1024, L0_xattn_in_proj_w, L0_xattn_conv_w, L0_xattn_conv_b, L0_xattn_x_proj_w, L0_xattn_dt_proj_w, L0_xattn_dt_proj_b, L0_xattn_A_log, L0_xattn_D, L0_ffn_gate_kernel, L0_ffn_w0_kernel, L0_ffn_w1_kernel, L0_ffn_wo_kernel):
    import jax
    import jax.numpy as jnp

    def _L0_xattn_ref(hidden_states, z, in_proj_w, conv_w, conv_b, x_proj_w, dt_proj_w, dt_proj_b, A_log, D):
        import jax, jax.numpy as jnp
        import numpy as np
        import math
        B, L, DM = (2, 512, 256)
        DS, DC, EXP = (16, 4, 2)
        DI = EXP * DM
        DR = math.ceil(DM / 16)
        DT_MIN, DT_MAX, DT_FLOOR = (0.001, 0.1, 0.0001)

        def _ssm_forward(hidden_states, z, in_proj_w, conv_w, conv_b, x_proj_w, dt_proj_w, dt_proj_b, A_log, D):
            b = hidden_states.shape[0]
            x = jnp.einsum('ed,bld->bel', in_proj_w, hidden_states)
            xp = jnp.pad(x, ((0, 0), (0, 0), (DC - 1, 0)))
            xc = jax.lax.conv_general_dilated(xp, conv_w[:, None, :], window_strides=(1,), padding='VALID', dimension_numbers=('NCH', 'OIH', 'NCH'), feature_group_count=DI)
            u = jax.nn.silu(xc + conv_b[None, :, None])
            x_dbl = jnp.einsum('ke,bel->bkl', x_proj_w, u)
            dt_lo = x_dbl[:, :DR]
            Bm = x_dbl[:, DR:DR + DS]
            Cm = x_dbl[:, DR + DS:]
            delta = jax.nn.softplus(jnp.einsum('er,brl->bel', dt_proj_w, dt_lo) + dt_proj_b[None, :, None])
            A = -jnp.exp(A_log)

            def step(state, xs):
                d_t, B_t, C_t, u_t = xs
                dA = jnp.exp(d_t[..., None] * A)
                state = state * dA + (d_t * u_t)[..., None] * B_t[:, None, :]
                y_t = jnp.einsum('ben,bn->be', state, C_t)
                return (state, y_t)
            xs = (jnp.moveaxis(delta, -1, 0), jnp.moveaxis(Bm, -1, 0), jnp.moveaxis(Cm, -1, 0), jnp.moveaxis(u, -1, 0))
            state0 = jnp.zeros((b, DI, DS), delta.dtype)
            _, ys = jax.lax.scan(step, state0, xs)
            y = jnp.moveaxis(ys, 0, -1)
            y = y + D[None, :, None] * u
            y = y * jax.nn.silu(z)
            return jnp.swapaxes(y, 1, 2)
        return _ssm_forward(hidden_states, z, in_proj_w, conv_w, conv_b, x_proj_w, dt_proj_w, dt_proj_b, A_log, D)

    def _L0_ffn_ref(x, gate_kernel, w0_kernel, w1_kernel, wo_kernel):
        import jax, jax.numpy as jnp
        import numpy as np
        NUM_EXPERTS = 8
        TOP_K = 2
        EMB = 512
        MLP = 1024
        B, S = (4, 256)
        gate_logits = jnp.einsum('bsd,de->bse', x, gate_kernel)
        top_k_weights, top_k_indices = jax.lax.top_k(gate_logits, TOP_K)
        top_k_weights = jax.nn.softmax(top_k_weights.astype(jnp.float32), axis=-1).astype(x.dtype)
        one_hot = jax.nn.one_hot(top_k_indices, NUM_EXPERTS, dtype=x.dtype)
        combine = jnp.einsum('bsk,bske->bse', top_k_weights, one_hot)
        h0 = jnp.einsum('bsd,edm->bsem', x, w0_kernel)
        h1 = jnp.einsum('bsd,edm->bsem', x, w1_kernel)
        inter = jax.nn.silu(h0) * h1
        out = jnp.einsum('bse,bsem,emd->bsd', combine, inter, wo_kernel)
        return out
    x = x + _L0_xattn_ref(ctx_1024, _layernorm(x, axis=-1), L0_xattn_in_proj_w, L0_xattn_conv_w, L0_xattn_conv_b, L0_xattn_x_proj_w, L0_xattn_dt_proj_w, L0_xattn_dt_proj_b, L0_xattn_A_log, L0_xattn_D)
    x = x + _L0_ffn_ref(_layernorm(x, axis=-1), L0_ffn_gate_kernel, L0_ffn_w0_kernel, L0_ffn_w1_kernel, L0_ffn_wo_kernel)
    return x

_drawn_inputs = setup_inputs


def setup_inputs(seed=0):
    import zlib

    import numpy as np

    out = dict(_drawn_inputs(seed))
    spreads = {'L0_xattn_conv_b': (0.0, 0.1), 'L0_xattn_D': (1.0, 0.2)}
    factors = {}
    for name, (base, spread) in spreads.items():
        noise = np.random.default_rng([zlib.crc32(name.encode()), seed]).standard_normal(out[name].shape)
        drawn = base * np.exp(spread * noise) if base else spread * noise
        out[name] = jnp.asarray(drawn.astype(out[name].dtype))
    for name, factor in factors.items():
        out[name] = (out[name] * factor).astype(out[name].dtype)
    return out
```

```python
import concourse.bass as bass
from concourse import mybir
from contextlib import ExitStack

NB, L, DM, DI = 4, 512, 256, 512
DS, DC, DR = 16, 4, 16
P = 128
EB = DI // P
LB = L // P
KB = DM // P
UPH = DS
NT = NB * LB
EPS = 1e-5

fp32 = mybir.dt.float32
ALU = mybir.AluOpType
ACT = mybir.ActivationFunctionType


def mamba_block(nc, x, ctx_in, in_proj_w, conv_w, conv_b, x_proj_w, dt_proj_w, dt_proj_b, A_log, D, gate_w,
                xall, logits, bcs, xln_dram):
    ctx = ExitStack()
    with ctx:
        def sb(name, shape, dt=fp32):
            return ctx.enter_context(nc.sbuf_tensor(name, shape, dt))

        def sem(name):
            return ctx.enter_context(nc.semaphore(name))

        ident = sb("ident", [P, P])
        ctx_rows = sb("ctx_rows", [P, LB, DM])
        gT = sb("gT", [P, LB, DI])
        w_rows = gT[:, 0:2, :].rearrange("p a (c d) -> p (a c) d", d=DM)
        wT = sb("wT", [P, KB, DI])
        xp_rows = gT[0:DR + 2 * DS, 2, :]
        xpT = sb("xpT", [P, EB, DR + 2 * DS])
        dt_rows = gT[:, 3, 0:EB * DR].rearrange("p (e r) -> p e r", e=EB)
        dtT = sb("dtT", [DR, DI])
        convw = sb("convw", [P, EB, DC])
        convb = sb("convb", [P, EB])
        dtb = sb("dtb", [P, EB])
        Dp = sb("Dp", [P, EB])
        Acol = sb("Acol", [P, EB, DS])
        gate = sb("gate", [P, DI // P, 8])
        epsc = sb("epsc", [P, 1])
        st1 = sb("st1", [P, NT, 6])
        mv1 = sb("mv1", [P, NT, 2])
        rs1 = sb("rs1", [P, 4, NT])
        nm1 = sb("nm1", [P, NT])
        st2 = sb("st2", [P, LB, 6])
        mv2 = sb("mv2", [P, LB, 2])
        rs2 = sb("rs2", [P, 4, LB])
        nm2 = sb("nm2", [P, LB])
        ctxT = sb("ctxT", [P, KB, L])
        u = sb("u", [P, 2, EB * L])
        delta = sb("delta", [P, 2, EB * L])
        du = sb("du", [P, 2, EB * L])
        zs = sb("zs", [P, 2, EB * L])
        xdbl = sb("xdbl", [DR + 2 * DS, L])
        spy = sb("spy", [P, EB * L])
        spw = sb("spw", [P, EB * L])
        bc = sb("bc", [P, 4, 2, 2, L])
        dbu = sb("dbu", [P, 2, 2 * L])
        hs = sb("hs", [P, 2, 2 * L])
        hc = sb("hc", [P, 2, 2 * L])
        g = sb("g", [P, 2 * L])
        xlnb = sb("xlnb", [P, LB, DI])

        dA = [ctx.enter_context(nc.psum_tensor(f"dA{i}", [P, 2, L], fp32)) for i in range(2)]
        yacc = ctx.enter_context(nc.psum_tensor("yacc", [P, 2, L], fp32))
        pp = [ctx.enter_context(nc.psum_tensor(f"pp{i}", [P, L], fp32)) for i in range(2)]

        x_in, ctx_loaded, small_in = sem("x_in"), sem("ctx_loaded"), sem("small_in")
        ident_ok, zeros_ok = sem("ident_ok"), sem("zeros_ok")
        exp_done, dbu_done, scan_done, hc_done, acc_done = (sem(n) for n in
            ("exp_done", "dbu_done", "scan_done", "hc_done", "acc_done"))
        bc_in = [sem(f"bc_in{i}") for i in range(4)]
        filled = [sem(f"filled{i}") for i in range(2)]
        freed = [sem(f"freed{i}") for i in range(2)]
        consts_ok, stats1, rstd1_guess, rstd1_ok = sem("consts_ok"), sem("stats1"), sem("rstd1_guess"), sem("rstd1_ok")
        tap_done, conv_step, u_ready, bcs_out = sem("tap_done"), sem("conv_step"), sem("u_ready"), sem("bcs_out")
        abs_done, sp_step, soft_in, soft_loss, soft_sub, delta_ready, du_ready, zs_ready = (sem(n) for n in
            ("abs_done", "sp_step", "soft_in", "soft_loss", "soft_sub", "delta_ready", "du_ready", "zs_ready"))
        y_drained, g_done = sem("y_drained"), sem("g_done")
        stats2, guess2, rstd2_ok, xln_done, xln_out, logits_ok = (sem(n) for n in
            ("stats2", "guess2", "rstd2_ok", "xln_done", "xln_out", "logits_ok"))
        pool_step, dve_step, act_step = sem("pool_step"), sem("dve_step"), sem("act_step")

        def order(names, base):
            return {n: base + i for i, n in enumerate(names)}

        T, X, XB = ["T0", "T1"], ["X0", "X1"], ["X2", "X3"]
        DTA, DTB, E, G = ["DT0", "DT1"], ["DT2", "DT3"], ["E0", "E1"], ["G0", "G1", "G2", "G3", "LG"]
        CONST = order(["W0", "W1", "XPT", "DTT"], 0)
        FIRST = order(T + X + XB + ["XP"] + DTA + DTB, 4)
        HALF0_0 = order(T + X + XB, 15)
        LOOP1 = order(["XP"] + DTA + E + DTB, 21)
        LOOP0 = order(T + X + E + XB + G, 28)
        PER_TURN = 20
        TURNS = NB - 2
        POST = 21 + TURNS * PER_TURN
        POST1 = order(["XP"] + DTA + E + DTB, POST)
        POST0 = order(E + G, POST + 7)
        LAST1 = order(E, POST + 14)
        TAIL = order(E + G, POST + 16)

        def bank(k):
            return pp[k % 2]

        def before(k, turns=0):
            return k // 2 + (PER_TURN // 2) * turns

        block = ctx.enter_context(nc.Block())

        def cols(t, b, lo, n):
            if isinstance(b, int):
                return t[:, b % 2, lo:lo + n]
            return t[:, bass.ds(b % 2, 1), lo:lo + n].rearrange("p a n -> p (a n)")

        def row(t, b, i):
            return t[:, bass.ds(b * LB + i, 1), :].rearrange("p a n -> p (a n)")

        def q0(b, h):
            return b * (2 * UPH) + h * UPH

        def known(b, value):
            return isinstance(b, int) and b == value

        def hold(eng, sem, value):
            if not isinstance(value, int):
                value = eng.to_reg(value)
                eng.wait_ge(sem, 1)
            eng.wait_ge(sem, value)

        def start(b, h, n):
            return known(b, 0) and h == 0 and n < 2

        @block.sync
        def _(sp):
            sp.dma_start(w_rows, in_proj_w.rearrange("(e p) d -> p e d", p=P)).then_inc(small_in, 16)
            sp.dma_start(xp_rows, x_proj_w).then_inc(small_in, 16)
            sp.dma_start(dt_rows, dt_proj_w.rearrange("(e p) r -> p e r", p=P)).then_inc(small_in, 16)
            sp.dma_start(convw[:, :, :], conv_w.rearrange("(e p) c -> p e c", p=P)).then_inc(small_in, 16)
            with nc.allow_non_contiguous_dma(reason="512 values, once"):
                for t, s in ((convb, conv_b), (dtb, dt_proj_b), (Dp, D)):
                    sp.dma_start(t[:, :], s.rearrange("(e p) -> p e", p=P)).then_inc(small_in, 16)
            sp.dma_start(Acol[:, :, :], A_log.rearrange("(e p) n -> p e n", p=P)).then_inc(small_in, 16)
            sp.dma_start(gate[:, :, :], gate_w.rearrange("(e p) n -> p e n", p=P)).then_inc(small_in, 16)

            def load_ctx(b):
                if not known(b, 0):
                    sp.wait_ge(tap_done, (b - 1) * EB + 1)
                sp.dma_start(ctx_rows[:, :, :], ctx_in[bass.ds(b, 1), :, :].rearrange("b (t p) d -> p (b t) d", p=P)).then_inc(ctx_loaded, 16)

            def store_bc(b, uses, turn):
                k = uses["XP"]
                sp.wait_ge(freed[k % 2], before(k, turn) + 1)
                sp.dma_start(bcs[bass.ds(b, 1), :, :].rearrange("a n l -> (a n) l"), xdbl[DR:, :]).then_inc(bcs_out, 16)

            def load_bc(b, h):
                sp.wait_ge(bcs_out, (b + 1) * 16)
                for c in range(UPH // 2):
                    slot = c % 4
                    if not (known(b, 0) and h == 0 and c < 4):
                        sp.wait_ge(dbu_done, q0(b, h) + 2 * (c - 4) + 2)
                        sp.wait_ge(hc_done, q0(b, h) + 2 * (c - 4) + 2)
                    for kind in range(2):
                        lo = kind * DS + 2 * c
                        src = bcs[bass.ds(b, 1), lo:lo + 2, :].rearrange("a n l -> a (n l)")
                        sp.dma_start(bc[:, slot, kind, :, :].rearrange("p n l -> p (n l)"),
                                     src.to_broadcast([P, 2 * L])).then_inc(bc_in[slot], 16)

            def store_xln(b):
                sp.wait_ge(xln_done, b + 1)
                sp.dma_start(xln_dram[bass.ds(b * L, L), :].rearrange("(t p) d -> p t d", p=P), xlnb[:, :, :]).then_inc(xln_out, 16)

            load_ctx(0)
            sp.sem_inc(xln_out, 16)
            sp.dma_start(xall[:, :, :], x.rearrange("b (t p) d -> p (b t) d", p=P)).then_inc(x_in, 16)
            load_ctx(1)
            store_bc(0, FIRST, 0)
            load_bc(0, 0)
            with sp.Fori(0, TURNS) as b:
                load_bc(b, 1)
                store_bc(b + 1, LOOP1, b)
                load_ctx(b + 2)
                load_bc(b + 1, 0)
                store_xln(b)
            load_bc(NB - 2, 1)
            store_bc(NB - 1, POST1, 0)
            load_bc(NB - 1, 0)
            store_xln(NB - 2)
            load_bc(NB - 1, 1)
            store_xln(NB - 1)
            sp.wait_ge(xln_out, 16 * NB + 16)

        @block.gpsimd
        def _(pool):
            g_ = nc.gpsimd
            g_.memset(ident[:, :], 0.0).then_inc(pool_step, 1)
            g_.memset(epsc[:, :], EPS).then_inc(ident_ok, 1)
            hold(pool, pool_step, 1)
            g_.affine_select(out=ident[:, :], in_=ident[:, :], compare_op=ALU.not_equal, fill=1.0, base=0,
                             pattern=[[-1, P]], channel_multiplier=1).then_inc(ident_ok, 1)

            def rstd(rs, mv, nm, n, steps, done):
                g_.tensor_tensor(rs[:, 2, :], rs[:, 0, :], rs[:, 1, :], ALU.mult).then_inc(pool_step, 1)
                hold(pool, pool_step, steps + 1)
                g_.tensor_tensor(rs[:, 2, :], rs[:, 2, :], rs[:, 1, :], ALU.mult).then_inc(pool_step, 1)
                hold(pool, pool_step, steps + 2)
                g_.tensor_scalar(rs[:, 2, :], rs[:, 2, :], -0.5, 1.5, ALU.mult, ALU.add).then_inc(pool_step, 1)
                hold(pool, pool_step, steps + 3)
                g_.tensor_tensor(rs[:, 3, :], rs[:, 2, :], rs[:, 1, :], ALU.mult).then_inc(pool_step, 1)
                hold(pool, pool_step, steps + 4)
                g_.tensor_tensor(nm[:, :], mv[:, :, 0], rs[:, 3, :], ALU.mult).then_inc(pool_step, 1)
                hold(pool, pool_step, steps + 5)
                g_.tensor_scalar(nm[:, :], nm[:, :], -1.0, None, ALU.mult).then_inc(done, 1)

            def unit(b, h, n):
                c = n // 2
                if n % 2 == 0:
                    hold(pool, bc_in[c % 4], 32 * (b * 4 + 2 * h + c // 4 + 1))
                if n == 0:
                    hold(pool, du_ready, b * 2 + h + 1)
                if not start(b, h, n):
                    hold(pool, scan_done, q0(b, h) + n - 1)
                B = bc[:, c % 4, 0, n % 2:n % 2 + 1, :].to_broadcast([P, 2, L])
                g_.tensor_tensor(dbu[:, n % 2, :].rearrange("p (e l) -> p e l", e=2),
                                 cols(du, b, h * 2 * L, 2 * L).rearrange("p (e l) -> p e l", e=2), B,
                                 ALU.mult).then_inc(dbu_done, 1)

            def soft(b, i):
                s = slice(i * 2 * L, (i + 1) * 2 * L)
                d, o = cols(delta, b, i * 2 * L, 2 * L), cols(du, b, i * 2 * L, 2 * L)

                def loss():
                    hold(pool, soft_in, b + 1)
                    g_.tensor_tensor(spy[:, s], o, spy[:, s], ALU.subtract).then_inc(soft_loss, 1)

                def sub():
                    hold(pool, soft_loss, b * 2 + i + 1)
                    g_.tensor_tensor(d, d, spy[:, s], ALU.subtract).then_inc(soft_sub, 1)

                def add():
                    hold(pool, soft_sub, b * 2 + i + 1)
                    g_.tensor_tensor(d, d, spw[:, s], ALU.add).then_inc(delta_ready, 1)

                def times_u():
                    hold(pool, delta_ready, b * 2 + i + 1)
                    hold(pool, u_ready, b + 1)
                    g_.tensor_tensor(o, d, cols(u, b, i * 2 * L, 2 * L), ALU.mult).then_inc(du_ready, 1)

                return [loss, sub, add, times_u]

            def gate_y(b, h):
                hold(pool, zs_ready, b + 1)
                hold(pool, y_drained, b * 2 + h + 1)
                g_.tensor_tensor(g[:, :], g[:, :], cols(zs, b, h * 2 * L, 2 * L), ALU.mult).then_inc(g_done, 1)

            def rstd2(b):
                hold(pool, guess2, b + 1)
                rstd(rs2, mv2, nm2, LB, 6 + 5 * b, rstd2_ok)

            def half(b, h, tasks):
                for n in range(UPH):
                    unit(b, h, n)
                    for f in tasks.get(n, []):
                        f()

            def half1(b, soft_next=True):
                nxt = soft(b + 1, 0) if soft_next else []
                half(b, 1, {2: [lambda: gate_y(b, 0)], **{11 + i: [f] for i, f in enumerate(nxt)}})

            def half0(b, rest=True):
                second = soft(b, 1)
                tasks = {3: [second[0]], 5: [second[1]], 7: [second[2]], 11: [second[3]]}
                if rest:
                    tasks[2] = [lambda: gate_y(b - 1, 1)]
                    tasks[8] = [lambda: rstd2(b - 1)]
                half(b, 0, tasks)

            hold(pool, rstd1_guess, 1)
            rstd(rs1, mv1, nm1, NT, 1, rstd1_ok)
            for f in soft(0, 0):
                f()
            half0(0, rest=False)
            with pool.Fori(0, TURNS) as b:
                half1(b)
                half0(b + 1)
            half1(NB - 2)
            half0(NB - 1)
            half1(NB - 1, soft_next=False)
            gate_y(NB - 1, 1)
            rstd2(NB - 1)

        @block.scalar
        def _(act):
            a_ = nc.scalar

            def copy_use(dst, k, turn, width=L, parts=P):
                hold(act, filled[k % 2], before(k, turn) + 1)
                a_.activation(dst, bank(k)[0:parts, 0:width], ACT.Copy).then_inc(freed[k % 2], 1)

            def unit(b, h, n):
                if n == 0:
                    hold(act, delta_ready, b * 2 + h + 1)
                if start(b, h, n):
                    hold(act, zeros_ok, 1)
                else:
                    hold(act, scan_done, q0(b, h) + n - 1)
                for e in range(2):
                    eb = 2 * h + e
                    last = a_.activation(dA[n % 2][:, e, 1:L], cols(delta, b, eb * L + 1, L - 1), ACT.Exp,
                                         scale=Acol[:, eb, n:n + 1])
                last.then_inc(exp_done, 1)

            def ctx_T(uses, turn, i):
                copy_use(ctxT[:, i, :], uses["T%d" % i], turn)

            def tap(b, uses, turn, eb):
                k = uses["X%d" % eb]
                hold(act, filled[k % 2], before(k, turn) + 1)
                a_.activation(cols(u, b, eb * L, L), bank(k)[:, :], ACT.Identity, scale=convw[:, eb, DC - 1:DC],
                              bias=convb[:, eb:eb + 1]).then_inc(tap_done, 1)

            def silus(b, uses, turn):
                for name in XB:
                    k = uses[name]
                    hold(act, freed[k % 2], before(k, turn) + 1)
                a_.activation(cols(u, b, 0, EB * L), cols(u, b, 0, EB * L), ACT.Silu).then_inc(u_ready, 1)
                hold(act, rstd1_ok, 1)
                for eb in range(EB):
                    last = a_.activation(cols(zs, b, eb * L, L), row(xall, b, eb), ACT.Silu,
                                         scale=rs1[:, 3, bass.ds(b * LB + eb, 1)], bias=nm1[:, bass.ds(b * LB + eb, 1)])
                last.then_inc(zs_ready, 1)

            def xdbl_copy(b, uses, turn):
                if not known(b, 0):
                    hold(act, bcs_out, b * 16)
                copy_use(xdbl[:, :], uses["XP"], turn, parts=DR + 2 * DS)

            def dt_eb(b, uses, turn, eb):
                k = uses["DT%d" % eb]
                hold(act, filled[k % 2], before(k, turn) + 1)
                a_.activation(spy[:, eb * L:(eb + 1) * L], bank(k)[:, :], ACT.Abs, bias=dtb[:, eb:eb + 1]).then_inc(abs_done, 1)
                a_.activation(cols(delta, b, eb * L, L), bank(k)[:, :], ACT.Relu, bias=dtb[:, eb:eb + 1]).then_inc(freed[k % 2], 1)

            def soft(b):
                hold(act, abs_done, b * EB + EB)
                a_.activation(spy[:, :], spy[:, :], ACT.Exp, scale=-1.0).then_inc(sp_step, 1)
                hold(act, sp_step, b * 3 + 1)
                a_.activation(spw[:, :], spy[:, :], ACT.Copy, bias=1.0).then_inc(sp_step, 1)
                hold(act, sp_step, b * 3 + 2)
                a_.activation(cols(du, b, 0, EB * L), spw[:, :], ACT.Copy, bias=-1.0).then_inc(sp_step, 1)
                hold(act, sp_step, b * 3 + 3)
                a_.activation(spw[:, :], spw[:, :], ACT.Ln).then_inc(soft_in, 1)

            def guess(rs, mv, done, base):
                a_.activation(rs[:, 0, :], mv[:, :, 1], ACT.Identity, bias=epsc[:, 0:1]).then_inc(act_step, 1)
                hold(act, act_step, base + 1)
                a_.activation(rs[:, 1, :], rs[:, 0, :], ACT.Ln).then_inc(act_step, 1)
                hold(act, act_step, base + 2)
                a_.activation(rs[:, 1, :], rs[:, 1, :], ACT.Exp, scale=-0.5).then_inc(done, 1)

            def guess_2(b):
                hold(act, stats2, b + 1)
                guess(rs2, mv2, guess2, 3 + 2 * b)

            def xln(b):
                hold(act, rstd2_ok, b + 1)
                hold(act, xln_out, b * 16 + 16)
                for i in range(LB):
                    last = a_.activation(xlnb[:, i, :], row(xall, b, i), ACT.Identity, scale=rs2[:, 3, i:i + 1], bias=nm2[:, i:i + 1])
                last.then_inc(xln_done, 1)

            def gate_T(uses, turn, i):
                copy_use(gT[:, i, :], uses["G%d" % i], turn)

            def logit_copy(b, uses, turn):
                k = uses["LG"]
                hold(act, filled[k % 2], before(k, turn) + 1)
                a_.activation(logits[:, bass.ds(b * LB, LB), :].rearrange("p t e -> p (t e)"), bank(k)[:, 0:LB * 8],
                              ACT.Copy).then_inc(freed[k % 2], 1)

            def half(b, h, tasks):
                for n in range(UPH):
                    unit(b, h, n)
                    for f in tasks.get(n, []):
                        f()

            def half1(b, uses, turn, nxt=True):
                tasks = {}
                if nxt:
                    tasks = {1: [lambda: xdbl_copy(b + 1, uses, turn)],
                             3: [lambda: dt_eb(b + 1, uses, turn, 0), lambda: dt_eb(b + 1, uses, turn, 1)],
                             7: [lambda: dt_eb(b + 1, uses, turn, 2), lambda: dt_eb(b + 1, uses, turn, 3)],
                             8: [lambda: soft(b + 1)]}
                half(b, 1, tasks)

            def half0(b, uses, turn, nxt=True, rest=True):
                tasks = {n: [] for n in range(UPH)}
                if nxt:
                    tasks[1] += [lambda: ctx_T(uses, turn, 0), lambda: ctx_T(uses, turn, 1)]
                    tasks[3] += [lambda: tap(b + 1, uses, turn, 0), lambda: tap(b + 1, uses, turn, 1)]
                    tasks[8] += [lambda: tap(b + 1, uses, turn, 2), lambda: tap(b + 1, uses, turn, 3)]
                if rest:
                    tasks[7] += [lambda: guess_2(b - 1)]
                    tasks[9] += [lambda: xln(b - 1)]
                    tasks[11] += [lambda: gate_T(uses, turn, 0), lambda: gate_T(uses, turn, 1)]
                    tasks[13] += [lambda: gate_T(uses, turn, 2), lambda: gate_T(uses, turn, 3)]
                    tasks[15] += [lambda: logit_copy(b - 1, uses, turn)]
                if nxt:
                    tasks[10] += [lambda: silus(b + 1, uses, turn)]
                half(b, 0, tasks)

            hold(act, small_in, 16 * 9)
            hold(act, ident_ok, 2)
            a_.activation(Acol[:, :, :], Acol[:, :, :], ACT.Exp).then_inc(act_step, 1)
            copy_use(wT[:, 0, :], CONST["W0"], 0)
            copy_use(wT[:, 1, :], CONST["W1"], 0)
            copy_use(xpT[:, :, :].rearrange("p e k -> p (e k)"), CONST["XPT"], 0, width=EB * (DR + 2 * DS))
            copy_use(dtT[:, :], CONST["DTT"], 0, parts=DR)
            hold(act, act_step, 1)
            a_.activation(Acol[:, :, :], Acol[:, :, :], ACT.Copy, scale=-1.0).then_inc(consts_ok, 1)

            for i in range(2):
                ctx_T(FIRST, 0, i)
            for eb in range(EB):
                tap(0, FIRST, 0, eb)
            hold(act, stats1, 1)
            guess(rs1, mv1, rstd1_guess, 1)
            silus(0, FIRST, 0)
            xdbl_copy(0, FIRST, 0)
            for eb in range(EB):
                dt_eb(0, FIRST, 0, eb)
            soft(0)
            hold(act, consts_ok, 1)
            half0(0, HALF0_0, 0, rest=False)
            with act.Fori(0, TURNS) as b:
                half1(b, LOOP1, b)
                half0(b + 1, LOOP0, b)
            half1(NB - 2, POST1, 0)
            half0(NB - 1, POST0, 0, nxt=False)
            half1(NB - 1, LAST1, 0, nxt=False)
            guess_2(NB - 1)
            xln(NB - 1)
            for i in range(LB):
                gate_T(TAIL, 0, i)
            logit_copy(NB - 1, TAIL, 0)

        @block.vector
        def _(dve):
            v_ = nc.vector
            for i in range(2):
                last = v_.memset(dA[i][:, :, 0:1], 0.0)
            last.then_inc(zeros_ok, 1)

            def scan(b, h, n):
                dve.wait_ge(exp_done, q0(b, h) + n + 1)
                dve.wait_ge(dbu_done, q0(b, h) + n + 1)
                if not start(b, h, n):
                    dve.wait_ge(hc_done, q0(b, h) + n - 1)
                v_.tensor_tensor_scan(hs[:, n % 2, :], dA[n % 2][:, :, :].rearrange("p e l -> p (e l)"), dbu[:, n % 2, :],
                                      0.0, ALU.mult, ALU.add).then_inc(scan_done, 1)

            def times_c(b, h, n):
                c = n // 2
                dve.wait_ge(scan_done, q0(b, h) + n + 1)
                if n % 2 == 0:
                    dve.wait_ge(bc_in[c % 4], 32 * (b * 4 + 2 * h + c // 4 + 1))
                if not start(b, h, n):
                    dve.wait_ge(acc_done, q0(b, h) + n - 1)
                C = bc[:, c % 4, 1, n % 2:n % 2 + 1, :].to_broadcast([P, 2, L])
                v_.tensor_tensor(hc[:, n % 2, :].rearrange("p (e l) -> p e l", e=2),
                                 hs[:, n % 2, :].rearrange("p (e l) -> p e l", e=2), C, ALU.mult).then_inc(hc_done, 1)

            def conv(b, uses, turn, eb):
                k = uses["X%d" % eb]
                dve.wait_ge(tap_done, b * EB + eb + 1)
                dve.wait_ge(filled[k % 2], before(k, turn) + 1)
                for j in range(1, DC):
                    o = cols(u, b, eb * L + j, L - j)
                    if j > 1:
                        dve.wait_ge(conv_step, (b * EB + eb) * (DC - 2) + j - 1)
                    last = v_.scalar_tensor_tensor(o, bank(k)[:, 0:L - j], convw[:, eb, DC - 1 - j:DC - j], o, ALU.mult, ALU.add)
                    if j < DC - 1:
                        last.then_inc(conv_step, 1)
                last.then_inc(freed[k % 2], 1)

            def drain_y(b, h, last_e):
                dve.wait_ge(acc_done, q0(b, h) + UPH)
                if last_e is not None:
                    dve.wait_ge(filled[last_e[0] % 2], before(*last_e) + 1)
                for e in range(2):
                    eb = 2 * h + e
                    last = v_.scalar_tensor_tensor(g[:, e * L:(e + 1) * L], cols(u, b, eb * L, L), Dp[:, eb:eb + 1],
                                                   yacc[:, e, :], ALU.mult, ALU.add)
                last.then_inc(y_drained, 1)

            def add_y(b, h, uses, turn):
                dve.wait_ge(zs_ready, b + 1)
                for e in range(2):
                    k = uses["E%d" % e]
                    eb = 2 * h + e
                    dve.wait_ge(filled[k % 2], before(k, turn) + 1)
                    xs = xall[:, bass.ds(b * LB, LB), eb * P:(eb + 1) * P]
                    v_.tensor_tensor(xs, bank(k)[:, :].rearrange("p (t e) -> p t e", t=LB), xs, ALU.add).then_inc(freed[k % 2], 1)

            def stats_2(b, uses, turn):
                for name in E:
                    k = uses[name]
                    hold(dve, freed[k % 2], before(k, turn) + 1)
                for t in range(LB):
                    last = v_.bn_stats(st2[:, t, :], row(xall, b, t))
                last.then_inc(dve_step, 1)
                hold(dve, dve_step, b + 2)
                for t in range(LB):
                    last = v_.bn_aggr(mv2[:, t, :], st2[:, t, :])
                last.then_inc(stats2, 1)

            def half(b, h, tasks):
                for n in range(UPH):
                    scan(b, h, n)
                    if n > 0:
                        times_c(b, h, n - 1)
                    for f in tasks.get(n, []):
                        f()
                times_c(b, h, UPH - 1)

            def half1(b, uses, turn, last_e):
                half(b, 1, {1: [lambda: drain_y(b, 0, last_e)], 5: [lambda: add_y(b, 0, uses, turn)]})

            def half0(b, uses, turn, last_e=None, nxt=True, rest=True):
                tasks = {n: [] for n in range(UPH)}
                if nxt:
                    tasks[4] += [lambda: conv(b + 1, uses, turn, 0), lambda: conv(b + 1, uses, turn, 1)]
                    tasks[9] += [lambda: conv(b + 1, uses, turn, 2), lambda: conv(b + 1, uses, turn, 3)]
                if rest:
                    tasks[1] += [lambda: drain_y(b - 1, 1, last_e)]
                    tasks[6] += [lambda: add_y(b - 1, 1, uses, turn), lambda: stats_2(b - 1, uses, turn)]
                half(b, 0, tasks)

            dve.wait_ge(x_in, 16)
            for t in range(NT):
                last = v_.bn_stats(st1[:, t, :], xall[:, t, :])
            last.then_inc(dve_step, 1)
            dve.wait_ge(dve_step, 1)
            for t in range(NT):
                last = v_.bn_aggr(mv1[:, t, :], st1[:, t, :])
            last.then_inc(stats1, 1)
            for eb in range(EB):
                conv(0, FIRST, 0, eb)
            half0(0, HALF0_0, 0, rest=False)
            with dve.Fori(0, TURNS) as b:
                half1(b, LOOP1, b, (LOOP0["E1"] - PER_TURN, b))
                half0(b + 1, LOOP0, b, (LOOP1["E1"], b))
            half1(NB - 2, POST1, 0, (LOOP0["E1"], TURNS - 1))
            half0(NB - 1, POST0, 0, (POST1["E1"], 0), nxt=False)
            half1(NB - 1, LAST1, 0, (POST0["E1"], 0))
            drain_y(NB - 1, 1, (LAST1["E1"], 0))
            add_y(NB - 1, 1, TAIL, 0)
            stats_2(NB - 1, TAIL, 0)

        @block.tensor
        def _(pe):
            t_ = nc.tensor

            def use(k, turn):
                if k > 1:
                    pe.wait_ge(freed[k % 2], before(k, turn))

            def acc(b, h, n):
                if n == 0 and not (known(b, 0) and h == 0):
                    pe.wait_ge(y_drained, b * 2 + h)
                pe.wait_ge(hc_done, q0(b, h) + n + 1)
                for e in range(2):
                    last = t_.matmul(yacc[:, e, :], ident[:, :], hc[:, n % 2, e * L:(e + 1) * L], start=(n == 0), stop=(n == UPH - 1))
                last.then_inc(acc_done, 1)

            def ctx_T(b, uses, turn):
                pe.wait_ge(ctx_loaded, (b + 1) * 16)
                for i in range(KB):
                    k = uses["T%d" % i]
                    use(k, turn)
                    for t in range(LB):
                        last = t_.transpose(bank(k)[:, t * P:(t + 1) * P], ctx_rows[:, t, i * P:(i + 1) * P], ident[:, :])
                    last.then_inc(filled[k % 2], 1)

            def in_proj(uses, turn, eb):
                if eb == 0:
                    for i in range(KB):
                        k = uses["T%d" % i]
                        pe.wait_ge(freed[k % 2], before(k, turn) + 1)
                k = uses["X%d" % eb]
                use(k, turn)
                for i in range(KB):
                    last = t_.matmul(bank(k)[:, :], wT[:, i, eb * P:(eb + 1) * P], ctxT[:, i, :], start=(i == 0), stop=(i == KB - 1))
                last.then_inc(filled[k % 2], 1)

            def x_proj(b, uses, turn):
                k = uses["XP"]
                use(k, turn)
                hold(pe, u_ready, b + 1)
                for eb in range(EB):
                    last = t_.matmul(bank(k)[0:DR + 2 * DS, :], xpT[:, eb, :], cols(u, b, eb * L, L), start=(eb == 0), stop=(eb == EB - 1))
                last.then_inc(filled[k % 2], 1)

            def dt_proj(uses, turn, eb):
                if eb == 0:
                    k = uses["XP"]
                    pe.wait_ge(freed[k % 2], before(k, turn) + 1)
                k = uses["DT%d" % eb]
                use(k, turn)
                t_.matmul(bank(k)[:, :], dtT[:, eb * P:(eb + 1) * P], xdbl[0:DR, :], start=True, stop=True).then_inc(filled[k % 2], 1)

            def y_T(b, h, uses, turn):
                pe.wait_ge(g_done, b * 2 + h + 1)
                for e in range(2):
                    k = uses["E%d" % e]
                    use(k, turn)
                    for t in range(LB):
                        last = t_.transpose(bank(k)[:, t * P:(t + 1) * P], g[:, e * L + t * P:e * L + (t + 1) * P], ident[:, :])
                    last.then_inc(filled[k % 2], 1)

            def gate_T(b, uses, turn, i):
                pe.wait_ge(xln_done, b + 1)
                k = uses["G%d" % i]
                use(k, turn)
                for d in range(DI // P):
                    last = t_.transpose(bank(k)[:, d * P:(d + 1) * P], xlnb[:, i, d * P:(d + 1) * P], ident[:, :])
                last.then_inc(filled[k % 2], 1)

            def logits_of(uses, turn):
                for i in (LB - 2, LB - 1):
                    k = uses["G%d" % i]
                    pe.wait_ge(freed[k % 2], before(k, turn) + 1)
                k = uses["LG"]
                use(k, turn)
                for i in range(LB):
                    for d in range(DI // P):
                        last = t_.matmul(bank(k)[:, i * 8:(i + 1) * 8], gT[:, i, d * P:(d + 1) * P], gate[:, d, :], start=(d == 0), stop=(d == DI // P - 1))
                last.then_inc(filled[k % 2], 1)

            def half(b, h, tasks):
                for n in range(UPH):
                    if n > 0:
                        acc(b, h, n - 1)
                    for f in tasks.get(n, []):
                        f()
                acc(b, h, UPH - 1)

            def half1(b, uses, turn, nxt=True):
                tasks = {4: [lambda: y_T(b, 0, uses, turn)]}
                if nxt:
                    tasks[0] = [lambda: x_proj(b + 1, uses, turn)]
                    tasks[2] = [lambda: dt_proj(uses, turn, 0), lambda: dt_proj(uses, turn, 1)]
                    tasks[6] = [lambda: dt_proj(uses, turn, 2), lambda: dt_proj(uses, turn, 3)]
                half(b, 1, tasks)

            def half0(b, uses, turn, nxt=True, rest=True):
                tasks = {n: [] for n in range(UPH)}
                if nxt:
                    tasks[0] += [lambda: ctx_T(b + 1, uses, turn)]
                    tasks[2] += [lambda: in_proj(uses, turn, 0), lambda: in_proj(uses, turn, 1)]
                    tasks[7] += [lambda: in_proj(uses, turn, 2), lambda: in_proj(uses, turn, 3)]
                if rest:
                    tasks[5] += [lambda: y_T(b - 1, 1, uses, turn)]
                    tasks[10] += [lambda: gate_T(b - 1, uses, turn, 0), lambda: gate_T(b - 1, uses, turn, 1)]
                    tasks[12] += [lambda: gate_T(b - 1, uses, turn, 2), lambda: gate_T(b - 1, uses, turn, 3)]
                    tasks[14] += [lambda: logits_of(uses, turn)]
                half(b, 0, tasks)

            pe.wait_ge(ident_ok, 2)
            pe.wait_ge(small_in, 16 * 9)
            for i in range(KB):
                k = CONST["W%d" % i]
                for eb in range(EB):
                    last = t_.transpose(bank(k)[:, eb * P:(eb + 1) * P], w_rows[:, eb, i * P:(i + 1) * P], ident[:, :])
                last.then_inc(filled[k % 2], 1)
            k, w = CONST["XPT"], DR + 2 * DS
            use(k, 0)
            for eb in range(EB):
                last = t_.transpose(bank(k)[:, eb * w:(eb + 1) * w], xp_rows[:, eb * P:(eb + 1) * P], ident[0:w, 0:w])
            last.then_inc(filled[k % 2], 1)
            k = CONST["DTT"]
            use(k, 0)
            for eb in range(EB):
                last = t_.transpose(bank(k)[0:DR, eb * P:(eb + 1) * P], dt_rows[:, eb, :], ident[:, :])
            last.then_inc(filled[k % 2], 1)

            ctx_T(0, FIRST, 0)
            for eb in range(EB):
                in_proj(FIRST, 0, eb)
            x_proj(0, FIRST, 0)
            for eb in range(EB):
                dt_proj(FIRST, 0, eb)
            half0(0, HALF0_0, 0, rest=False)
            with pe.Fori(0, TURNS) as b:
                half1(b, LOOP1, b)
                half0(b + 1, LOOP0, b)
            half1(NB - 2, POST1, 0)
            half0(NB - 1, POST0, 0, nxt=False)
            half1(NB - 1, LAST1, 0, nxt=False)
            y_T(NB - 1, 1, TAIL, 0)
            for i in range(LB):
                gate_T(NB - 1, TAIL, 0, i)
            logits_of(TAIL, 0)


NE, FF, TOPK = 8, 1024, 2
TOK = NB * L
KD = DI // P
KF = FF // P
SLOT_TILES = TOK * TOPK // P + NE - 1
ST = SLOT_TILES + 1
f32r, i32, u32 = mybir.dt.float32r, mybir.dt.int32, mybir.dt.uint32
AX = mybir.AxisListType


def ffn_block(nc, xall, logits, xln_dram, w0, w1, wo, y_dram, out):
    ctx = ExitStack()
    with ctx:
        def sb(name, shape, dt=fp32):
            return ctx.enter_context(nc.sbuf_tensor(name, shape, dt))

        def sem(name):
            return ctx.enter_context(nc.semaphore(name))

        NC = 6
        stage = [sb(f"stage{c}", [P, 4, 512]) for c in range(NC)]
        w_hi = [sb(f"w_hi{c}", [P, 4, 512], f32r) for c in range(NC)]
        w_lo = [sb(f"w_lo{c}", [P, 4, 512], f32r) for c in range(NC)]

        identf = sb("identf", [P, P])
        io8 = sb("io8", [P, NE])
        io_st = sb("io_st", [P, ST])
        io_cap = sb("io_cap", [P, NT])
        tokid = sb("tokid", [P, NT])
        first = sb("first", [P, NT])
        top = sb("top", [P, TOPK, NT])
        wgt = sb("wgt", [P, TOPK, NT])
        gap = sb("gap", [P, NT])
        expd = sb("expd", [P, NT])
        ntile = sb("ntile", [P, NE])
        tend = sb("tend", [P, NE])
        slotf = sb("slotf", [P, TOPK, NT])
        sloti = sb("sloti", [P, TOPK, NT], i32)
        quo_i = sb("quo_i", [P, TOPK * NT], i32)
        rem_i = sb("rem_i", [P, TOPK * NT], i32)
        texp = sb("texp", [P, ST])
        flag = sb("flag", [P, ST])
        texp_i = sb("texp_i", [P, ST], i32)
        nxt_i = sb("nxt_i", [P, ST], i32)
        flag_i = sb("flag_i", [P, ST], i32)
        tok_tab = sb("tok_tab", [P, ST], u32)
        index = [sb(f"index{i}", [P, 1], u32) for i in range(2)]
        index2 = [sb(f"index2{i}", [P, 1], u32) for i in range(8)]

        work = sb("work", [P, 8, 512])
        xg = [work[:, i, :] for i in range(2)]
        gated, inter = work[:, 2:4, :], work[:, 4:6, :]
        yb = [work[:, 6 + i, :] for i in range(2)]
        flat = work[:, :, :].rearrange("p a n -> p (a n)")
        carved = [0]

        def carve(*shape):
            n = 1
            for d in shape:
                n *= d
            part = flat[:, carved[0]:carved[0] + n]
            carved[0] += n
            names = "abc"[:len(shape)]
            return part.rearrange("p (" + " ".join(names) + ") -> p " + " ".join(names), **dict(zip(names, shape)))

        RT = 4
        R = carve(RT, P)
        S = carve(TOPK * NT, ST)
        ltri = carve(P)
        ones = carve(P)
        io128 = carve(P)
        segment, total, incl, over, base = (carve(NE, NT) for _ in range(5))
        cand, rest, ohs, pos = (carve(NT, NE) for _ in range(4))
        oh = carve(TOPK * NT, NE).rearrange("p (k t) e -> p k t e", k=TOPK)
        table8 = carve(ST, NE)
        quo, rem = carve(TOPK * NT), carve(TOPK * NT)
        tend_of, nxt = carve(ST), carve(ST)
        xT_hi, xT_lo = (sb(n, [P, KD, P], f32r) for n in ("xT_hi", "xT_lo"))
        iT_hi, iT_lo = (sb(n, [P, KF, P], f32r) for n in ("iT_hi", "iT_lo"))

        hp = [ctx.enter_context(nc.psum_tensor(f"hp{i}", [P, 512], fp32)) for i in range(4)]
        xp = ctx.enter_context(nc.psum_tensor("xp", [P, 512], fp32))
        yp = ctx.enter_context(nc.psum_tensor("yp", [P, 512], fp32))
        tp = [ctx.enter_context(nc.psum_tensor(f"tp{i}", [P, 512], fp32)) for i in range(2)]

        consts, routed, gap_exp, counted, tabled = (sem(n) for n in ("consts", "routed", "gap_exp", "counted", "tabled"))
        gap_ok, ohs_ok, RS_ok, tables_ok = (sem(n) for n in ("gap_ok", "ohs_ok", "RS_ok", "tables_ok"))
        stage_in = [sem(f"stage_in{c}") for c in range(NC)]
        hi_done, lo_done = sem("hi_done"), sem("lo_done")
        h_done, xT_done, y_done, iT_done = (sem(n) for n in ("h_done", "xT_done", "y_done", "iT_done"))
        silu_done, x_hi, x_lo, i_hi, i_lo, y_copied, inter_done = (sem(n) for n in
            ("silu_done", "x_hi", "x_lo", "i_hi", "i_lo", "y_copied", "inter_done"))
        index_ok, index2_ok = sem("index_ok"), sem("index2_ok")
        xg_in = [sem(f"xg_in{i}") for i in range(2)]
        y_out = [sem(f"y_out{i}") for i in range(2)]
        pair_in = [sem(f"pair_in{i}") for i in range(4)]
        half_sum, summed, out_done = sem("half_sum"), sem("summed"), sem("out_done")

        block = ctx.enter_context(nc.Block())
        LAST = SLOT_TILES - 1
        TURNS = LAST // 2
        assert LAST == 2 * TURNS

        def hold(eng, sem, value, least=1):
            if not isinstance(value, int):
                value = eng.to_reg(value)
                eng.wait_ge(sem, least)
            eng.wait_ge(sem, value)

        def weights_of(c, e):
            if c < 4:
                src = (w0, w1)[c // 2]
                return src[bass.ds(e, 1), :, (c % 2) * 512:(c % 2 + 1) * 512].rearrange("e (k p) f -> p (e k) f", p=P)
            return wo[bass.ds(e, 1), (c - 4) * 512:(c - 3) * 512, :].rearrange("e (k p) d -> p (e k) d", p=P)

        def splits(s, c):
            return 4 + NC * s + c + 1

        def loads_of(c, s):
            return 2 + s + (1 if c < 4 else 0)

        def pair_buf(i, k):
            return stage[i][:, k, :]

        @block.sync
        def _(sp):
            for c in range(NC):
                sp.dma_start(stage[c][:, :, :], weights_of(c, 0)).then_inc(stage_in[c], 16)
            sp.wait_ge(tables_ok, 1)
            e0 = sp.value_load(texp_i[0:1, 0:1], min_val=0, max_val=NE - 1)
            for c in range(NC):
                sp.wait_ge(stage_in[c], 16)
                sp.dma_start(stage[c][:, :, :], weights_of(c, e0), cond=e0 > 0).then_inc(stage_in[c], 16)
            n0 = sp.value_load(nxt_i[0:1, 0:1], min_val=0, max_val=NE - 1)
            for c in range(4):
                sp.wait_ge(hi_done, c + 1)
                sp.wait_ge(lo_done, c + 1)
                sp.dma_start(stage[c][:, :, :], weights_of(c, n0)).then_inc(stage_in[c], 16)

            def reload(s, c, f, e):
                sp.wait_ge(hi_done, splits(s, c))
                sp.wait_ge(lo_done, splits(s, c))
                sp.dma_start(stage[c][:, :, :], weights_of(c, e), cond=f > 0).then_inc(stage_in[c], 16)

            def step(s, parity, y=True):
                f = sp.value_load(flag_i[0:1, bass.ds(s + 1, 1)], min_val=0, max_val=1)
                e = sp.value_load(nxt_i[0:1, bass.ds(s + 1, 1)], min_val=0, max_val=NE - 1)
                for c in range(4):
                    reload(s, c, f, e)
                if y:
                    store(s - 1, 1 - parity)
                f = sp.value_load(flag_i[0:1, bass.ds(s, 1)], min_val=0, max_val=1)
                e = sp.value_load(nxt_i[0:1, bass.ds(s, 1)], min_val=0, max_val=NE - 1)
                for c in range(4, NC):
                    reload(s, c, f, e)

            def store(s, parity):
                sp.wait_ge(y_copied, s + 2)
                sp.dma_start(y_dram[bass.ds(s * P, P), :], yb[parity][:, :]).then_inc(y_out[parity], 16)

            step(0, 0, y=False)
            with sp.Fori(0, TURNS) as t:
                step(2 * t + 1, 1)
                step(2 * t + 2, 0)
            store(LAST, 0)
            with sp.Fori(0, NB) as b:
                for i in range(LB):
                    sp.wait_ge(summed, b * LB + i + 1)
                    sp.dma_start(out[bass.ds(b, 1), i * P:(i + 1) * P, :].rearrange("b p d -> p (b d)"),
                                 xall[:, bass.ds(b * LB + i, 1), :].rearrange("p a d -> p (a d)")).then_inc(out_done, 16)
            sp.wait_ge(out_done, 16 * NT)
            for c in range(NC):
                sp.wait_ge(stage_in[c], 16 * loads_of(c, SLOT_TILES))

        @block.gpsimd
        def _(pool):
            g_ = nc.gpsimd
            g_.memset(identf[:, :], 0.0).then_inc(consts, 1)
            g_.memset(ltri[:, :], 1.0).then_inc(consts, 1)
            g_.memset(ones[:, :], 1.0).then_inc(consts, 1)
            g_.memset(segment[:, :, :], 1.0).then_inc(consts, 1)
            g_.iota(io8[:, :], [[1, NE]], base=0, channel_multiplier=0, allow_small_or_imprecise_dtypes=True).then_inc(consts, 1)
            g_.iota(io128[:, :], [[1, P]], base=0, channel_multiplier=0, allow_small_or_imprecise_dtypes=True).then_inc(consts, 1)
            g_.iota(io_st[:, :], [[1, ST]], base=0, channel_multiplier=0, allow_small_or_imprecise_dtypes=True).then_inc(consts, 1)
            g_.iota(io_cap[:, :], [[P, NT]], base=0, channel_multiplier=0, allow_small_or_imprecise_dtypes=True).then_inc(consts, 1)
            g_.iota(tokid[:, :], [[P, NT]], base=0, channel_multiplier=1, allow_small_or_imprecise_dtypes=True).then_inc(consts, 1)
            pool.wait_ge(consts, 9)
            g_.memset(segment[:, :, 0:1], 0.0).then_inc(consts, 1)
            g_.affine_select(out=identf[:, :], in_=identf[:, :], compare_op=ALU.not_equal, fill=1.0, base=0,
                             pattern=[[-1, P]], channel_multiplier=1).then_inc(consts, 1)
            g_.affine_select(out=ltri[:, :], in_=ltri[:, :], compare_op=ALU.is_gt, fill=0.0, base=0,
                             pattern=[[1, P]], channel_multiplier=-1).then_inc(consts, 1)

            def gather(half, parity):
                s = 2 * half + parity
                if not isinstance(s, int):
                    hold(pool, xg_in[parity], 16 * half, 16)
                g_.tensor_copy(index[parity][:, :], tok_tab[:, bass.ds(s, 1)]).then_inc(index_ok, 1)
                hold(pool, index_ok, s + 1)
                if not isinstance(s, int):
                    hold(pool, xT_done, s - 1)
                g_.indirect_dma_start(out=xg[parity][:, :], out_offset=None, in_=xln_dram,
                                      in_offset=bass.IndirectOffsetOnAxis(ap=index[parity][:, 0:1], axis=0)).then_inc(xg_in[parity], 16)

            pool.wait_ge(tabled, 1)
            gather(0, 0)
            gather(0, 1)
            with pool.Fori(0, TURNS) as t:
                gather(t + 1, 0)
                gather(t + 1, 1)

            pool.wait_ge(y_out[0], 16 * (TURNS + 1))
            pool.wait_ge(y_out[1], 16 * TURNS)
            pool.wait_ge(lo_done, splits(LAST, NC - 1))
            for c in range(4):
                pool.wait_ge(stage_in[c], 16 * loads_of(c, SLOT_TILES))

            def pair(b, i):
                for k in range(TOPK):
                    n = 2 * i + k
                    if not isinstance(b, int):
                        hold(pool, pair_in[i], 32 * b, 16)
                    g_.tensor_copy(index2[n][:, :], sloti[:, k, bass.ds(b * LB + i, 1)].bitcast(u32)).then_inc(index2_ok, 1)
                for k in range(TOPK):
                    n = 2 * i + k
                    hold(pool, index2_ok, (b * LB + i) * TOPK + k + 1)
                    if not isinstance(b, int):
                        hold(pool, summed, (b - 1) * LB + i + 1)
                    g_.indirect_dma_start(out=pair_buf(i, k), out_offset=None, in_=y_dram,
                                          in_offset=bass.IndirectOffsetOnAxis(ap=index2[n][:, 0:1], axis=0)).then_inc(pair_in[i], 16)

            for i in range(LB):
                pair(0, i)
            with pool.Fori(1, NB) as b:
                for i in range(LB):
                    pair(b, i)

        @block.scalar
        def _(act):
            s_ = nc.scalar
            act.wait_ge(gap_ok, 1)
            s_.activation(expd[:, :], gap[:, :], ACT.Exp).then_inc(gap_exp, 1)

            def split(c, loads):
                hold(act, stage_in[c], 16 * loads, 16)
                s_.copy(w_hi[c][:, :, :], stage[c][:, :, :]).then_inc(hi_done, 1)

            def split_if(f, s, c):
                with act.If(f > 0):
                    split(c, loads_of(c, s))
                with act.Else():
                    hold(act, hi_done, splits(s, c) - 1)
                    act.sem_inc(hi_done, 1)

            def x_part(s):
                hold(act, xT_done, s + 1)
                s_.copy(xT_hi[:, :, :], xp[:, :].rearrange("p (k t) -> p k t", t=P)).then_inc(x_hi, 1)

            def step(half, parity, y=True):
                s = 2 * half + parity
                f = act.value_load(flag_i[0:1, bass.ds(s + 1, 1)], min_val=0, max_val=1)
                for h in range(2):
                    hold(act, h_done, 4 * s + h + 1)
                    if h == 0 and y:
                        hold(act, inter_done, 2 * s)
                    s_.activation(gated[:, h, :], hp[h][:, :], ACT.Silu).then_inc(silu_done, 1)
                    split_if(f, s, h)
                hold(act, h_done, 4 * s + 3)
                split_if(f, s, 2)
                x_part(s + 1)
                hold(act, h_done, 4 * s + 4)
                split_if(f, s, 3)
                if y:
                    out_part(half + parity - 1, 1 - parity)
                f = act.value_load(flag_i[0:1, bass.ds(s, 1)], min_val=0, max_val=1)
                for h in range(2):
                    hold(act, iT_done, 2 * s + h + 1)
                    s_.copy(iT_hi[:, 4 * h:4 * h + 4, :], tp[h][:, :].rearrange("p (k t) -> p k t", t=P)).then_inc(i_hi, 1)
                for c in range(4, NC):
                    split_if(f, s, c)

            def out_part(half, parity):
                hold(act, y_done, 2 * half + parity + 1)
                if not isinstance(half, int) or half > 0:
                    hold(act, y_out[parity], 16 * half, 16)
                s_.copy(yb[parity][:, :], yp[:, :]).then_inc(y_copied, 1)

            act.sem_inc(y_copied, 1)
            act.wait_ge(tables_ok, 1)
            for c in range(4):
                split(c, 2)
            x_part(0)
            step(0, 0, y=False)
            step(0, 1)
            step(1, 0)
            with act.Fori(0, TURNS - 1) as t:
                step(t + 1, 1)
                step(t + 2, 0)
            out_part(TURNS, 0)

        @block.vector
        def _(dve):
            v = nc.vector

            def over_e(a, n=NT):
                return a.unsqueeze(2).to_broadcast([P, n, NE])

            def over_t(a, n=NT):
                return a.unsqueeze(1).to_broadcast([P, n, NE])

            dve.wait_ge(consts, 12)
            source = logits
            for k in range(TOPK):
                n = 6 * k
                if k:
                    dve.wait_ge(routed, 6)
                v.tensor_reduce(top[:, k, :], source[:, :, :], axis=AX.X, op=ALU.max).then_inc(routed, 1)
                dve.wait_ge(routed, n + 1)
                v.tensor_tensor(cand[:, :, :], source[:, :, :], over_e(top[:, k, :]), ALU.is_equal).then_inc(routed, 1)
                dve.wait_ge(routed, n + 2)
                v.scalar_tensor_tensor(cand[:, :, :], cand[:, :, :], -float(NE), over_t(io8[:, :]), ALU.mult, ALU.add).then_inc(routed, 1)
                dve.wait_ge(routed, n + 3)
                v.tensor_reduce(first[:, :], cand[:, :, :], axis=AX.X, op=ALU.min).then_inc(routed, 1)
                dve.wait_ge(routed, n + 4)
                v.tensor_tensor(oh[:, k, :, :], cand[:, :, :], over_e(first[:, :]), ALU.is_equal).then_inc(routed, 1)
                if k == 0:
                    dve.wait_ge(routed, 5)
                    v.scalar_tensor_tensor(rest[:, :, :], oh[:, 0, :, :], -3e38, logits[:, :, :], ALU.mult, ALU.add).then_inc(routed, 1)
                    source = rest
            dve.wait_ge(routed, 11)
            v.tensor_tensor(gap[:, :], top[:, 1, :], top[:, 0, :], ALU.subtract).then_inc(gap_ok, 1)
            v.tensor_tensor(ohs[:, :, :], oh[:, 0, :, :], oh[:, 1, :, :], ALU.add).then_inc(ohs_ok, 1)

            dve.wait_ge(gap_exp, 1)
            v.tensor_scalar(wgt[:, 1, :], expd[:, :], 1.0, None, ALU.add).then_inc(routed, 1)
            dve.wait_ge(routed, 12)
            v.reciprocal(wgt[:, 0, :], wgt[:, 1, :]).then_inc(routed, 1)
            dve.wait_ge(routed, 13)
            v.tensor_tensor(wgt[:, 1, :], wgt[:, 0, :], expd[:, :], ALU.mult).then_inc(routed, 1)

            dve.wait_ge(counted, 2)
            v.tensor_copy(total[:, :, :].rearrange("p e t -> p t e"), hp[1][:, 0:P].rearrange("p (t e) -> p t e", e=NE)).then_inc(routed, 1)
            dve.wait_ge(routed, 15)
            v.tensor_tensor_scan(incl[:, :, :].rearrange("p e t -> p (e t)"), segment[:, :, :].rearrange("p e t -> p (e t)"),
                                 total[:, :, :].rearrange("p e t -> p (e t)"), 0.0, ALU.mult, ALU.add).then_inc(routed, 1)
            dve.wait_ge(routed, 16)
            v.tensor_tensor(over[:, :, :], incl[:, :, NT - 1:NT].to_broadcast([P, NE, NT]),
                            io_cap[:, :].unsqueeze(1).to_broadcast([P, NE, NT]), ALU.is_gt).then_inc(routed, 1)
            dve.wait_ge(routed, 17)
            v.tensor_reduce(ntile[:, :], over[:, :, :], axis=AX.X, op=ALU.add).then_inc(routed, 1)
            dve.wait_ge(routed, 18)
            v.tensor_tensor_scan(tend[:, :], ones[:, 0:NE], ntile[:, :], 0.0, ALU.mult, ALU.add).then_inc(routed, 1)
            dve.wait_ge(routed, 19)
            v.tensor_tensor(ntile[:, :], tend[:, :], ntile[:, :], ALU.subtract).then_inc(routed, 1)
            v.tensor_tensor(incl[:, :, :], incl[:, :, :], total[:, :, :], ALU.subtract).then_inc(routed, 1)
            dve.wait_ge(routed, 21)
            v.scalar_tensor_tensor(base[:, :, :], ntile[:, :].unsqueeze(2).to_broadcast([P, NE, NT]), float(P), incl[:, :, :], ALU.mult, ALU.add).then_inc(routed, 1)
            dve.wait_ge(routed, 22)
            v.tensor_tensor(pos[:, :, :], hp[0][:, 0:P].rearrange("p (t e) -> p t e", e=NE),
                            base[:, :, :].rearrange("p e t -> p t e"), ALU.add).then_inc(routed, 1)
            dve.wait_ge(routed, 23)
            for k in range(TOPK):
                v.tensor_tensor(oh[:, k, :, :], oh[:, k, :, :], pos[:, :, :], ALU.mult).then_inc(routed, 1)
            dve.wait_ge(routed, 25)
            v.tensor_reduce(slotf[:, :, :].rearrange("p k t -> p (k t)"), oh[:, :, :, :].rearrange("p k t e -> p (k t) e"), axis=AX.X, op=ALU.add).then_inc(routed, 1)
            dve.wait_ge(routed, 26)
            v.tensor_copy(sloti[:, :, :], slotf[:, :, :]).then_inc(routed, 1)
            dve.wait_ge(routed, 27)
            slots = sloti[:, :, :].rearrange("p k t -> p (k t)")
            v.tensor_scalar(quo_i[:, :], slots, 7, None, ALU.logical_shift_right).then_inc(routed, 1)
            v.tensor_scalar(rem_i[:, :], slots, P - 1, None, ALU.bitwise_and).then_inc(routed, 1)
            dve.wait_ge(routed, 29)
            v.tensor_copy(quo[:, :], quo_i[:, :]).then_inc(routed, 1)
            v.tensor_copy(rem[:, :], rem_i[:, :]).then_inc(routed, 1)
            dve.wait_ge(routed, 31)
            v.tensor_tensor(S[:, :, :], quo[:, :].unsqueeze(2).to_broadcast([P, TOPK * NT, ST]),
                            io_st[:, :].unsqueeze(1).to_broadcast([P, TOPK * NT, ST]), ALU.is_equal).then_inc(routed, 1)
            dve.wait_ge(routed, 32)
            for k in range(TOPK):
                v.tensor_tensor(S[:, k * NT:(k + 1) * NT, :], S[:, k * NT:(k + 1) * NT, :], tokid[:, :].unsqueeze(2).to_broadcast([P, NT, ST]), ALU.mult).then_inc(routed, 1)
            dve.wait_ge(routed, 34)
            for i in range(TOPK * NT // RT):
                if i:
                    dve.wait_ge(counted, 2 + i)
                v.tensor_tensor(R[:, :, :], rem[:, i * RT:(i + 1) * RT].unsqueeze(2).to_broadcast([P, RT, P]),
                                io128[:, :].unsqueeze(1).to_broadcast([P, RT, P]), ALU.is_equal).then_inc(RS_ok, 1)

            tend_b = over_t(tend[:, :], ST)
            v.tensor_tensor(table8[:, :, :], tend_b, over_e(io_st[:, :], ST), ALU.is_le).then_inc(routed, 1)
            dve.wait_ge(routed, 35)
            v.tensor_reduce(texp[:, :], table8[:, :, :], axis=AX.X, op=ALU.add).then_inc(routed, 1)
            dve.wait_ge(routed, 36)
            v.tensor_scalar(texp[:, :], texp[:, :], float(NE - 1), None, ALU.min).then_inc(routed, 1)
            dve.wait_ge(routed, 37)
            v.memset(flag[:, 0:1], 1.0).then_inc(routed, 1)
            v.tensor_tensor(flag[:, 1:ST], texp[:, 1:ST], texp[:, 0:ST - 1], ALU.not_equal).then_inc(routed, 1)
            v.tensor_tensor(table8[:, :, :], over_t(io8[:, :], ST), over_e(texp[:, :], ST), ALU.is_equal).then_inc(routed, 1)
            dve.wait_ge(routed, 40)
            v.tensor_tensor(table8[:, :, :], table8[:, :, :], tend_b, ALU.mult).then_inc(routed, 1)
            dve.wait_ge(routed, 41)
            v.tensor_reduce(tend_of[:, :], table8[:, :, :], axis=AX.X, op=ALU.add).then_inc(routed, 1)
            dve.wait_ge(routed, 42)
            v.tensor_tensor(table8[:, :, :], tend_b, over_e(tend_of[:, :], ST), ALU.is_le).then_inc(routed, 1)
            dve.wait_ge(routed, 43)
            v.tensor_reduce(nxt[:, :], table8[:, :, :], axis=AX.X, op=ALU.add).then_inc(routed, 1)
            dve.wait_ge(routed, 44)
            v.tensor_scalar(nxt[:, :], nxt[:, :], float(NE - 1), None, ALU.min).then_inc(routed, 1)
            dve.wait_ge(routed, 45)
            v.tensor_copy(texp_i[:, :], texp[:, :]).then_inc(routed, 1)
            v.tensor_copy(nxt_i[:, :], nxt[:, :]).then_inc(routed, 1)
            v.tensor_copy(flag_i[:, :], flag[:, :]).then_inc(routed, 1)
            dve.wait_ge(routed, 48)
            dve.sem_inc(tables_ok, 1)
            dve.wait_ge(counted, 2 + TOPK * NT // RT)
            v.tensor_copy(tok_tab[:, :], hp[2][:, 0:ST]).then_inc(tabled, 1)

            def split(c, done):
                hold(dve, hi_done, done)
                v.tensor_tensor(w_lo[c][:, :, :], stage[c][:, :, :], w_hi[c][:, :, :].bitcast(fp32), ALU.subtract).then_inc(lo_done, 1)

            def split_if(f, s, c):
                with dve.If(f > 0):
                    split(c, splits(s, c))
                with dve.Else():
                    hold(dve, lo_done, splits(s, c) - 1)
                    dve.sem_inc(lo_done, 1)

            def x_part(s):
                hold(dve, x_hi, s + 1)
                v.tensor_tensor(xT_lo[:, :, :], xp[:, :].rearrange("p (k t) -> p k t", t=P), xT_hi[:, :, :].bitcast(fp32), ALU.subtract).then_inc(x_lo, 1)

            def step(s, nxt=True):
                f = dve.value_load(flag_i[0:1, bass.ds(s + 1, 1)], min_val=0, max_val=1)
                split_if(f, s, 0)
                split_if(f, s, 1)
                for h in range(2):
                    hold(dve, h_done, 4 * s + 3 + h)
                    hold(dve, silu_done, 2 * s + h + 1)
                    if not (isinstance(s, int) and s == 0):
                        hold(dve, iT_done, 2 * s - 1 + h)
                    v.tensor_tensor(inter[:, h, :], hp[2 + h][:, :], gated[:, h, :], ALU.mult).then_inc(inter_done, 1)
                    if h == 0:
                        split_if(f, s, 2)
                if nxt:
                    x_part(s + 1)
                split_if(f, s, 3)
                f = dve.value_load(flag_i[0:1, bass.ds(s, 1)], min_val=0, max_val=1)
                for h in range(2):
                    hold(dve, i_hi, 2 * s + h + 1)
                    v.tensor_tensor(iT_lo[:, 4 * h:4 * h + 4, :], tp[h][:, :].rearrange("p (k t) -> p k t", t=P),
                                    iT_hi[:, 4 * h:4 * h + 4, :].bitcast(fp32), ALU.subtract).then_inc(i_lo, 1)
                for c in range(4, NC):
                    split_if(f, s, c)

            for c in range(4):
                split(c, c + 1)
            x_part(0)
            step(0)
            with dve.Fori(0, TURNS) as t:
                step(2 * t + 1)
                step(2 * t + 2)

            with dve.Fori(0, NB) as b:
                for i in range(LB):
                    hold(dve, pair_in[i], 32 * b + 32, 16)
                    tile = xall[:, bass.ds(b * LB + i, 1), :].rearrange("p a d -> p (a d)")
                    for k in range(TOPK):
                        if k:
                            hold(dve, half_sum, b * LB + i + 1)
                        v.scalar_tensor_tensor(tile, pair_buf(i, k), wgt[:, k, bass.ds(b * LB + i, 1)], tile,
                                               ALU.mult, ALU.add).then_inc(summed if k else half_sum, 1)

        @block.tensor
        def _(pe):
            t_ = nc.tensor
            pe.wait_ge(consts, 12)
            pe.wait_ge(ohs_ok, 1)
            both = ohs[:, :, :].rearrange("p t e -> p (t e)")
            t_.matmul(hp[0][:, 0:P], ltri[:, :], both, start=True, stop=True).then_inc(counted, 1)
            t_.matmul(hp[1][:, 0:P], ones[:, :], both, start=True, stop=True).then_inc(counted, 1)
            for i in range(TOPK * NT // RT):
                pe.wait_ge(RS_ok, i + 1)
                for j in range(RT):
                    last = t_.matmul(hp[2][:, 0:ST], R[:, j, :], S[:, i * RT + j, :], start=(i + j == 0), stop=(i * RT + j == TOPK * NT - 1))
                last.then_inc(counted, 1)

            def x_T(half, parity):
                s = 2 * half + parity
                pe.wait_ge(xg_in[parity], 16 * half + 16)
                if not (isinstance(s, int) and s == 0):
                    pe.wait_ge(x_lo, s)
                for k in range(KD):
                    last = t_.transpose(xp[:, k * P:(k + 1) * P], xg[parity][:, k * P:(k + 1) * P], identf[:, :])
                last.then_inc(xT_done, 1)

            def product(bank, a_hi, a_lo, ks, b_hi, b_lo, start, stop):
                for k in ks:
                    b = k % 4
                    t_.matmul(bank[:, :], a_hi[:, k, :], b_hi[:, b, :], start=(start and k == ks[0]), stop=False)
                    t_.matmul(bank[:, :], a_hi[:, k, :], b_lo[:, b, :], start=False, stop=False)
                    last = t_.matmul(bank[:, :], a_lo[:, k, :], b_hi[:, b, :], start=False, stop=(stop and k == ks[-1]))
                return last

            def inner(s):
                for c in range(4):
                    if c == 0:
                        pe.wait_ge(x_lo, s + 1)
                    ready = c + 1 if isinstance(s, int) and s == 0 else splits(s - 1, c)
                    pe.wait_ge(lo_done, ready)
                    if not (isinstance(s, int) and s == 0):
                        if c < 2:
                            pe.wait_ge(silu_done, 2 * s - 1 + c)
                        else:
                            pe.wait_ge(inter_done, 2 * s - 3 + c)
                    product(hp[c], xT_hi, xT_lo, range(4), w_hi[c], w_lo[c], True, True).then_inc(h_done, 1)

            def outer(s):
                pe.wait_ge(i_lo, 2 * s + 2)
                pe.wait_ge(y_copied, s + 1)
                pe.wait_ge(lo_done, splits(s, 4))
                product(yp, iT_hi, iT_lo, range(4), w_hi[4], w_lo[4], True, False)
                pe.wait_ge(lo_done, splits(s, 5))
                product(yp, iT_hi, iT_lo, range(4, 8), w_hi[5], w_lo[5], False, True).then_inc(y_done, 1)

            def inter_T(s):
                for h in range(2):
                    pe.wait_ge(inter_done, 2 * s + h + 1)
                    if not (isinstance(s, int) and s == 0):
                        pe.wait_ge(i_lo, 2 * s - 1 + h)
                    for k in range(4):
                        last = t_.transpose(tp[h][:, k * P:(k + 1) * P], inter[:, h, k * P:(k + 1) * P], identf[:, :])
                    last.then_inc(iT_done, 1)

            x_T(0, 0)
            inner(0)
            x_T(0, 1)
            inter_T(0)
            with pe.Fori(0, TURNS) as t:
                for j in range(2):
                    s = 2 * t + 1 + j
                    inner(s)
                    x_T(t + 1, j)
                    outer(s - 1)
                    inter_T(s)
            outer(LAST)


def model(nc, x, ctx_in, in_proj_w, conv_w, conv_b, x_proj_w, dt_proj_w, dt_proj_b, A_log, D, gate_w, w0, w1, wo, out):
    ctx = ExitStack()
    with ctx:
        xall = ctx.enter_context(nc.sbuf_tensor("xall", [P, NT, DI], fp32))
        logits = ctx.enter_context(nc.sbuf_tensor("logits", [P, NT, 8], fp32))
        bcs = nc.dram_tensor("bcs", [NB, 2 * DS, L], fp32).ap()
        xln_dram = nc.dram_tensor("xln_dram", [TOK, DI], fp32).ap()
        y_dram = nc.dram_tensor("y_dram", [SLOT_TILES * P, DI], fp32).ap()
        mamba_block(nc, x, ctx_in, in_proj_w, conv_w, conv_b, x_proj_w, dt_proj_w, dt_proj_b, A_log, D, gate_w, xall, logits, bcs, xln_dram)
        ffn_block(nc, xall, logits, xln_dram, w0, w1, wo, y_dram, out)


_INS = (['x', 'ctx_1024'] + ['L0_xattn_' + n for n in ('in_proj_w', 'conv_w', 'conv_b', 'x_proj_w', 'dt_proj_w', 'dt_proj_b', 'A_log', 'D')]
        + ['L0_ffn_' + n for n in ('gate_kernel', 'w0_kernel', 'w1_kernel', 'wo_kernel')])


def kernel(**inputs):
    import numpy as _np
    import concourse.bacc as _bacc
    from concourse import mybir as _mybir
    from concourse.bass_utils import run_bass_kernel_spmd as _run
    nc = _bacc.Bacc("TRN2", target_bir_lowering=False, num_devices=1)
    arrays, args = {}, []
    for name in _INS:
        a = _np.ascontiguousarray(inputs[name])
        arrays[f"in_{name}_dram"] = a
        args.append(nc.dram_tensor(f"in_{name}_dram", a.shape, _mybir.dt.from_np(a.dtype), kind="ExternalInput").ap())
    args.append(nc.dram_tensor("out_0_dram", (4, 512, 512), _mybir.dt.float32, kind="ExternalOutput").ap())
    model(nc, *args)
    r = _run(nc, [arrays], core_ids=[0])
    return r.results[0]["out_0_dram"]
```

```python
import concourse.bass as bass
from concourse import mybir
from contextlib import ExitStack

NB, L, DM, DI = 4, 512, 256, 512
DS, DC, DR = 16, 4, 16
P = 128
EB = DI // P
LB = L // P
KB = DM // P
RING = 8
UPH = DS
NT = NB * LB
EPS = 1e-5

fp32 = mybir.dt.float32
ALU = mybir.AluOpType
ACT = mybir.ActivationFunctionType


def mamba_block(nc, x, ctx_in, in_proj_w, conv_w, conv_b, x_proj_w, dt_proj_w, dt_proj_b, A_log, D, gate_w,
                xall, logits, bcs, xln_dram):
    ctx = ExitStack()
    with ctx:
        def sb(name, shape, dt=fp32):
            return ctx.enter_context(nc.sbuf_tensor(name, shape, dt))

        def sem(name):
            return ctx.enter_context(nc.semaphore(name))

        ident = sb("ident", [P, P])
        ctx_rows = sb("ctx_rows", [P, LB, DM])
        gT = sb("gT", [P, LB, DI])
        w_rows = gT[:, 0:2, :].rearrange("p a (c d) -> p (a c) d", d=DM)
        wT = sb("wT", [P, KB, DI])
        xp_rows = gT[0:DR + 2 * DS, 2, :]
        xpT = sb("xpT", [P, EB, DR + 2 * DS])
        dt_rows = gT[:, 3, 0:EB * DR].rearrange("p (e r) -> p e r", e=EB)
        dtT = sb("dtT", [DR, DI])
        convw = sb("convw", [P, EB, DC])
        convb = sb("convb", [P, EB])
        dtb = sb("dtb", [P, EB])
        Dp = sb("Dp", [P, EB])
        Acol = sb("Acol", [P, EB, DS])
        gate = sb("gate", [P, DI // P, 8])
        epsc = sb("epsc", [P, 1])
        st1 = sb("st1", [P, NT, 6])
        mv1 = sb("mv1", [P, NT, 2])
        rs1 = sb("rs1", [P, 4, NT])
        nm1 = sb("nm1", [P, NT])
        st2 = sb("st2", [P, LB, 6])
        mv2 = sb("mv2", [P, LB, 2])
        rs2 = sb("rs2", [P, 4, LB])
        nm2 = sb("nm2", [P, LB])
        ctxT = sb("ctxT", [P, KB, L])
        u = sb("u", [P, 2, EB * L])
        delta = sb("delta", [P, 2, EB * L])
        du = sb("du", [P, 2, EB * L])
        zs = sb("zs", [P, EB * L])
        xdbl = sb("xdbl", [DR + 2 * DS, L])
        spy = sb("spy", [P, 2 * L])
        spw = sb("spw", [P, EB * L])
        bc = sb("bc", [P, 4, 2, 2, L])
        ring = sb("ring", [P, RING, 2 * L])
        diagD = sb("diagD", [P, EB, P])
        g = sb("g", [P, 2 * L])
        xlnb = sb("xlnb", [P, LB, DI])

        dA = [ctx.enter_context(nc.psum_tensor(f"dA{i}", [P, 2, L], fp32)) for i in range(2)]
        yacc = ctx.enter_context(nc.psum_tensor("yacc", [P, 2, L], fp32))
        pp = [ctx.enter_context(nc.psum_tensor(f"pp{i}", [P, L], fp32)) for i in range(2)]

        x_in, ctx_loaded, small_in = sem("x_in"), sem("ctx_loaded"), sem("small_in")
        ident_ok, zeros_ok, diag_ok = sem("ident_ok"), sem("zeros_ok"), sem("diag_ok")
        exp_done, dbu_done, scan_done, hc_done, acc_done = (sem(n) for n in
            ("exp_done", "dbu_done", "scan_done", "hc_done", "acc_done"))
        bc_in = [sem(f"bc_in{i}") for i in range(4)]
        filled = [sem(f"filled{i}") for i in range(2)]
        freed = [sem(f"freed{i}") for i in range(2)]
        consts_ok, stats1, rstd1_guess, rstd1_ok = sem("consts_ok"), sem("stats1"), sem("rstd1_guess"), sem("rstd1_ok")
        tap_done, u_ready, bcs_out = sem("tap_done"), sem("u_ready"), sem("bcs_out")
        conv_step = [sem(f"conv_step{i}") for i in range(2)]
        sp_step, soft_w, soft_ln, soft_loss, soft_sub, delta_ready, du_ready, zs_ready = (sem(n) for n in
            ("sp_step", "soft_w", "soft_ln", "soft_loss", "soft_sub", "delta_ready", "du_ready", "zs_ready"))
        abs_done, y_gated = sem("abs_done"), sem("y_gated")
        stats2, guess2, rstd2_ok, xln_done, xln_out, logits_ok = (sem(n) for n in
            ("stats2", "guess2", "rstd2_ok", "xln_done", "xln_out", "logits_ok"))
        pool_step, dve_step, act_step = sem("pool_step"), sem("dve_step"), sem("act_step")

        def order(names, base):
            return {n: base + i for i, n in enumerate(names)}

        T, X, XB, XP = ["T0", "T1"], ["X0", "X1"], ["X2", "X3"], ["XP"]
        DTA, DTB, E, F = ["DT0", "DT1"], ["DT2", "DT3"], ["E0", "E1"], ["F0", "F1"]
        GA, GB = ["G0", "G1"], ["G2", "G3", "LG"]
        CONST = order(["W0", "W1", "XPT", "DTT"], 0)
        FIRST = order(T + X + XB + XP + DTA + DTB, 4)
        TURN0 = order(T + X + XB + XP + F + DTA + DTB, 15)
        LOOP = order(T + E + X + XB + GA + XP + F + DTA + DTB + GB, 28)
        PER_TURN = 20
        TURNS = NB - 2
        LAST = order(E + GA + F + GB, 28 + TURNS * PER_TURN)
        TAIL = order(E + GA + GB, 28 + TURNS * PER_TURN + 9)

        def bank(k):
            return pp[k % 2]

        def before(k, turns=0):
            return k // 2 + (PER_TURN // 2) * turns

        block = ctx.enter_context(nc.Block())

        def cols(t, b, lo, n):
            if isinstance(b, int):
                return t[:, b % 2, lo:lo + n]
            return t[:, bass.ds(b % 2, 1), lo:lo + n].rearrange("p a n -> p (a n)")

        def row(t, b, i):
            return t[:, bass.ds(b * LB + i, 1), :].rearrange("p a n -> p (a n)")

        def q0(b, h):
            return b * (2 * UPH) + h * UPH

        def known(b, value):
            return isinstance(b, int) and b == value

        def hold(eng, sem, value, least=1):
            if not isinstance(value, int):
                value = eng.to_reg(value)
                eng.wait_ge(sem, least)
            eng.wait_ge(sem, value)

        def start(b, h, n):
            return known(b, 0) and h == 0 and n < 2

        def fresh(b, h, n):
            return known(b, 0) and h == 0 and n < RING

        @block.sync
        def _(sp):
            sp.dma_start(w_rows, in_proj_w.rearrange("(e p) d -> p e d", p=P)).then_inc(small_in, 16)
            sp.dma_start(xp_rows, x_proj_w).then_inc(small_in, 16)
            sp.dma_start(dt_rows, dt_proj_w.rearrange("(e p) r -> p e r", p=P)).then_inc(small_in, 16)
            sp.dma_start(convw[:, :, :], conv_w.rearrange("(e p) c -> p e c", p=P)).then_inc(small_in, 16)
            with nc.allow_non_contiguous_dma(reason="512 values, once"):
                for t, s in ((convb, conv_b), (dtb, dt_proj_b), (Dp, D)):
                    sp.dma_start(t[:, :], s.rearrange("(e p) -> p e", p=P)).then_inc(small_in, 16)
            sp.dma_start(Acol[:, :, :], A_log.rearrange("(e p) n -> p e n", p=P)).then_inc(small_in, 16)
            sp.dma_start(gate[:, :, :], gate_w.rearrange("(e p) n -> p e n", p=P)).then_inc(small_in, 16)

            def load_ctx(b):
                if not known(b, 0):
                    hold(sp, tap_done, (b - 1) * EB + 1)
                sp.dma_start(ctx_rows[:, :, :], ctx_in[bass.ds(b, 1), :, :].rearrange("b (t p) d -> p (b t) d", p=P)).then_inc(ctx_loaded, 16)

            def store_bc(b, uses, turn):
                k = uses["XP"]
                hold(sp, freed[k % 2], before(k, turn) + 1)
                sp.dma_start(bcs[bass.ds(b, 1), :, :].rearrange("a n l -> (a n) l"), xdbl[DR:, :]).then_inc(bcs_out, 16)

            def load_bc(b, h):
                hold(sp, bcs_out, (b + 1) * 16, 16)
                for c in range(UPH // 2):
                    slot = c % 4
                    if not (known(b, 0) and h == 0 and c < 4):
                        hold(sp, dbu_done, q0(b, h) + 2 * (c - 4) + 2)
                        hold(sp, hc_done, q0(b, h) + 2 * (c - 4) + 2)
                    for kind in range(2):
                        lo = kind * DS + 2 * c
                        src = bcs[bass.ds(b, 1), lo:lo + 2, :].rearrange("a n l -> a (n l)")
                        sp.dma_start(bc[:, slot, kind, :, :].rearrange("p n l -> p (n l)"),
                                     src.to_broadcast([P, 2 * L])).then_inc(bc_in[slot], 16)

            def store_xln(b):
                hold(sp, xln_done, b + 1)
                sp.dma_start(xln_dram[bass.ds(b * L, L), :].rearrange("(t p) d -> p t d", p=P), xlnb[:, :, :]).then_inc(xln_out, 16)

            load_ctx(0)
            sp.sem_inc(xln_out, 16)
            sp.dma_start(xall[:, :, :], x.rearrange("b (t p) d -> p (b t) d", p=P)).then_inc(x_in, 16)
            store_bc(0, FIRST, 0)
            load_ctx(1)
            load_bc(0, 0)
            load_bc(0, 1)
            store_bc(1, TURN0, 0)
            with sp.Fori(1, NB - 1) as b:
                load_ctx(b + 1)
                load_bc(b, 0)
                load_bc(b, 1)
                store_xln(b - 1)
                store_bc(b + 1, LOOP, b - 1)
            load_bc(NB - 1, 0)
            load_bc(NB - 1, 1)
            store_xln(NB - 2)
            store_xln(NB - 1)
            sp.wait_ge(xln_out, 16 * NB + 16)

        @block.gpsimd
        def _(pool):
            g_ = nc.gpsimd
            g_.memset(ident[:, :], 0.0).then_inc(pool_step, 1)
            g_.memset(epsc[:, :], EPS).then_inc(ident_ok, 1)
            hold(pool, pool_step, 1)
            g_.affine_select(out=ident[:, :], in_=ident[:, :], compare_op=ALU.not_equal, fill=1.0, base=0,
                             pattern=[[-1, P]], channel_multiplier=1).then_inc(ident_ok, 1)

            def rstd(rs, mv, nm, n, steps, done):
                g_.tensor_tensor(rs[:, 2, :], rs[:, 0, :], rs[:, 1, :], ALU.mult).then_inc(pool_step, 1)
                hold(pool, pool_step, steps + 1)
                g_.tensor_tensor(rs[:, 2, :], rs[:, 2, :], rs[:, 1, :], ALU.mult).then_inc(pool_step, 1)
                hold(pool, pool_step, steps + 2)
                g_.tensor_scalar(rs[:, 2, :], rs[:, 2, :], -0.5, 1.5, ALU.mult, ALU.add).then_inc(pool_step, 1)
                hold(pool, pool_step, steps + 3)
                g_.tensor_tensor(rs[:, 3, :], rs[:, 2, :], rs[:, 1, :], ALU.mult).then_inc(pool_step, 1)
                hold(pool, pool_step, steps + 4)
                g_.tensor_tensor(nm[:, :], mv[:, :, 0], rs[:, 3, :], ALU.mult).then_inc(pool_step, 1)
                hold(pool, pool_step, steps + 5)
                g_.tensor_scalar(nm[:, :], nm[:, :], -1.0, None, ALU.mult).then_inc(done, 1)

            def unit(b, h, n):
                c = n // 2
                if n % 2 == 0:
                    hold(pool, bc_in[c % 4], 32 * (b * 4 + 2 * h + c // 4 + 1))
                if n == 0:
                    hold(pool, du_ready, b * 2 + h + 1)
                if not fresh(b, h, n):
                    hold(pool, acc_done, q0(b, h) + n - RING + 1)
                B = bc[:, c % 4, 0, n % 2:n % 2 + 1, :].to_broadcast([P, 2, L])
                g_.tensor_tensor(ring[:, n % RING, :].rearrange("p (e l) -> p e l", e=2),
                                 cols(du, b, h * 2 * L, 2 * L).rearrange("p (e l) -> p e l", e=2), B,
                                 ALU.mult).then_inc(dbu_done, 1)

            def soft(b, i):
                s = slice(i * 2 * L, (i + 1) * 2 * L)
                d, o = cols(delta, b, i * 2 * L, 2 * L), cols(du, b, i * 2 * L, 2 * L)

                def sub():
                    hold(pool, soft_loss, b * 2 + i + 1)
                    g_.tensor_tensor(d, d, o, ALU.subtract).then_inc(soft_sub, 1)

                def add():
                    hold(pool, soft_sub, b * 2 + i + 1)
                    hold(pool, soft_ln, b * 2 + i + 1)
                    g_.tensor_tensor(d, d, spw[:, s], ALU.add).then_inc(delta_ready, 1)

                def times_u():
                    hold(pool, delta_ready, b * 2 + i + 1)
                    hold(pool, u_ready, b + 1)
                    g_.tensor_tensor(o, d, cols(u, b, i * 2 * L, 2 * L), ALU.mult).then_inc(du_ready, 1)

                return [sub, add, times_u]

            def rstd1():
                hold(pool, rstd1_guess, 1)
                rstd(rs1, mv1, nm1, NT, 1, rstd1_ok)

            def rstd2(b):
                hold(pool, guess2, b + 1)
                rstd(rs2, mv2, nm2, LB, 6 + 5 * b, rstd2_ok)

            def half(b, h, tasks):
                for n in range(UPH):
                    unit(b, h, n)
                    for f in tasks.get(n, []):
                        f()

            def turn(b, nxt=True, rest=True):
                sub, add, times_u = soft(b, 1)
                tasks = {8: [sub], 10: [add], 13: [times_u]}
                if known(b, 0):
                    tasks[4] = [rstd1]
                if rest:
                    tasks[11] = [lambda: rstd2(b - 1)]
                half(b, 0, tasks)
                tasks = {}
                if nxt:
                    sub, add, times_u = soft(b + 1, 0)
                    tasks = {12: [sub], 14: [add], 15: [times_u]}
                half(b, 1, tasks)

            for f in soft(0, 0):
                f()
            turn(0, rest=False)
            with pool.Fori(1, NB - 1) as b:
                turn(b)
            turn(NB - 1, nxt=False)
            rstd2(NB - 1)

        @block.scalar
        def _(act):
            a_ = nc.scalar

            def copy_use(dst, k, turn, width=L, parts=P):
                hold(act, filled[k % 2], before(k, turn) + 1)
                a_.activation(dst, bank(k)[0:parts, 0:width], ACT.Copy).then_inc(freed[k % 2], 1)

            def unit(b, h, n):
                if n == 0:
                    hold(act, delta_ready, b * 2 + h + 1)
                if start(b, h, n):
                    hold(act, zeros_ok, 1)
                else:
                    hold(act, scan_done, q0(b, h) + n - 1)
                for e in range(2):
                    eb = 2 * h + e
                    last = a_.activation(dA[n % 2][:, e, 1:L], cols(delta, b, eb * L + 1, L - 1), ACT.Exp,
                                         scale=Acol[:, eb, n:n + 1])
                last.then_inc(exp_done, 1)

            def ctx_T(uses, turn, i):
                copy_use(ctxT[:, i, :], uses["T%d" % i], turn)

            def tap(b, uses, turn, eb):
                k = uses["X%d" % eb]
                hold(act, filled[k % 2], before(k, turn) + 1)
                a_.activation(cols(u, b, eb * L, L), bank(k)[:, :], ACT.Identity, scale=convw[:, eb, DC - 1:DC],
                              bias=convb[:, eb:eb + 1]).then_inc(tap_done, 1)

            def silu_u(b, uses, turn):
                for name in XB:
                    k = uses[name]
                    hold(act, freed[k % 2], before(k, turn) + 1)
                a_.activation(cols(u, b, 0, EB * L), cols(u, b, 0, EB * L), ACT.Silu).then_inc(u_ready, 1)

            def silu_z(b):
                if not known(b, 0):
                    hold(act, y_gated, b * 2)
                hold(act, rstd1_ok, 1)
                for eb in range(EB):
                    last = a_.activation(zs[:, eb * L:(eb + 1) * L], row(xall, b, eb), ACT.Silu,
                                         scale=rs1[:, 3, bass.ds(b * LB + eb, 1)], bias=nm1[:, bass.ds(b * LB + eb, 1)])
                last.then_inc(zs_ready, 1)

            def xdbl_copy(b, uses, turn):
                if not known(b, 0):
                    hold(act, bcs_out, b * 16)
                copy_use(xdbl[:, :], uses["XP"], turn, parts=DR + 2 * DS)

            def dt_eb(b, uses, turn, eb):
                k = uses["DT%d" % eb]
                hold(act, filled[k % 2], before(k, turn) + 1)
                a_.activation(spy[:, eb % 2 * L:(eb % 2 + 1) * L], bank(k)[:, :], ACT.Abs, bias=dtb[:, eb:eb + 1]).then_inc(abs_done, 1)
                a_.activation(cols(delta, b, eb * L, L), bank(k)[:, :], ACT.Relu, bias=dtb[:, eb:eb + 1]).then_inc(freed[k % 2], 1)

            def soft(b, i):
                s = slice(i * 2 * L, (i + 1) * 2 * L)
                hold(act, abs_done, b * EB + 2 * i + 2)
                a_.activation(spy[:, :], spy[:, :], ACT.Exp, scale=-1.0).then_inc(sp_step, 1)
                hold(act, sp_step, b * 2 + i + 1)
                a_.activation(spw[:, s], spy[:, :], ACT.Copy, bias=1.0).then_inc(soft_w, 1)

            def soft_log(b, i):
                s = slice(i * 2 * L, (i + 1) * 2 * L)
                hold(act, soft_loss, b * 2 + i + 1)
                a_.activation(spw[:, s], spw[:, s], ACT.Ln).then_inc(soft_ln, 1)

            def guess(rs, mv, done, base):
                a_.activation(rs[:, 0, :], mv[:, :, 1], ACT.Identity, bias=epsc[:, 0:1]).then_inc(act_step, 1)
                hold(act, act_step, base + 1)
                a_.activation(rs[:, 1, :], rs[:, 0, :], ACT.Ln).then_inc(act_step, 1)
                hold(act, act_step, base + 2)
                a_.activation(rs[:, 1, :], rs[:, 1, :], ACT.Exp, scale=-0.5).then_inc(done, 1)

            def guess_1():
                hold(act, stats1, 1)
                guess(rs1, mv1, rstd1_guess, 1)

            def guess_2(b):
                hold(act, stats2, b + 1)
                guess(rs2, mv2, guess2, 3 + 2 * b)

            def xln(b):
                hold(act, rstd2_ok, b + 1)
                hold(act, xln_out, b * 16 + 16)
                for i in range(LB):
                    last = a_.activation(xlnb[:, i, :], row(xall, b, i), ACT.Identity, scale=rs2[:, 3, i:i + 1], bias=nm2[:, i:i + 1])
                last.then_inc(xln_done, 1)

            def gate_T(uses, turn, i):
                copy_use(gT[:, i, :], uses["G%d" % i], turn)

            def half(b, h, tasks):
                for n in range(UPH):
                    unit(b, h, n)
                    for f in tasks.get(n, []):
                        f()

            def turn(b, uses, k, nxt=True, rest=True):
                tasks = {n: [] for n in range(2 * UPH)}
                if nxt:
                    tasks[3] += [lambda: ctx_T(uses, k, 0), lambda: ctx_T(uses, k, 1)]
                    tasks[8] += [lambda: tap(b + 1, uses, k, 0), lambda: tap(b + 1, uses, k, 1)]
                    tasks[13] += [lambda: tap(b + 1, uses, k, 2), lambda: tap(b + 1, uses, k, 3)]
                    tasks[15] += [lambda: silu_u(b + 1, uses, k)]
                if known(b, 0):
                    tasks[3] += [guess_1]
                tasks[2] += [lambda: soft(b, 1)]
                tasks[5] += [lambda: soft_log(b, 1)]
                tasks[6] += [lambda: silu_z(b)]
                if rest:
                    tasks[7] += [lambda: guess_2(b - 1)]
                    tasks[10] += [lambda: xln(b - 1)]
                    tasks[18] += [lambda: gate_T(uses, k, 0), lambda: gate_T(uses, k, 1)]
                if nxt:
                    tasks[21] += [lambda: xdbl_copy(b + 1, uses, k)]
                    tasks[24] += [lambda: dt_eb(b + 1, uses, k, 0), lambda: dt_eb(b + 1, uses, k, 1), lambda: soft(b + 1, 0)]
                    tasks[27] += [lambda: soft_log(b + 1, 0)]
                    tasks[28] += [lambda: dt_eb(b + 1, uses, k, 2), lambda: dt_eb(b + 1, uses, k, 3)]
                if rest:
                    tasks[30 if nxt else 23] += [lambda: gate_T(uses, k, 2), lambda: gate_T(uses, k, 3)]
                for h in range(2):
                    half(b, h, {n: tasks[h * UPH + n] for n in range(UPH)})

            hold(act, small_in, 16 * 9)
            hold(act, ident_ok, 2)
            a_.activation(Acol[:, :, :], Acol[:, :, :], ACT.Exp).then_inc(act_step, 1)
            copy_use(wT[:, 0, :], CONST["W0"], 0)
            copy_use(wT[:, 1, :], CONST["W1"], 0)
            copy_use(xpT[:, :, :].rearrange("p e k -> p (e k)"), CONST["XPT"], 0, width=EB * (DR + 2 * DS))
            copy_use(dtT[:, :], CONST["DTT"], 0, parts=DR)
            hold(act, act_step, 1)
            a_.activation(Acol[:, :, :], Acol[:, :, :], ACT.Copy, scale=-1.0).then_inc(consts_ok, 1)
            for eb in range(EB):
                last = a_.activation(diagD[:, eb, :], ident[:, :], ACT.Identity, scale=Dp[:, eb:eb + 1])
            last.then_inc(diag_ok, 1)

            for i in range(2):
                ctx_T(FIRST, 0, i)
            for eb in range(EB):
                tap(0, FIRST, 0, eb)
            silu_u(0, FIRST, 0)
            xdbl_copy(0, FIRST, 0)
            for i in range(2):
                for eb in range(2 * i, 2 * i + 2):
                    dt_eb(0, FIRST, 0, eb)
                if i == 0:
                    soft(0, 0)
                    soft_log(0, 0)
            hold(act, consts_ok, 1)
            turn(0, TURN0, 0, rest=False)
            with act.Fori(1, NB - 1) as b:
                turn(b, LOOP, b - 1)
            turn(NB - 1, LAST, 0, nxt=False)
            guess_2(NB - 1)
            xln(NB - 1)
            for i in range(LB):
                gate_T(TAIL, 0, i)

        @block.vector
        def _(dve):
            v_ = nc.vector
            for i in range(2):
                last = v_.memset(dA[i][:, :, 0:1], 0.0)
            last.then_inc(zeros_ok, 1)

            def scan(b, h, n):
                dve.wait_ge(exp_done, q0(b, h) + n + 1)
                dve.wait_ge(dbu_done, q0(b, h) + n + 1)
                v_.tensor_tensor_scan(ring[:, n % RING, :], dA[n % 2][:, :, :].rearrange("p e l -> p (e l)"), ring[:, n % RING, :],
                                      0.0, ALU.mult, ALU.add).then_inc(scan_done, 1)

            def times_c(b, h, n):
                c = n // 2
                dve.wait_ge(scan_done, q0(b, h) + n + 1)
                if n % 2 == 0:
                    dve.wait_ge(bc_in[c % 4], 32 * (b * 4 + 2 * h + c // 4 + 1))
                C = bc[:, c % 4, 1, n % 2:n % 2 + 1, :].to_broadcast([P, 2, L])
                states = ring[:, n % RING, :].rearrange("p (e l) -> p e l", e=2)
                v_.tensor_tensor(states, states, C, ALU.mult).then_inc(hc_done, 1)

            def conv(b, uses, turn, ebs):
                for j in range(1, DC):
                    for eb in ebs:
                        k = uses["X%d" % eb]
                        if j == 1:
                            dve.wait_ge(tap_done, b * EB + eb + 1)
                        else:
                            dve.wait_ge(conv_step[eb % 2], (b * EB // 2 + eb // 2) * (DC - 2) + j - 1)
                        o = cols(u, b, eb * L + j, L - j)
                        last = v_.scalar_tensor_tensor(o, bank(k)[:, 0:L - j], convw[:, eb, DC - 1 - j:DC - j], o, ALU.mult, ALU.add)
                        last.then_inc(conv_step[eb % 2] if j < DC - 1 else freed[k % 2], 1)

            def loss(b, i):
                s = slice(i * 2 * L, (i + 1) * 2 * L)
                hold(dve, soft_w, b * 2 + i + 1)
                v_.scalar_tensor_tensor(cols(du, b, i * 2 * L, 2 * L), spw[:, s], -1.0, spy[:, :], ALU.add, ALU.subtract).then_inc(soft_loss, 1)

            def drain_y(b, h):
                dve.wait_ge(acc_done, q0(b, h) + UPH)
                dve.wait_ge(zs_ready, b + 1)
                v_.tensor_tensor(g[:, :], yacc[:, :, :].rearrange("p e l -> p (e l)"), zs[:, h * 2 * L:(h + 1) * 2 * L], ALU.mult).then_inc(y_gated, 1)

            def add_y(b, h, uses, turn):
                for e in range(2):
                    k = uses["FE"[h] + str(e)]
                    eb = 2 * h + e
                    dve.wait_ge(filled[k % 2], before(k, turn) + 1)
                    xs = xall[:, bass.ds(b * LB, LB), eb * P:(eb + 1) * P]
                    v_.tensor_tensor(xs, bank(k)[:, :].rearrange("p (t e) -> p t e", t=LB), xs, ALU.add).then_inc(freed[k % 2], 1)

            def logit_copy(b, uses, turn):
                k = uses["LG"]
                dve.wait_ge(filled[k % 2], before(k, turn) + 1)
                v_.tensor_copy(logits[:, bass.ds(b * LB, LB), :].rearrange("p t e -> p (t e)"), bank(k)[:, 0:LB * 8]).then_inc(freed[k % 2], 1)

            def stats_2(b, uses, turn):
                for name in E:
                    k = uses[name]
                    hold(dve, freed[k % 2], before(k, turn) + 1)
                for t in range(LB):
                    last = v_.bn_stats(st2[:, t, :], row(xall, b, t))
                last.then_inc(dve_step, 1)
                hold(dve, dve_step, b + 2)
                for t in range(LB):
                    last = v_.bn_aggr(mv2[:, t, :], st2[:, t, :])
                last.then_inc(stats2, 1)

            def half(b, h, tasks):
                for n in range(UPH):
                    scan(b, h, n)
                    if n > 0:
                        times_c(b, h, n - 1)
                    for f in tasks.get(n, []):
                        f()
                times_c(b, h, UPH - 1)

            def turn(b, uses, k, nxt=True, rest=True):
                tasks = {n: [] for n in range(2 * UPH)}
                if rest:
                    tasks[1] += [lambda: drain_y(b - 1, 1)]
                    tasks[4] += [lambda: add_y(b - 1, 1, uses, k)]
                    tasks[5] += [lambda: stats_2(b - 1, uses, k)]
                if nxt:
                    tasks[8] += [lambda: conv(b + 1, uses, k, (0, 1))]
                    tasks[13] += [lambda: conv(b + 1, uses, k, (2, 3))]
                    tasks[26] += [lambda: loss(b + 1, 0)]
                tasks[3] += [lambda: loss(b, 1)]
                tasks[17] += [lambda: drain_y(b, 0)]
                tasks[21] += [lambda: add_y(b, 0, uses, k)]
                for h in range(2):
                    half(b, h, {n: tasks[h * UPH + n] for n in range(UPH)})
                if rest:
                    logit_copy(b - 1, uses, k)

            conv(0, FIRST, 0, (0, 1))
            conv(0, FIRST, 0, (2, 3))
            dve.wait_ge(x_in, 16)
            for t in range(NT):
                last = v_.bn_stats(st1[:, t, :], xall[:, t, :])
            last.then_inc(dve_step, 1)
            dve.wait_ge(dve_step, 1)
            for t in range(NT):
                last = v_.bn_aggr(mv1[:, t, :], st1[:, t, :])
            last.then_inc(stats1, 1)
            loss(0, 0)
            turn(0, TURN0, 0, rest=False)
            with dve.Fori(1, NB - 1) as b:
                turn(b, LOOP, b - 1)
            turn(NB - 1, LAST, 0, nxt=False)
            drain_y(NB - 1, 1)
            add_y(NB - 1, 1, TAIL, 0)
            stats_2(NB - 1, TAIL, 0)
            logit_copy(NB - 1, TAIL, 0)

        @block.tensor
        def _(pe):
            t_ = nc.tensor

            def use(k, turn):
                if k > 1:
                    pe.wait_ge(freed[k % 2], before(k, turn))

            def acc(b, h, n):
                if n == 0:
                    if known(b, 0) and h == 0:
                        pe.wait_ge(diag_ok, 1)
                    else:
                        pe.wait_ge(y_gated, b * 2 + h)
                    pe.wait_ge(u_ready, b + 1)
                    for e in range(2):
                        t_.matmul(yacc[:, e, :], diagD[:, 2 * h + e, :], cols(u, b, (2 * h + e) * L, L), start=True, stop=False)
                pe.wait_ge(hc_done, q0(b, h) + n + 1)
                for e in range(2):
                    last = t_.matmul(yacc[:, e, :], ident[:, :], ring[:, n % RING, e * L:(e + 1) * L], start=False, stop=(n == UPH - 1))
                last.then_inc(acc_done, 1)

            def ctx_T(b, uses, turn):
                pe.wait_ge(ctx_loaded, (b + 1) * 16)
                for i in range(KB):
                    k = uses["T%d" % i]
                    use(k, turn)
                    for t in range(LB):
                        last = t_.transpose(bank(k)[:, t * P:(t + 1) * P], ctx_rows[:, t, i * P:(i + 1) * P], ident[:, :])
                    last.then_inc(filled[k % 2], 1)

            def in_proj(uses, turn, eb):
                if eb == 0:
                    for i in range(KB):
                        k = uses["T%d" % i]
                        pe.wait_ge(freed[k % 2], before(k, turn) + 1)
                k = uses["X%d" % eb]
                use(k, turn)
                for i in range(KB):
                    last = t_.matmul(bank(k)[:, :], wT[:, i, eb * P:(eb + 1) * P], ctxT[:, i, :], start=(i == 0), stop=(i == KB - 1))
                last.then_inc(filled[k % 2], 1)

            def x_proj(b, uses, turn):
                k = uses["XP"]
                use(k, turn)
                hold(pe, u_ready, b + 1)
                for eb in range(EB):
                    last = t_.matmul(bank(k)[0:DR + 2 * DS, :], xpT[:, eb, :], cols(u, b, eb * L, L), start=(eb == 0), stop=(eb == EB - 1))
                last.then_inc(filled[k % 2], 1)

            def dt_proj(uses, turn, eb):
                if eb == 0:
                    k = uses["XP"]
                    pe.wait_ge(freed[k % 2], before(k, turn) + 1)
                k = uses["DT%d" % eb]
                use(k, turn)
                t_.matmul(bank(k)[:, :], dtT[:, eb * P:(eb + 1) * P], xdbl[0:DR, :], start=True, stop=True).then_inc(filled[k % 2], 1)

            def y_T(b, h, uses, turn):
                pe.wait_ge(y_gated, b * 2 + h + 1)
                for e in range(2):
                    k = uses["FE"[h] + str(e)]
                    use(k, turn)
                    for t in range(LB):
                        last = t_.transpose(bank(k)[:, t * P:(t + 1) * P], g[:, e * L + t * P:e * L + (t + 1) * P], ident[:, :])
                    last.then_inc(filled[k % 2], 1)

            def gate_T(b, uses, turn, i):
                pe.wait_ge(xln_done, b + 1)
                k = uses["G%d" % i]
                use(k, turn)
                for d in range(DI // P):
                    last = t_.transpose(bank(k)[:, d * P:(d + 1) * P], xlnb[:, i, d * P:(d + 1) * P], ident[:, :])
                last.then_inc(filled[k % 2], 1)

            def logits_of(uses, turn):
                for i in (LB - 2, LB - 1):
                    k = uses["G%d" % i]
                    pe.wait_ge(freed[k % 2], before(k, turn) + 1)
                k = uses["LG"]
                use(k, turn)
                for i in range(LB):
                    for d in range(DI // P):
                        last = t_.matmul(bank(k)[:, i * 8:(i + 1) * 8], gT[:, i, d * P:(d + 1) * P], gate[:, d, :], start=(d == 0), stop=(d == DI // P - 1))
                last.then_inc(filled[k % 2], 1)

            def half(b, h, tasks):
                for n in range(UPH):
                    if n > 0:
                        acc(b, h, n - 1)
                    for f in tasks.get(n, []):
                        f()
                acc(b, h, UPH - 1)

            def turn(b, uses, k, nxt=True, rest=True):
                tasks = {n: [] for n in range(2 * UPH)}
                if nxt:
                    tasks[0] += [lambda: ctx_T(b + 1, uses, k)]
                if rest:
                    tasks[1] += [lambda: y_T(b - 1, 1, uses, k)]
                if nxt:
                    tasks[4] += [lambda: in_proj(uses, k, 0), lambda: in_proj(uses, k, 1)]
                    tasks[9] += [lambda: in_proj(uses, k, 2), lambda: in_proj(uses, k, 3)]
                if rest:
                    tasks[14] += [lambda: gate_T(b - 1, uses, k, 0), lambda: gate_T(b - 1, uses, k, 1)]
                if nxt:
                    tasks[16] += [lambda: x_proj(b + 1, uses, k)]
                tasks[18] += [lambda: y_T(b, 0, uses, k)]
                if nxt:
                    tasks[20] += [lambda: dt_proj(uses, k, 0), lambda: dt_proj(uses, k, 1)]
                    tasks[24] += [lambda: dt_proj(uses, k, 2), lambda: dt_proj(uses, k, 3)]
                if rest:
                    tasks[27 if nxt else 20] += [lambda: gate_T(b - 1, uses, k, 2), lambda: gate_T(b - 1, uses, k, 3)]
                    tasks[29 if nxt else 22] += [lambda: logits_of(uses, k)]
                for h in range(2):
                    half(b, h, {n: tasks[h * UPH + n] for n in range(UPH)})

            pe.wait_ge(ident_ok, 2)
            pe.wait_ge(small_in, 16 * 9)
            for i in range(KB):
                k = CONST["W%d" % i]
                for eb in range(EB):
                    last = t_.transpose(bank(k)[:, eb * P:(eb + 1) * P], w_rows[:, eb, i * P:(i + 1) * P], ident[:, :])
                last.then_inc(filled[k % 2], 1)
            k, w = CONST["XPT"], DR + 2 * DS
            use(k, 0)
            for eb in range(EB):
                last = t_.transpose(bank(k)[:, eb * w:(eb + 1) * w], xp_rows[:, eb * P:(eb + 1) * P], ident[0:w, 0:w])
            last.then_inc(filled[k % 2], 1)
            k = CONST["DTT"]
            use(k, 0)
            for eb in range(EB):
                last = t_.transpose(bank(k)[0:DR, eb * P:(eb + 1) * P], dt_rows[:, eb, :], ident[:, :])
            last.then_inc(filled[k % 2], 1)

            ctx_T(0, FIRST, 0)
            for eb in range(EB):
                in_proj(FIRST, 0, eb)
            x_proj(0, FIRST, 0)
            for eb in range(EB):
                dt_proj(FIRST, 0, eb)
            turn(0, TURN0, 0, rest=False)
            with pe.Fori(1, NB - 1) as b:
                turn(b, LOOP, b - 1)
            turn(NB - 1, LAST, 0, nxt=False)
            y_T(NB - 1, 1, TAIL, 0)
            for i in range(LB):
                gate_T(NB - 1, TAIL, 0, i)
            logits_of(TAIL, 0)


NE, FF, TOPK = 8, 1024, 2
TOK = NB * L
KD = DI // P
KF = FF // P
SLOT_TILES = TOK * TOPK // P + NE - 1
ST = SLOT_TILES + 1
f32r, i32, u32 = mybir.dt.float32r, mybir.dt.int32, mybir.dt.uint32
AX = mybir.AxisListType


def ffn_block(nc, xall, logits, xln_dram, w0, w1, wo, y_dram, out):
    ctx = ExitStack()
    with ctx:
        def sb(name, shape, dt=fp32):
            return ctx.enter_context(nc.sbuf_tensor(name, shape, dt))

        def sem(name):
            return ctx.enter_context(nc.semaphore(name))

        NC = 6
        stage = [sb(f"stage{c}", [P, 4, 512]) for c in range(NC)]
        w_hi = [sb(f"w_hi{c}", [P, 4, 512], f32r) for c in range(NC)]
        w_lo = [sb(f"w_lo{c}", [P, 4, 512], f32r) for c in range(NC)]

        identf = sb("identf", [P, P])
        io8 = sb("io8", [P, NE])
        io_st = sb("io_st", [P, ST])
        io_cap = sb("io_cap", [P, NT])
        tokid = sb("tokid", [P, NT])
        first = sb("first", [P, NT])
        top = sb("top", [P, TOPK, NT])
        wgt = sb("wgt", [P, TOPK, NT])
        gap = sb("gap", [P, NT])
        expd = sb("expd", [P, NT])
        ntile = sb("ntile", [P, NE])
        tend = sb("tend", [P, NE])
        slotf = sb("slotf", [P, TOPK, NT])
        sloti = sb("sloti", [P, TOPK, NT], i32)
        quo_i = sb("quo_i", [P, TOPK * NT], i32)
        rem_i = sb("rem_i", [P, TOPK * NT], i32)
        texp = sb("texp", [P, ST])
        flag = sb("flag", [P, ST])
        texp_i = sb("texp_i", [P, ST], i32)
        nxt_i = sb("nxt_i", [P, ST], i32)
        flag_i = sb("flag_i", [P, ST], i32)
        tiles_i = sb("tiles_i", [P, 1], i32)
        turns_i = sb("turns_i", [P, 1], i32)
        tok_tab = sb("tok_tab", [P, ST], u32)
        index = [sb(f"index{i}", [P, 1], u32) for i in range(2)]
        index2 = [sb(f"index2{i}", [P, 1], u32) for i in range(8)]

        work = sb("work", [P, 8, 512])
        xg = [work[:, i, :] for i in range(2)]
        gated, inter = work[:, 2:4, :], work[:, 4:6, :]
        yb = [work[:, 6 + i, :] for i in range(2)]
        R = [w_lo[1 + k][:, :, :].rearrange("p a n -> p (a n)").rearrange("p (t r) -> p t r", r=P) for k in range(TOPK)]
        S = w_lo[3][:, :, :].rearrange("p a n -> p (a n)")[:, 0:TOPK * NT * ST].rearrange("p (t s) -> p t s", s=ST)
        flat = work[:, :, :].rearrange("p a n -> p (a n)")
        carved = [0]

        def carve(*shape):
            n = 1
            for d in shape:
                n *= d
            part = flat[:, carved[0]:carved[0] + n]
            carved[0] += n
            names = "abc"[:len(shape)]
            return part.rearrange("p (" + " ".join(names) + ") -> p " + " ".join(names), **dict(zip(names, shape)))

        ltri = carve(P)
        ones = carve(P)
        io128 = carve(P)
        segment, total, incl, over, base = (carve(NE, NT) for _ in range(5))
        cand, rest, ohs, pos = (carve(NT, NE) for _ in range(4))
        oh = carve(TOPK * NT, NE).rearrange("p (k t) e -> p k t e", k=TOPK)
        table8 = carve(ST, NE)
        quo, rem = carve(TOPK * NT), carve(TOPK * NT)
        tend_of, nxt = carve(ST), carve(ST)
        xT_hi, xT_lo = (sb(n, [P, KD, P], f32r) for n in ("xT_hi", "xT_lo"))
        iT_hi, iT_lo = (sb(n, [P, KF, P], f32r) for n in ("iT_hi", "iT_lo"))

        hp = [ctx.enter_context(nc.psum_tensor(f"hp{i}", [P, 512], fp32)) for i in range(4)]
        xp = ctx.enter_context(nc.psum_tensor("xp", [P, 512], fp32))
        yp = ctx.enter_context(nc.psum_tensor("yp", [P, 512], fp32))
        tp = [ctx.enter_context(nc.psum_tensor(f"tp{i}", [P, 512], fp32)) for i in range(2)]

        consts, routed, gap_exp, counted, tabled = (sem(n) for n in ("consts", "routed", "gap_exp", "counted", "tabled"))
        gap_ok, ohs_ok, RS_ok, tables_ok = (sem(n) for n in ("gap_ok", "ohs_ok", "RS_ok", "tables_ok"))
        stage_in = [sem(f"stage_in{c}") for c in range(NC)]
        hi_done, lo_done = sem("hi_done"), sem("lo_done")
        h_done, xT_done, y_done, iT_done = (sem(n) for n in ("h_done", "xT_done", "y_done", "iT_done"))
        silu_done, x_hi, x_lo, i_hi, i_lo, y_copied, inter_done = (sem(n) for n in
            ("silu_done", "x_hi", "x_lo", "i_hi", "i_lo", "y_copied", "inter_done"))
        index_ok, index2_ok, filling = sem("index_ok"), sem("index2_ok"), sem("filling")
        xg_in = [sem(f"xg_in{i}") for i in range(2)]
        y_out = [sem(f"y_out{i}") for i in range(2)]
        pair_in = [sem(f"pair_in{i}") for i in range(4)]
        half_sum, summed, out_done = sem("half_sum"), sem("summed"), sem("out_done")

        block = ctx.enter_context(nc.Block())
        LAST = SLOT_TILES - 1
        TURNS = LAST // 2
        assert LAST == 2 * TURNS
        MIN_TURNS = TOK * TOPK // P // 2

        def hold(eng, sem, value, least=1):
            if not isinstance(value, int):
                value = eng.to_reg(value)
                eng.wait_ge(sem, least)
            eng.wait_ge(sem, value)

        def weights_of(c, e):
            if c < 4:
                src = (w0, w1)[c // 2]
                return src[bass.ds(e, 1), :, (c % 2) * 512:(c % 2 + 1) * 512].rearrange("e (k p) f -> p (e k) f", p=P)
            return wo[bass.ds(e, 1), (c - 4) * 512:(c - 3) * 512, :].rearrange("e (k p) d -> p (e k) d", p=P)

        def splits(s, c):
            return 4 + NC * s + c + 1

        def loads_of(c, s):
            return 2 + s + (1 if c < 4 else 0)

        def pair_buf(i, k):
            return stage[i][:, k, :]

        @block.sync
        def _(sp):
            for c in range(NC):
                sp.dma_start(stage[c][:, :, :], weights_of(c, 0)).then_inc(stage_in[c], 16)
            maybe = (2 * MIN_TURNS + 1) * P
            sp.dma_start(y_dram[maybe:, :], xln_dram[0:SLOT_TILES * P - maybe, :]).then_inc(filling, 16)
            sp.wait_ge(tables_ok, 1)
            e0 = sp.value_load(texp_i[0:1, 0:1], min_val=0, max_val=NE - 1)
            for c in range(NC):
                sp.wait_ge(stage_in[c], 16)
                sp.dma_start(stage[c][:, :, :], weights_of(c, e0), cond=e0 > 0).then_inc(stage_in[c], 16)
            n0 = sp.value_load(nxt_i[0:1, 0:1], min_val=0, max_val=NE - 1)
            for c in range(4):
                sp.wait_ge(hi_done, c + 1)
                sp.wait_ge(lo_done, c + 1)
                sp.dma_start(stage[c][:, :, :], weights_of(c, n0)).then_inc(stage_in[c], 16)

            def reload(s, c, f, e):
                sp.wait_ge(hi_done, splits(s, c))
                sp.wait_ge(lo_done, splits(s, c))
                sp.dma_start(stage[c][:, :, :], weights_of(c, e), cond=f > 0).then_inc(stage_in[c], 16)

            def step(s, parity, y=True):
                f = sp.value_load(flag_i[0:1, bass.ds(s + 1, 1)], min_val=0, max_val=1)
                e = sp.value_load(nxt_i[0:1, bass.ds(s + 1, 1)], min_val=0, max_val=NE - 1)
                for c in range(4):
                    reload(s, c, f, e)
                if y:
                    store(s - 1, 1 - parity)
                f = sp.value_load(flag_i[0:1, bass.ds(s, 1)], min_val=0, max_val=1)
                e = sp.value_load(nxt_i[0:1, bass.ds(s, 1)], min_val=0, max_val=NE - 1)
                for c in range(4, NC):
                    reload(s, c, f, e)

            def store(s, parity):
                hold(sp, y_copied, s + 2)
                sp.dma_start(y_dram[bass.ds(s * P, P), :], yb[parity][:, :]).then_inc(y_out[parity], 16)

            step(0, 0, y=False)
            sp.wait_ge(filling, 16)
            turns = sp.value_load(turns_i[0:1, 0:1], min_val=MIN_TURNS, max_val=TURNS)
            with sp.Fori(0, TURNS) as t:
                with sp.If(turns > t):
                    step(2 * t + 1, 1)
                    step(2 * t + 2, 0)
            store(2 * turns, 0)
            with sp.Fori(0, NB) as b:
                for i in range(LB):
                    sp.wait_ge(summed, b * LB + i + 1)
                    sp.dma_start(out[bass.ds(b, 1), i * P:(i + 1) * P, :].rearrange("b p d -> p (b d)"),
                                 xall[:, bass.ds(b * LB + i, 1), :].rearrange("p a d -> p (a d)")).then_inc(out_done, 16)
            sp.wait_ge(out_done, 16 * NT)
            for c in range(NC):
                hold(sp, stage_in[c], 16 * loads_of(c, 2 * turns + 1), 16)

        @block.gpsimd
        def _(pool):
            g_ = nc.gpsimd
            g_.memset(identf[:, :], 0.0).then_inc(consts, 1)
            g_.memset(ltri[:, :], 1.0).then_inc(consts, 1)
            g_.memset(ones[:, :], 1.0).then_inc(consts, 1)
            g_.memset(segment[:, :, :], 1.0).then_inc(consts, 1)
            g_.iota(io8[:, :], [[1, NE]], base=0, channel_multiplier=0, allow_small_or_imprecise_dtypes=True).then_inc(consts, 1)
            g_.iota(io128[:, :], [[1, P]], base=0, channel_multiplier=0, allow_small_or_imprecise_dtypes=True).then_inc(consts, 1)
            g_.iota(io_st[:, :], [[1, ST]], base=0, channel_multiplier=0, allow_small_or_imprecise_dtypes=True).then_inc(consts, 1)
            g_.iota(io_cap[:, :], [[P, NT]], base=0, channel_multiplier=0, allow_small_or_imprecise_dtypes=True).then_inc(consts, 1)
            g_.iota(tokid[:, :], [[P, NT]], base=0, channel_multiplier=1, allow_small_or_imprecise_dtypes=True).then_inc(consts, 1)
            pool.wait_ge(consts, 9)
            g_.memset(segment[:, :, 0:1], 0.0).then_inc(consts, 1)
            g_.affine_select(out=identf[:, :], in_=identf[:, :], compare_op=ALU.not_equal, fill=1.0, base=0,
                             pattern=[[-1, P]], channel_multiplier=1).then_inc(consts, 1)
            g_.affine_select(out=ltri[:, :], in_=ltri[:, :], compare_op=ALU.is_gt, fill=0.0, base=0,
                             pattern=[[1, P]], channel_multiplier=-1).then_inc(consts, 1)

            def gather(half, parity):
                s = 2 * half + parity
                if not isinstance(s, int):
                    hold(pool, xg_in[parity], 16 * half, 16)
                g_.tensor_copy(index[parity][:, :], tok_tab[:, bass.ds(s, 1)]).then_inc(index_ok, 1)
                hold(pool, index_ok, s + 1)
                if not isinstance(s, int):
                    hold(pool, xT_done, s - 1)
                g_.indirect_dma_start(out=xg[parity][:, :], out_offset=None, in_=xln_dram,
                                      in_offset=bass.IndirectOffsetOnAxis(ap=index[parity][:, 0:1], axis=0)).then_inc(xg_in[parity], 16)

            pool.wait_ge(tabled, 1)
            gather(0, 0)
            gather(0, 1)
            turns = pool.value_load(turns_i[0:1, 0:1], min_val=MIN_TURNS, max_val=TURNS)
            with pool.Fori(0, TURNS) as t:
                with pool.If(turns > t):
                    gather(t + 1, 0)
                    gather(t + 1, 1)

            hold(pool, y_out[0], 16 * turns + 16, 16)
            hold(pool, y_out[1], 16 * turns, 16)
            hold(pool, lo_done, splits(2 * turns, NC - 1))
            for c in range(4):
                hold(pool, stage_in[c], 16 * loads_of(c, 2 * turns + 1), 16)

            def pair(b, i):
                for k in range(TOPK):
                    n = 2 * i + k
                    if not isinstance(b, int):
                        hold(pool, pair_in[i], 32 * b, 16)
                    g_.tensor_copy(index2[n][:, :], sloti[:, k, bass.ds(b * LB + i, 1)].bitcast(u32)).then_inc(index2_ok, 1)
                for k in range(TOPK):
                    n = 2 * i + k
                    hold(pool, index2_ok, (b * LB + i) * TOPK + k + 1)
                    if not isinstance(b, int):
                        hold(pool, summed, (b - 1) * LB + i + 1)
                    g_.indirect_dma_start(out=pair_buf(i, k), out_offset=None, in_=y_dram,
                                          in_offset=bass.IndirectOffsetOnAxis(ap=index2[n][:, 0:1], axis=0)).then_inc(pair_in[i], 16)

            for i in range(LB):
                pair(0, i)
            with pool.Fori(1, NB) as b:
                for i in range(LB):
                    pair(b, i)

        @block.scalar
        def _(act):
            s_ = nc.scalar
            act.wait_ge(gap_ok, 1)
            s_.activation(expd[:, :], gap[:, :], ACT.Exp).then_inc(gap_exp, 1)

            def split(c, loads):
                hold(act, stage_in[c], 16 * loads, 16)
                s_.copy(w_hi[c][:, :, :], stage[c][:, :, :]).then_inc(hi_done, 1)

            def split_if(f, s, c):
                with act.If(f > 0):
                    split(c, loads_of(c, s))
                with act.Else():
                    hold(act, hi_done, splits(s, c) - 1)
                    act.sem_inc(hi_done, 1)

            def x_part(s):
                hold(act, xT_done, s + 1)
                s_.copy(xT_hi[:, :, :], xp[:, :].rearrange("p (k t) -> p k t", t=P)).then_inc(x_hi, 1)

            def step(half, parity, y=True):
                s = 2 * half + parity
                f = act.value_load(flag_i[0:1, bass.ds(s + 1, 1)], min_val=0, max_val=1)
                for h in range(2):
                    hold(act, h_done, 4 * s + h + 1)
                    if h == 0 and y:
                        hold(act, inter_done, 2 * s)
                    s_.activation(gated[:, h, :], hp[h][:, :], ACT.Silu).then_inc(silu_done, 1)
                    split_if(f, s, h)
                hold(act, h_done, 4 * s + 3)
                split_if(f, s, 2)
                x_part(s + 1)
                hold(act, h_done, 4 * s + 4)
                split_if(f, s, 3)
                if y:
                    out_part(half + parity - 1, 1 - parity)
                f = act.value_load(flag_i[0:1, bass.ds(s, 1)], min_val=0, max_val=1)
                for h in range(2):
                    hold(act, iT_done, 2 * s + h + 1)
                    s_.copy(iT_hi[:, 4 * h:4 * h + 4, :], tp[h][:, :].rearrange("p (k t) -> p k t", t=P)).then_inc(i_hi, 1)
                for c in range(4, NC):
                    split_if(f, s, c)

            def out_part(half, parity):
                hold(act, y_done, 2 * half + parity + 1)
                if not isinstance(half, int) or half > 0:
                    hold(act, y_out[parity], 16 * half, 16)
                s_.copy(yb[parity][:, :], yp[:, :]).then_inc(y_copied, 1)

            act.sem_inc(y_copied, 1)
            act.wait_ge(tables_ok, 1)
            for c in range(4):
                split(c, 2)
            x_part(0)
            step(0, 0, y=False)
            step(0, 1)
            step(1, 0)
            turns = act.value_load(turns_i[0:1, 0:1], min_val=MIN_TURNS, max_val=TURNS)
            with act.Fori(0, TURNS - 1) as t:
                with act.If(turns > t + 1):
                    step(t + 1, 1)
                    step(t + 2, 0)
            out_part(turns, 0)

        @block.vector
        def _(dve):
            v = nc.vector

            def over_e(a, n=NT):
                return a.unsqueeze(2).to_broadcast([P, n, NE])

            def over_t(a, n=NT):
                return a.unsqueeze(1).to_broadcast([P, n, NE])

            dve.wait_ge(consts, 12)
            source = logits
            for k in range(TOPK):
                n = 6 * k
                if k:
                    dve.wait_ge(routed, 6)
                v.tensor_reduce(top[:, k, :], source[:, :, :], axis=AX.X, op=ALU.max).then_inc(routed, 1)
                dve.wait_ge(routed, n + 1)
                v.tensor_tensor(cand[:, :, :], source[:, :, :], over_e(top[:, k, :]), ALU.is_equal).then_inc(routed, 1)
                dve.wait_ge(routed, n + 2)
                v.scalar_tensor_tensor(cand[:, :, :], cand[:, :, :], -float(NE), over_t(io8[:, :]), ALU.mult, ALU.add).then_inc(routed, 1)
                dve.wait_ge(routed, n + 3)
                v.tensor_reduce(first[:, :], cand[:, :, :], axis=AX.X, op=ALU.min).then_inc(routed, 1)
                dve.wait_ge(routed, n + 4)
                v.tensor_tensor(oh[:, k, :, :], cand[:, :, :], over_e(first[:, :]), ALU.is_equal).then_inc(routed, 1)
                if k == 0:
                    dve.wait_ge(routed, 5)
                    v.scalar_tensor_tensor(rest[:, :, :], oh[:, 0, :, :], -3e38, logits[:, :, :], ALU.mult, ALU.add).then_inc(routed, 1)
                    source = rest
            dve.wait_ge(routed, 11)
            v.tensor_tensor(gap[:, :], top[:, 1, :], top[:, 0, :], ALU.subtract).then_inc(gap_ok, 1)
            v.tensor_tensor(ohs[:, :, :], oh[:, 0, :, :], oh[:, 1, :, :], ALU.add).then_inc(ohs_ok, 1)

            dve.wait_ge(gap_exp, 1)
            v.tensor_scalar(wgt[:, 1, :], expd[:, :], 1.0, None, ALU.add).then_inc(routed, 1)
            dve.wait_ge(routed, 12)
            v.reciprocal(wgt[:, 0, :], wgt[:, 1, :]).then_inc(routed, 1)
            dve.wait_ge(routed, 13)
            v.tensor_tensor(wgt[:, 1, :], wgt[:, 0, :], expd[:, :], ALU.mult).then_inc(routed, 1)

            dve.wait_ge(counted, 2)
            v.tensor_copy(total[:, :, :].rearrange("p e t -> p t e"), hp[1][:, 0:P].rearrange("p (t e) -> p t e", e=NE)).then_inc(routed, 1)
            dve.wait_ge(routed, 15)
            v.tensor_tensor_scan(incl[:, :, :].rearrange("p e t -> p (e t)"), segment[:, :, :].rearrange("p e t -> p (e t)"),
                                 total[:, :, :].rearrange("p e t -> p (e t)"), 0.0, ALU.mult, ALU.add).then_inc(routed, 1)
            dve.wait_ge(routed, 16)
            v.tensor_tensor(over[:, :, :], incl[:, :, NT - 1:NT].to_broadcast([P, NE, NT]),
                            io_cap[:, :].unsqueeze(1).to_broadcast([P, NE, NT]), ALU.is_gt).then_inc(routed, 1)
            dve.wait_ge(routed, 17)
            v.tensor_reduce(ntile[:, :], over[:, :, :], axis=AX.X, op=ALU.add).then_inc(routed, 1)
            dve.wait_ge(routed, 18)
            v.tensor_tensor_scan(tend[:, :], ones[:, 0:NE], ntile[:, :], 0.0, ALU.mult, ALU.add).then_inc(routed, 1)
            dve.wait_ge(routed, 19)
            v.tensor_tensor(ntile[:, :], tend[:, :], ntile[:, :], ALU.subtract).then_inc(routed, 1)
            v.tensor_tensor(incl[:, :, :], incl[:, :, :], total[:, :, :], ALU.subtract).then_inc(routed, 1)
            dve.wait_ge(routed, 21)
            v.scalar_tensor_tensor(base[:, :, :], ntile[:, :].unsqueeze(2).to_broadcast([P, NE, NT]), float(P), incl[:, :, :], ALU.mult, ALU.add).then_inc(routed, 1)
            dve.wait_ge(routed, 22)
            v.tensor_tensor(pos[:, :, :], hp[0][:, 0:P].rearrange("p (t e) -> p t e", e=NE),
                            base[:, :, :].rearrange("p e t -> p t e"), ALU.add).then_inc(routed, 1)
            dve.wait_ge(routed, 23)
            for k in range(TOPK):
                v.tensor_tensor(oh[:, k, :, :], oh[:, k, :, :], pos[:, :, :], ALU.mult).then_inc(routed, 1)
            dve.wait_ge(routed, 25)
            v.tensor_reduce(slotf[:, :, :].rearrange("p k t -> p (k t)"), oh[:, :, :, :].rearrange("p k t e -> p (k t) e"), axis=AX.X, op=ALU.add).then_inc(routed, 1)
            dve.wait_ge(routed, 26)
            v.tensor_copy(sloti[:, :, :], slotf[:, :, :]).then_inc(routed, 1)
            dve.wait_ge(routed, 27)
            slots = sloti[:, :, :].rearrange("p k t -> p (k t)")
            v.tensor_scalar(quo_i[:, :], slots, 7, None, ALU.logical_shift_right).then_inc(routed, 1)
            v.tensor_scalar(rem_i[:, :], slots, P - 1, None, ALU.bitwise_and).then_inc(routed, 1)
            dve.wait_ge(routed, 29)
            v.tensor_copy(quo[:, :], quo_i[:, :]).then_inc(routed, 1)
            v.tensor_copy(rem[:, :], rem_i[:, :]).then_inc(routed, 1)
            dve.wait_ge(routed, 31)
            tend_b = over_t(tend[:, :], ST)
            v.tensor_tensor(table8[:, :, :], tend_b, over_e(io_st[:, :], ST), ALU.is_le).then_inc(routed, 1)
            dve.wait_ge(routed, 32)
            v.tensor_reduce(texp[:, :], table8[:, :, :], axis=AX.X, op=ALU.add).then_inc(routed, 1)
            dve.wait_ge(routed, 33)
            v.tensor_scalar(texp[:, :], texp[:, :], float(NE - 1), None, ALU.min).then_inc(routed, 1)
            dve.wait_ge(routed, 34)
            v.memset(flag[:, 0:1], 1.0).then_inc(routed, 1)
            v.tensor_tensor(flag[:, 1:ST], texp[:, 1:ST], texp[:, 0:ST - 1], ALU.not_equal).then_inc(routed, 1)
            v.tensor_tensor(table8[:, :, :], over_t(io8[:, :], ST), over_e(texp[:, :], ST), ALU.is_equal).then_inc(routed, 1)
            dve.wait_ge(routed, 37)
            v.tensor_tensor(table8[:, :, :], table8[:, :, :], tend_b, ALU.mult).then_inc(routed, 1)
            dve.wait_ge(routed, 38)
            v.tensor_reduce(tend_of[:, :], table8[:, :, :], axis=AX.X, op=ALU.add).then_inc(routed, 1)
            dve.wait_ge(routed, 39)
            v.tensor_tensor(table8[:, :, :], tend_b, over_e(tend_of[:, :], ST), ALU.is_le).then_inc(routed, 1)
            dve.wait_ge(routed, 40)
            v.tensor_reduce(nxt[:, :], table8[:, :, :], axis=AX.X, op=ALU.add).then_inc(routed, 1)
            dve.wait_ge(routed, 41)
            v.tensor_scalar(nxt[:, :], nxt[:, :], float(NE - 1), None, ALU.min).then_inc(routed, 1)
            dve.wait_ge(routed, 42)
            v.tensor_copy(texp_i[:, :], texp[:, :]).then_inc(routed, 1)
            v.tensor_copy(nxt_i[:, :], nxt[:, :]).then_inc(routed, 1)
            v.tensor_copy(flag_i[:, :], flag[:, :]).then_inc(routed, 1)
            v.tensor_copy(tiles_i[:, :], tend[:, NE - 1:NE]).then_inc(routed, 1)
            dve.wait_ge(routed, 46)
            v.tensor_scalar(turns_i[:, :], tiles_i[:, :], 1, None, ALU.logical_shift_right).then_inc(routed, 1)
            dve.wait_ge(routed, 47)
            dve.sem_inc(tables_ok, 1)
            v.tensor_tensor(S, quo[:, :].unsqueeze(2).to_broadcast([P, TOPK * NT, ST]),
                            io_st[:, :].unsqueeze(1).to_broadcast([P, TOPK * NT, ST]), ALU.is_equal).then_inc(routed, 1)
            dve.wait_ge(routed, 48)
            for k in range(TOPK):
                part = S[:, k * NT:(k + 1) * NT, :]
                v.tensor_tensor(part, part.bitcast(fp32), tokid[:, :].unsqueeze(2).to_broadcast([P, NT, ST]), ALU.mult).then_inc(routed, 1)
            dve.wait_ge(routed, 50)
            for k in range(TOPK):
                v.tensor_tensor(R[k], rem[:, k * NT:(k + 1) * NT].unsqueeze(2).to_broadcast([P, NT, P]),
                                io128[:, :].unsqueeze(1).to_broadcast([P, NT, P]), ALU.is_equal).then_inc(RS_ok, 1)

            def split(c, done):
                hold(dve, hi_done, done)
                v.tensor_tensor(w_lo[c][:, :, :], stage[c][:, :, :], w_hi[c][:, :, :].bitcast(fp32), ALU.subtract).then_inc(lo_done, 1)

            split(0, 1)
            dve.wait_ge(counted, 2 + TOPK)
            v.tensor_copy(tok_tab[:, :], hp[2][:, 0:ST]).then_inc(tabled, 1)

            def split_if(f, s, c):
                with dve.If(f > 0):
                    split(c, splits(s, c))
                with dve.Else():
                    hold(dve, lo_done, splits(s, c) - 1)
                    dve.sem_inc(lo_done, 1)

            def x_part(s):
                hold(dve, x_hi, s + 1)
                v.tensor_tensor(xT_lo[:, :, :], xp[:, :].rearrange("p (k t) -> p k t", t=P), xT_hi[:, :, :].bitcast(fp32), ALU.subtract).then_inc(x_lo, 1)

            def step(s, nxt=True):
                f = dve.value_load(flag_i[0:1, bass.ds(s + 1, 1)], min_val=0, max_val=1)
                split_if(f, s, 0)
                split_if(f, s, 1)
                for h in range(2):
                    hold(dve, h_done, 4 * s + 3 + h)
                    hold(dve, silu_done, 2 * s + h + 1)
                    if not (isinstance(s, int) and s == 0):
                        hold(dve, iT_done, 2 * s - 1 + h)
                    v.tensor_tensor(inter[:, h, :], hp[2 + h][:, :], gated[:, h, :], ALU.mult).then_inc(inter_done, 1)
                    if h == 0:
                        split_if(f, s, 2)
                if nxt:
                    x_part(s + 1)
                split_if(f, s, 3)
                f = dve.value_load(flag_i[0:1, bass.ds(s, 1)], min_val=0, max_val=1)
                for h in range(2):
                    hold(dve, i_hi, 2 * s + h + 1)
                    v.tensor_tensor(iT_lo[:, 4 * h:4 * h + 4, :], tp[h][:, :].rearrange("p (k t) -> p k t", t=P),
                                    iT_hi[:, 4 * h:4 * h + 4, :].bitcast(fp32), ALU.subtract).then_inc(i_lo, 1)
                for c in range(4, NC):
                    split_if(f, s, c)

            split(1, 2)
            split(2, 3)
            x_part(0)
            split(3, 4)
            step(0)
            turns = dve.value_load(turns_i[0:1, 0:1], min_val=MIN_TURNS, max_val=TURNS)
            with dve.Fori(0, TURNS) as t:
                with dve.If(turns > t):
                    step(2 * t + 1)
                    step(2 * t + 2)

            with dve.Fori(0, NB) as b:
                for i in range(LB):
                    hold(dve, pair_in[i], 32 * b + 32, 16)
                    tile = xall[:, bass.ds(b * LB + i, 1), :].rearrange("p a d -> p (a d)")
                    for k in range(TOPK):
                        if k:
                            hold(dve, half_sum, b * LB + i + 1)
                        v.scalar_tensor_tensor(tile, pair_buf(i, k), wgt[:, k, bass.ds(b * LB + i, 1)], tile,
                                               ALU.mult, ALU.add).then_inc(summed if k else half_sum, 1)

        @block.tensor
        def _(pe):
            t_ = nc.tensor
            pe.wait_ge(consts, 12)
            pe.wait_ge(ohs_ok, 1)
            both = ohs[:, :, :].rearrange("p t e -> p (t e)")
            t_.matmul(hp[0][:, 0:P], ltri[:, :], both, start=True, stop=True).then_inc(counted, 1)
            t_.matmul(hp[1][:, 0:P], ones[:, :], both, start=True, stop=True).then_inc(counted, 1)
            for k in range(TOPK):
                pe.wait_ge(RS_ok, k + 1)
                for t in range(NT):
                    last = t_.matmul(hp[2][:, 0:ST], R[k][:, t, :], S[:, k * NT + t, :], start=(k + t == 0), stop=(k * NT + t == TOPK * NT - 1))
                last.then_inc(counted, 1)

            def x_T(half, parity):
                s = 2 * half + parity
                pe.wait_ge(xg_in[parity], 16 * half + 16)
                if not (isinstance(s, int) and s == 0):
                    pe.wait_ge(x_lo, s)
                for k in range(KD):
                    last = t_.transpose(xp[:, k * P:(k + 1) * P], xg[parity][:, k * P:(k + 1) * P], identf[:, :])
                last.then_inc(xT_done, 1)

            def product(bank, a_hi, a_lo, ks, b_hi, b_lo, start, stop):
                for k in ks:
                    b = k % 4
                    t_.matmul(bank[:, :], a_hi[:, k, :], b_hi[:, b, :], start=(start and k == ks[0]), stop=False)
                    t_.matmul(bank[:, :], a_hi[:, k, :], b_lo[:, b, :], start=False, stop=False)
                    last = t_.matmul(bank[:, :], a_lo[:, k, :], b_hi[:, b, :], start=False, stop=(stop and k == ks[-1]))
                return last

            def inner(s):
                for c in range(4):
                    if c == 0:
                        pe.wait_ge(x_lo, s + 1)
                    ready = c + 1 if isinstance(s, int) and s == 0 else splits(s - 1, c)
                    pe.wait_ge(lo_done, ready)
                    if not (isinstance(s, int) and s == 0):
                        if c < 2:
                            pe.wait_ge(silu_done, 2 * s - 1 + c)
                        else:
                            pe.wait_ge(inter_done, 2 * s - 3 + c)
                    product(hp[c], xT_hi, xT_lo, range(4), w_hi[c], w_lo[c], True, True).then_inc(h_done, 1)

            def outer(s):
                pe.wait_ge(i_lo, 2 * s + 2)
                pe.wait_ge(y_copied, s + 1)
                pe.wait_ge(lo_done, splits(s, 4))
                product(yp, iT_hi, iT_lo, range(4), w_hi[4], w_lo[4], True, False)
                pe.wait_ge(lo_done, splits(s, 5))
                product(yp, iT_hi, iT_lo, range(4, 8), w_hi[5], w_lo[5], False, True).then_inc(y_done, 1)

            def inter_T(s):
                for h in range(2):
                    pe.wait_ge(inter_done, 2 * s + h + 1)
                    if not (isinstance(s, int) and s == 0):
                        pe.wait_ge(i_lo, 2 * s - 1 + h)
                    for k in range(4):
                        last = t_.transpose(tp[h][:, k * P:(k + 1) * P], inter[:, h, k * P:(k + 1) * P], identf[:, :])
                    last.then_inc(iT_done, 1)

            x_T(0, 0)
            inner(0)
            x_T(0, 1)
            inter_T(0)
            pe.wait_ge(tables_ok, 1)
            turns = pe.value_load(turns_i[0:1, 0:1], min_val=MIN_TURNS, max_val=TURNS)
            with pe.Fori(0, TURNS) as t:
                with pe.If(turns > t):
                    for j in range(2):
                        s = 2 * t + 1 + j
                        inner(s)
                        x_T(t + 1, j)
                        outer(s - 1)
                        inter_T(s)
            outer(2 * turns)


def model(nc, x, ctx_in, in_proj_w, conv_w, conv_b, x_proj_w, dt_proj_w, dt_proj_b, A_log, D, gate_w, w0, w1, wo, out):
    ctx = ExitStack()
    with ctx:
        xall = ctx.enter_context(nc.sbuf_tensor("xall", [P, NT, DI], fp32))
        logits = ctx.enter_context(nc.sbuf_tensor("logits", [P, NT, 8], fp32))
        bcs = nc.dram_tensor("bcs", [NB, 2 * DS, L], fp32).ap()
        xln_dram = nc.dram_tensor("xln_dram", [TOK, DI], fp32).ap()
        y_dram = nc.dram_tensor("y_dram", [SLOT_TILES * P, DI], fp32).ap()
        mamba_block(nc, x, ctx_in, in_proj_w, conv_w, conv_b, x_proj_w, dt_proj_w, dt_proj_b, A_log, D, gate_w, xall, logits, bcs, xln_dram)
        ffn_block(nc, xall, logits, xln_dram, w0, w1, wo, y_dram, out)


_INS = (['x', 'ctx_1024'] + ['L0_xattn_' + n for n in ('in_proj_w', 'conv_w', 'conv_b', 'x_proj_w', 'dt_proj_w', 'dt_proj_b', 'A_log', 'D')]
        + ['L0_ffn_' + n for n in ('gate_kernel', 'w0_kernel', 'w1_kernel', 'wo_kernel')])


def kernel(**inputs):
    import numpy as _np
    import concourse.bacc as _bacc
    from concourse import mybir as _mybir
    from concourse.bass_utils import run_bass_kernel_spmd as _run
    nc = _bacc.Bacc("TRN2", target_bir_lowering=False, num_devices=1)
    arrays, args = {}, []
    for name in _INS:
        a = _np.ascontiguousarray(inputs[name])
        arrays[f"in_{name}_dram"] = a
        args.append(nc.dram_tensor(f"in_{name}_dram", a.shape, _mybir.dt.from_np(a.dtype), kind="ExternalInput").ap())
    args.append(nc.dram_tensor("out_0_dram", (4, 512, 512), _mybir.dt.float32, kind="ExternalOutput").ap())
    model(nc, *args)
    r = _run(nc, [arrays], core_ids=[0])
    return r.results[0]["out_0_dram"]
```

```python
import concourse.bass as bass
from concourse import mybir
from contextlib import ExitStack

NB, L, DM, DI = 4, 512, 256, 512
DS, DC, DR = 16, 4, 16
P = 128
EB = DI // P
LB = L // P
KB = DM // P
RING = 8
UPH = DS
NT = NB * LB
EPS = 1e-5

fp32 = mybir.dt.float32
ALU = mybir.AluOpType
ACT = mybir.ActivationFunctionType


def mamba_block(nc, x, ctx_in, in_proj_w, conv_w, conv_b, x_proj_w, dt_proj_w, dt_proj_b, A_log, D, gate_w,
                xall, logits, bcs, xln_dram, out):
    ctx = ExitStack()
    with ctx:
        def sb(name, shape, dt=fp32):
            return ctx.enter_context(nc.sbuf_tensor(name, shape, dt))

        def sem(name):
            return ctx.enter_context(nc.semaphore(name))

        ident = sb("ident", [P, P])
        ctx_rows = sb("ctx_rows", [P, LB, DM])
        gT = sb("gT", [P, LB, DI])
        w_rows = gT[:, 0:2, :].rearrange("p a (c d) -> p (a c) d", d=DM)
        wT = sb("wT", [P, KB, DI])
        xp_rows = gT[0:DR + 2 * DS, 2, :]
        xpT = sb("xpT", [P, EB, DR + 2 * DS])
        dt_rows = gT[:, 3, 0:EB * DR].rearrange("p (e r) -> p e r", e=EB)
        dtT = sb("dtT", [DR, DI])
        convw = sb("convw", [P, EB, DC])
        convb = sb("convb", [P, EB])
        dtb = sb("dtb", [P, EB])
        Dp = sb("Dp", [P, EB])
        Acol = sb("Acol", [P, EB, DS])
        gate = sb("gate", [P, DI // P, 8])
        epsc = sb("epsc", [P, 1])
        st1 = sb("st1", [P, NT, 6])
        mv1 = sb("mv1", [P, NT, 2])
        rs1 = sb("rs1", [P, 4, NT])
        nm1 = sb("nm1", [P, NT])
        st2 = sb("st2", [P, LB, 6])
        mv2 = sb("mv2", [P, LB, 2])
        rs2 = sb("rs2", [P, 4, LB])
        nm2 = sb("nm2", [P, LB])
        ctxT = sb("ctxT", [P, KB, L])
        u = sb("u", [P, 2, EB * L])
        delta = sb("delta", [P, 2, EB * L])
        du = sb("du", [P, 2, EB * L])
        zs = sb("zs", [P, EB * L])
        xdbl = sb("xdbl", [DR + 2 * DS, L])
        spy = sb("spy", [P, 2 * L])
        spw = sb("spw", [P, EB * L])
        bc = sb("bc", [P, 4, 2, 2, L])
        ring = sb("ring", [P, RING, 2 * L])
        diagD = sb("diagD", [P, EB, P])
        g = sb("g", [P, 2 * L])
        xlnb = sb("xlnb", [P, LB, DI])

        dA = [ctx.enter_context(nc.psum_tensor(f"dA{i}", [P, 2, L], fp32)) for i in range(2)]
        yacc = ctx.enter_context(nc.psum_tensor("yacc", [P, 2, L], fp32))
        pp = [ctx.enter_context(nc.psum_tensor(f"pp{i}", [P, L], fp32)) for i in range(2)]

        x_in, ctx_loaded, small_in = sem("x_in"), sem("ctx_loaded"), sem("small_in")
        ident_ok, zeros_ok, diag_ok = sem("ident_ok"), sem("zeros_ok"), sem("diag_ok")
        exp_done, dbu_done, scan_done, hc_done, acc_done = (sem(n) for n in
            ("exp_done", "dbu_done", "scan_done", "hc_done", "acc_done"))
        bc_in = [sem(f"bc_in{i}") for i in range(4)]
        filled = [sem(f"filled{i}") for i in range(2)]
        freed = [sem(f"freed{i}") for i in range(2)]
        consts_ok, stats1, rstd1_guess, rstd1_ok = sem("consts_ok"), sem("stats1"), sem("rstd1_guess"), sem("rstd1_ok")
        tap_done, u_ready, bcs_out = sem("tap_done"), sem("u_ready"), sem("bcs_out")
        x1_out = sem("x1_out")
        conv_step = [sem(f"conv_step{i}") for i in range(2)]
        sp_step, soft_w, soft_ln, soft_loss, soft_sub, delta_ready, du_ready, zs_ready = (sem(n) for n in
            ("sp_step", "soft_w", "soft_ln", "soft_loss", "soft_sub", "delta_ready", "du_ready", "zs_ready"))
        abs_done, y_gated = sem("abs_done"), sem("y_gated")
        stats2, guess2, rstd2_ok, xln_done, xln_out = (sem(n) for n in
            ("stats2", "guess2", "rstd2_ok", "xln_done", "xln_out"))
        pool_step, dve_step, act_step = sem("pool_step"), sem("dve_step"), sem("act_step")

        def order(names, base):
            return {n: base + i for i, n in enumerate(names)}

        T, X, XB, XP = ["T0", "T1"], ["X0", "X1"], ["X2", "X3"], ["XP"]
        DTA, DTB, E, F = ["DT0", "DT1"], ["DT2", "DT3"], ["E0", "E1"], ["F0", "F1"]
        GA, GB = ["G0", "G1"], ["G2", "G3", "LG"]
        CONST = order(["W0", "W1", "XPT", "DTT"], 0)
        FIRST = order(T + X + XB + XP + DTA + DTB, 4)
        TURN0 = order(T + X + XB + XP + F + DTA + DTB, 15)
        LOOP = order(T + E + X + XB + GA + XP + F + DTA + DTB + GB, 28)
        PER_TURN = 20
        TURNS = NB - 2
        LAST = order(E + GA + GB + F, 28 + TURNS * PER_TURN)
        TAIL = order(E + GA + GB, 28 + TURNS * PER_TURN + 9)

        def bank(k):
            return pp[k % 2]

        def before(k, turns=0):
            return k // 2 + (PER_TURN // 2) * turns

        block = ctx.enter_context(nc.Block())

        def cols(t, b, lo, n):
            if isinstance(b, int):
                return t[:, b % 2, lo:lo + n]
            return t[:, bass.ds(b % 2, 1), lo:lo + n].rearrange("p a n -> p (a n)")

        def row(t, b, i):
            return t[:, bass.ds(b * LB + i, 1), :].rearrange("p a n -> p (a n)")

        def q0(b, h):
            return b * (2 * UPH) + h * UPH

        def known(b, value):
            return isinstance(b, int) and b == value

        def hold(eng, sem, value, least=1):
            if not isinstance(value, int):
                value = eng.to_reg(value)
                eng.wait_ge(sem, least)
            eng.wait_ge(sem, value)

        def start(b, h, n):
            return known(b, 0) and h == 0 and n < 2

        def fresh(b, h, n):
            return known(b, 0) and h == 0 and n < RING

        def soft(eng, b, i):
            s = slice(i * 2 * L, (i + 1) * 2 * L)
            d, o = cols(delta, b, i * 2 * L, 2 * L), cols(du, b, i * 2 * L, 2 * L)

            def sub():
                hold(eng, soft_loss, b * 2 + i + 1)
                eng.tensor_tensor(d, d, o, ALU.subtract).then_inc(soft_sub, 1)

            def add():
                hold(eng, soft_sub, b * 2 + i + 1)
                hold(eng, soft_ln, b * 2 + i + 1)
                eng.tensor_tensor(d, d, spw[:, s], ALU.add).then_inc(delta_ready, 1)

            def times_u():
                hold(eng, delta_ready, b * 2 + i + 1)
                hold(eng, u_ready, b + 1)
                eng.tensor_tensor(o, d, cols(u, b, i * 2 * L, 2 * L), ALU.mult).then_inc(du_ready, 1)

            return [sub, add, times_u]


        @block.sync
        def _(sp):
            sp.dma_start(w_rows, in_proj_w.rearrange("(e p) d -> p e d", p=P)).then_inc(small_in, 16)
            sp.dma_start(xp_rows, x_proj_w).then_inc(small_in, 16)
            sp.dma_start(dt_rows, dt_proj_w.rearrange("(e p) r -> p e r", p=P)).then_inc(small_in, 16)
            sp.dma_start(convw[:, :, :], conv_w.rearrange("(e p) c -> p e c", p=P)).then_inc(small_in, 16)
            with nc.allow_non_contiguous_dma(reason="512 values, once"):
                for t, s in ((convb, conv_b), (dtb, dt_proj_b), (Dp, D)):
                    sp.dma_start(t[:, :], s.rearrange("(e p) -> p e", p=P)).then_inc(small_in, 16)
            sp.dma_start(Acol[:, :, :], A_log.rearrange("(e p) n -> p e n", p=P)).then_inc(small_in, 16)
            sp.dma_start(gate[:, :, :], gate_w.rearrange("(e p) n -> p e n", p=P)).then_inc(small_in, 16)

            def load_ctx(b):
                if not known(b, 0):
                    hold(sp, tap_done, (b - 1) * EB + 1)
                sp.dma_start(ctx_rows[:, :, :], ctx_in[bass.ds(b, 1), :, :].rearrange("b (t p) d -> p (b t) d", p=P)).then_inc(ctx_loaded, 16)

            def store_bc(b, uses, turn):
                k = uses["XP"]
                hold(sp, freed[k % 2], before(k, turn) + 1)
                sp.dma_start(bcs[bass.ds(b, 1), :, :].rearrange("a n l -> (a n) l"), xdbl[DR:, :]).then_inc(bcs_out, 16)

            def load_bc(b, h):
                hold(sp, bcs_out, (b + 1) * 16, 16)
                for c in range(UPH // 2):
                    slot = c % 4
                    if not (known(b, 0) and h == 0 and c < 4):
                        hold(sp, dbu_done, q0(b, h) + 2 * (c - 4) + 2)
                        hold(sp, hc_done, q0(b, h) + 2 * (c - 4) + 2)
                    for kind in range(2):
                        lo = kind * DS + 2 * c
                        src = bcs[bass.ds(b, 1), lo:lo + 2, :].rearrange("a n l -> a (n l)")
                        sp.dma_start(bc[:, slot, kind, :, :].rearrange("p n l -> p (n l)"),
                                     src.to_broadcast([P, 2 * L])).then_inc(bc_in[slot], 16)

            def store_xln(b):
                hold(sp, xln_done, b * LB + LB)
                sp.dma_start(xln_dram[bass.ds(b * L, L), :].rearrange("(t p) d -> p t d", p=P), xlnb[:, :, :]).then_inc(xln_out, 16)
                sp.dma_start(out[bass.ds(b, 1), :, :].rearrange("b (t p) d -> p (b t) d", p=P),
                             xall[:, bass.ds(b * LB, LB), :]).then_inc(x1_out, 16)

            load_ctx(0)
            sp.sem_inc(xln_out, 16)
            sp.dma_start(xall[:, :, :], x.rearrange("b (t p) d -> p (b t) d", p=P)).then_inc(x_in, 16)
            store_bc(0, FIRST, 0)
            load_ctx(1)
            load_bc(0, 0)
            load_bc(0, 1)
            store_bc(1, TURN0, 0)
            with sp.Fori(1, NB - 1) as b:
                load_ctx(b + 1)
                load_bc(b, 0)
                load_bc(b, 1)
                store_xln(b - 1)
                store_bc(b + 1, LOOP, b - 1)
            load_bc(NB - 1, 0)
            load_bc(NB - 1, 1)
            store_xln(NB - 2)
            store_xln(NB - 1)
            sp.wait_ge(xln_out, 16 * NB + 16)
            sp.wait_ge(x1_out, 16 * NB)

        @block.gpsimd
        def _(pool):
            g_ = nc.gpsimd
            g_.memset(ident[:, :], 0.0).then_inc(pool_step, 1)
            g_.memset(epsc[:, :], EPS).then_inc(ident_ok, 1)
            hold(pool, pool_step, 1)
            g_.affine_select(out=ident[:, :], in_=ident[:, :], compare_op=ALU.not_equal, fill=1.0, base=0,
                             pattern=[[-1, P]], channel_multiplier=1).then_inc(ident_ok, 1)

            def rstd(rs, mv, nm, n, steps, done):
                g_.tensor_tensor(rs[:, 2, :], rs[:, 0, :], rs[:, 1, :], ALU.mult).then_inc(pool_step, 1)
                hold(pool, pool_step, steps + 1)
                g_.tensor_tensor(rs[:, 2, :], rs[:, 2, :], rs[:, 1, :], ALU.mult).then_inc(pool_step, 1)
                hold(pool, pool_step, steps + 2)
                g_.tensor_scalar(rs[:, 2, :], rs[:, 2, :], -0.5, 1.5, ALU.mult, ALU.add).then_inc(pool_step, 1)
                hold(pool, pool_step, steps + 3)
                g_.tensor_tensor(rs[:, 3, :], rs[:, 2, :], rs[:, 1, :], ALU.mult).then_inc(pool_step, 1)
                hold(pool, pool_step, steps + 4)
                g_.tensor_tensor(nm[:, :], mv[:, :, 0], rs[:, 3, :], ALU.mult).then_inc(pool_step, 1)
                hold(pool, pool_step, steps + 5)
                g_.tensor_scalar(nm[:, :], nm[:, :], -1.0, None, ALU.mult).then_inc(done, 1)

            def unit(b, h, n):
                c = n // 2
                if n % 2 == 0:
                    hold(pool, bc_in[c % 4], 32 * (b * 4 + 2 * h + c // 4 + 1))
                if n == 0:
                    hold(pool, du_ready, b * 2 + h + 1)
                if not fresh(b, h, n):
                    hold(pool, acc_done, q0(b, h) + n - RING + 1)
                B = bc[:, c % 4, 0, n % 2:n % 2 + 1, :].to_broadcast([P, 2, L])
                g_.tensor_tensor(ring[:, n % RING, :].rearrange("p (e l) -> p e l", e=2),
                                 cols(du, b, h * 2 * L, 2 * L).rearrange("p (e l) -> p e l", e=2), B,
                                 ALU.mult).then_inc(dbu_done, 1)

            def rstd1():
                hold(pool, rstd1_guess, 1)
                rstd(rs1, mv1, nm1, NT, 1, rstd1_ok)

            def rstd2(b):
                hold(pool, guess2, b + 1)
                rstd(rs2, mv2, nm2, LB, 6 + 5 * b, rstd2_ok)

            def half(b, h, tasks):
                for n in range(UPH):
                    unit(b, h, n)
                    for f in tasks.get(n, []):
                        f()

            def turn(b, nxt=True, rest=True):
                sub, add, times_u = soft(pool, b, 1)
                tasks = {8: [sub], 10: [add], 13: [times_u]}
                if known(b, 0):
                    tasks[4] = [rstd1]
                if rest:
                    tasks[11] = [lambda: rstd2(b - 1)]
                half(b, 0, tasks)
                tasks = {}
                if nxt:
                    sub, add, times_u = soft(pool, b + 1, 0)
                    tasks = {12: [sub], 14: [add], 15: [times_u]}
                half(b, 1, tasks)

            turn(0, rest=False)
            with pool.Fori(1, NB - 1) as b:
                turn(b)
            turn(NB - 1, nxt=False)
            rstd2(NB - 1)

        @block.scalar
        def _(act):
            a_ = nc.scalar

            def copy_use(dst, k, turn, width=L, parts=P):
                hold(act, filled[k % 2], before(k, turn) + 1)
                a_.activation(dst, bank(k)[0:parts, 0:width], ACT.Copy).then_inc(freed[k % 2], 1)

            def unit(b, h, n):
                if n == 0:
                    hold(act, delta_ready, b * 2 + h + 1)
                if start(b, h, n):
                    hold(act, zeros_ok, 1)
                else:
                    hold(act, scan_done, q0(b, h) + n - 1)
                for e in range(2):
                    eb = 2 * h + e
                    last = a_.activation(dA[n % 2][:, e, 1:L], cols(delta, b, eb * L + 1, L - 1), ACT.Exp,
                                         scale=Acol[:, eb, n:n + 1])
                last.then_inc(exp_done, 1)

            def ctx_T(uses, turn, i):
                copy_use(ctxT[:, i, :], uses["T%d" % i], turn)

            def tap(b, uses, turn, eb):
                k = uses["X%d" % eb]
                hold(act, filled[k % 2], before(k, turn) + 1)
                a_.activation(cols(u, b, eb * L, L), bank(k)[:, :], ACT.Identity, scale=convw[:, eb, DC - 1:DC],
                              bias=convb[:, eb:eb + 1]).then_inc(tap_done, 1)

            def silu_u(b, uses, turn):
                for name in XB:
                    k = uses[name]
                    hold(act, freed[k % 2], before(k, turn) + 1)
                a_.activation(cols(u, b, 0, EB * L), cols(u, b, 0, EB * L), ACT.Silu).then_inc(u_ready, 1)

            def silu_z(b):
                if not known(b, 0):
                    hold(act, y_gated, b * 2)
                hold(act, rstd1_ok, 1)
                for eb in range(EB):
                    last = a_.activation(zs[:, eb * L:(eb + 1) * L], row(xall, b, eb), ACT.Silu,
                                         scale=rs1[:, 3, bass.ds(b * LB + eb, 1)], bias=nm1[:, bass.ds(b * LB + eb, 1)])
                last.then_inc(zs_ready, 1)

            def xdbl_copy(b, uses, turn):
                if not known(b, 0):
                    hold(act, bcs_out, b * 16)
                copy_use(xdbl[:, :], uses["XP"], turn, parts=DR + 2 * DS)

            def dt_eb(b, uses, turn, eb):
                k = uses["DT%d" % eb]
                hold(act, filled[k % 2], before(k, turn) + 1)
                a_.activation(spy[:, eb % 2 * L:(eb % 2 + 1) * L], bank(k)[:, :], ACT.Abs, bias=dtb[:, eb:eb + 1]).then_inc(abs_done, 1)
                a_.activation(cols(delta, b, eb * L, L), bank(k)[:, :], ACT.Relu, bias=dtb[:, eb:eb + 1]).then_inc(freed[k % 2], 1)

            def soft(b, i):
                s = slice(i * 2 * L, (i + 1) * 2 * L)
                hold(act, abs_done, b * EB + 2 * i + 2)
                a_.activation(spy[:, :], spy[:, :], ACT.Exp, scale=-1.0).then_inc(sp_step, 1)
                hold(act, sp_step, b * 2 + i + 1)
                a_.activation(spw[:, s], spy[:, :], ACT.Copy, bias=1.0).then_inc(soft_w, 1)

            def soft_log(b, i):
                s = slice(i * 2 * L, (i + 1) * 2 * L)
                hold(act, soft_loss, b * 2 + i + 1)
                a_.activation(spw[:, s], spw[:, s], ACT.Ln).then_inc(soft_ln, 1)

            def guess(rs, mv, done, base):
                a_.activation(rs[:, 0, :], mv[:, :, 1], ACT.Identity, bias=epsc[:, 0:1]).then_inc(act_step, 1)
                hold(act, act_step, base + 1)
                a_.activation(rs[:, 1, :], rs[:, 0, :], ACT.Ln).then_inc(act_step, 1)
                hold(act, act_step, base + 2)
                a_.activation(rs[:, 1, :], rs[:, 1, :], ACT.Exp, scale=-0.5).then_inc(done, 1)

            def guess_1():
                hold(act, stats1, 1)
                guess(rs1, mv1, rstd1_guess, 1)

            def guess_2(b):
                hold(act, stats2, b + 1)
                guess(rs2, mv2, guess2, 3 + 2 * b)

            def xln(b):
                hold(act, rstd2_ok, b + 1)
                hold(act, xln_out, b * 16 + 16)
                for i in range(LB):
                    a_.activation(xlnb[:, i, :], row(xall, b, i), ACT.Identity, scale=rs2[:, 3, i:i + 1], bias=nm2[:, i:i + 1]).then_inc(xln_done, 1)

            def gate_T(uses, turn, i):
                copy_use(gT[:, i, :], uses["G%d" % i], turn)

            def half(b, h, tasks):
                for n in range(UPH):
                    unit(b, h, n)
                    for f in tasks.get(n, []):
                        f()

            def turn(b, uses, k, nxt=True, rest=True):
                tasks = {n: [] for n in range(2 * UPH)}
                if nxt:
                    tasks[3] += [lambda: ctx_T(uses, k, 0), lambda: ctx_T(uses, k, 1)]
                    tasks[8] += [lambda: tap(b + 1, uses, k, 0), lambda: tap(b + 1, uses, k, 1)]
                    tasks[13] += [lambda: tap(b + 1, uses, k, 2), lambda: tap(b + 1, uses, k, 3)]
                    tasks[15] += [lambda: silu_u(b + 1, uses, k)]
                if known(b, 0):
                    tasks[3] += [guess_1]
                tasks[2] += [lambda: soft(b, 1)]
                tasks[5] += [lambda: soft_log(b, 1)]
                tasks[6] += [lambda: silu_z(b)]
                if rest:
                    tasks[7] += [lambda: guess_2(b - 1)]
                    tasks[10] += [lambda: xln(b - 1)]
                    tasks[18 if nxt else 13] += [lambda: gate_T(uses, k, 0), lambda: gate_T(uses, k, 1)]
                if nxt:
                    tasks[21] += [lambda: xdbl_copy(b + 1, uses, k)]
                    tasks[24] += [lambda: dt_eb(b + 1, uses, k, 0), lambda: dt_eb(b + 1, uses, k, 1), lambda: soft(b + 1, 0)]
                    tasks[27] += [lambda: soft_log(b + 1, 0)]
                    tasks[28] += [lambda: dt_eb(b + 1, uses, k, 2), lambda: dt_eb(b + 1, uses, k, 3)]
                if rest:
                    tasks[30 if nxt else 16] += [lambda: gate_T(uses, k, 2), lambda: gate_T(uses, k, 3)]
                for h in range(2):
                    half(b, h, {n: tasks[h * UPH + n] for n in range(UPH)})

            hold(act, small_in, 16 * 9)
            hold(act, ident_ok, 2)
            a_.activation(Acol[:, :, :], Acol[:, :, :], ACT.Exp).then_inc(act_step, 1)
            copy_use(wT[:, 0, :], CONST["W0"], 0)
            copy_use(wT[:, 1, :], CONST["W1"], 0)
            copy_use(xpT[:, :, :].rearrange("p e k -> p (e k)"), CONST["XPT"], 0, width=EB * (DR + 2 * DS))
            copy_use(dtT[:, :], CONST["DTT"], 0, parts=DR)
            hold(act, act_step, 1)
            a_.activation(Acol[:, :, :], Acol[:, :, :], ACT.Copy, scale=-1.0).then_inc(consts_ok, 1)
            for eb in range(EB):
                last = a_.activation(diagD[:, eb, :], ident[:, :], ACT.Identity, scale=Dp[:, eb:eb + 1])
            last.then_inc(diag_ok, 1)

            for i in range(2):
                ctx_T(FIRST, 0, i)
            for eb in range(EB):
                tap(0, FIRST, 0, eb)
            silu_u(0, FIRST, 0)
            xdbl_copy(0, FIRST, 0)
            for i in range(2):
                for eb in range(2 * i, 2 * i + 2):
                    dt_eb(0, FIRST, 0, eb)
                if i == 0:
                    soft(0, 0)
                    soft_log(0, 0)
            hold(act, consts_ok, 1)
            turn(0, TURN0, 0, rest=False)
            with act.Fori(1, NB - 1) as b:
                turn(b, LOOP, b - 1)
            turn(NB - 1, LAST, 0, nxt=False)
            guess_2(NB - 1)
            xln(NB - 1)
            for i in range(LB):
                gate_T(TAIL, 0, i)

        @block.vector
        def _(dve):
            v_ = nc.vector
            for i in range(2):
                last = v_.memset(dA[i][:, :, 0:1], 0.0)
            last.then_inc(zeros_ok, 1)

            def scan(b, h, n):
                dve.wait_ge(exp_done, q0(b, h) + n + 1)
                dve.wait_ge(dbu_done, q0(b, h) + n + 1)
                v_.tensor_tensor_scan(ring[:, n % RING, :], dA[n % 2][:, :, :].rearrange("p e l -> p (e l)"), ring[:, n % RING, :],
                                      0.0, ALU.mult, ALU.add).then_inc(scan_done, 1)

            def times_c(b, h, n):
                c = n // 2
                dve.wait_ge(scan_done, q0(b, h) + n + 1)
                if n % 2 == 0:
                    dve.wait_ge(bc_in[c % 4], 32 * (b * 4 + 2 * h + c // 4 + 1))
                C = bc[:, c % 4, 1, n % 2:n % 2 + 1, :].to_broadcast([P, 2, L])
                states = ring[:, n % RING, :].rearrange("p (e l) -> p e l", e=2)
                v_.tensor_tensor(states, states, C, ALU.mult).then_inc(hc_done, 1)

            def conv(b, uses, turn, ebs):
                for j in range(1, DC):
                    for eb in ebs:
                        k = uses["X%d" % eb]
                        if j == 1:
                            dve.wait_ge(tap_done, b * EB + eb + 1)
                        else:
                            dve.wait_ge(conv_step[eb % 2], (b * EB // 2 + eb // 2) * (DC - 2) + j - 1)
                        o = cols(u, b, eb * L + j, L - j)
                        last = v_.scalar_tensor_tensor(o, bank(k)[:, 0:L - j], convw[:, eb, DC - 1 - j:DC - j], o, ALU.mult, ALU.add)
                        last.then_inc(conv_step[eb % 2] if j < DC - 1 else freed[k % 2], 1)

            def loss(b, i):
                s = slice(i * 2 * L, (i + 1) * 2 * L)
                hold(dve, soft_w, b * 2 + i + 1)
                v_.scalar_tensor_tensor(cols(du, b, i * 2 * L, 2 * L), spw[:, s], -1.0, spy[:, :], ALU.add, ALU.subtract).then_inc(soft_loss, 1)

            def drain_y(b, h):
                dve.wait_ge(acc_done, q0(b, h) + UPH)
                dve.wait_ge(zs_ready, b + 1)
                v_.tensor_tensor(g[:, :], yacc[:, :, :].rearrange("p e l -> p (e l)"), zs[:, h * 2 * L:(h + 1) * 2 * L], ALU.mult).then_inc(y_gated, 1)

            def add_y(b, h, uses, turn):
                for e in range(2):
                    k = uses["FE"[h] + str(e)]
                    eb = 2 * h + e
                    dve.wait_ge(filled[k % 2], before(k, turn) + 1)
                    xs = xall[:, bass.ds(b * LB, LB), eb * P:(eb + 1) * P]
                    v_.tensor_tensor(xs, bank(k)[:, :].rearrange("p (t e) -> p t e", t=LB), xs, ALU.add).then_inc(freed[k % 2], 1)

            def logit_copy(b, uses, turn):
                k = uses["LG"]
                dve.wait_ge(filled[k % 2], before(k, turn) + 1)
                v_.tensor_copy(logits[:, bass.ds(b * LB, LB), :].rearrange("p t e -> p (t e)"), bank(k)[:, 0:LB * 8]).then_inc(freed[k % 2], 1)

            def stats_2(b, uses, turn):
                for name in E:
                    k = uses[name]
                    hold(dve, freed[k % 2], before(k, turn) + 1)
                for t in range(LB):
                    last = v_.bn_stats(st2[:, t, :], row(xall, b, t))
                last.then_inc(dve_step, 1)
                hold(dve, dve_step, b + 2)
                for t in range(LB):
                    last = v_.bn_aggr(mv2[:, t, :], st2[:, t, :])
                last.then_inc(stats2, 1)

            def half(b, h, tasks):
                for n in range(UPH):
                    scan(b, h, n)
                    if n > 0:
                        times_c(b, h, n - 1)
                    for f in tasks.get(n, []):
                        f()
                times_c(b, h, UPH - 1)

            def turn(b, uses, k, nxt=True, rest=True):
                tasks = {n: [] for n in range(2 * UPH)}
                if rest:
                    tasks[1] += [lambda: drain_y(b - 1, 1)]
                    tasks[4] += [lambda: add_y(b - 1, 1, uses, k)]
                    tasks[5] += [lambda: stats_2(b - 1, uses, k)]
                if nxt:
                    tasks[8] += [lambda: conv(b + 1, uses, k, (0, 1))]
                    tasks[13] += [lambda: conv(b + 1, uses, k, (2, 3))]
                    tasks[26] += [lambda: loss(b + 1, 0)]
                tasks[3] += [lambda: loss(b, 1)]
                tasks[17] += [lambda: drain_y(b, 0)]
                if not nxt:
                    tasks[20] += [lambda: logit_copy(b - 1, uses, k)]
                tasks[21] += [lambda: add_y(b, 0, uses, k)]
                for h in range(2):
                    half(b, h, {n: tasks[h * UPH + n] for n in range(UPH)})
                if rest and nxt:
                    logit_copy(b - 1, uses, k)

            conv(0, FIRST, 0, (0, 1))
            conv(0, FIRST, 0, (2, 3))
            dve.wait_ge(x_in, 16)
            for t in range(NT):
                last = v_.bn_stats(st1[:, t, :], xall[:, t, :])
            last.then_inc(dve_step, 1)
            dve.wait_ge(dve_step, 1)
            for t in range(NT):
                last = v_.bn_aggr(mv1[:, t, :], st1[:, t, :])
            last.then_inc(stats1, 1)
            loss(0, 0)
            for f in soft(dve, 0, 0):
                f()
            turn(0, TURN0, 0, rest=False)
            with dve.Fori(1, NB - 1) as b:
                turn(b, LOOP, b - 1)
            turn(NB - 1, LAST, 0, nxt=False)
            drain_y(NB - 1, 1)
            add_y(NB - 1, 1, TAIL, 0)
            stats_2(NB - 1, TAIL, 0)
            logit_copy(NB - 1, TAIL, 0)

        @block.tensor
        def _(pe):
            t_ = nc.tensor

            def use(k, turn):
                if k > 1:
                    pe.wait_ge(freed[k % 2], before(k, turn))

            def acc(b, h, n):
                if n == 0:
                    if known(b, 0) and h == 0:
                        pe.wait_ge(diag_ok, 1)
                    else:
                        pe.wait_ge(y_gated, b * 2 + h)
                    pe.wait_ge(u_ready, b + 1)
                    for e in range(2):
                        t_.matmul(yacc[:, e, :], diagD[:, 2 * h + e, :], cols(u, b, (2 * h + e) * L, L), start=True, stop=False)
                pe.wait_ge(hc_done, q0(b, h) + n + 1)
                for e in range(2):
                    last = t_.matmul(yacc[:, e, :], ident[:, :], ring[:, n % RING, e * L:(e + 1) * L], start=False, stop=(n == UPH - 1))
                last.then_inc(acc_done, 1)

            def ctx_T(b, uses, turn):
                pe.wait_ge(ctx_loaded, (b + 1) * 16)
                for i in range(KB):
                    k = uses["T%d" % i]
                    use(k, turn)
                    for t in range(LB):
                        last = t_.transpose(bank(k)[:, t * P:(t + 1) * P], ctx_rows[:, t, i * P:(i + 1) * P], ident[:, :])
                    last.then_inc(filled[k % 2], 1)

            def in_proj(uses, turn, eb):
                if eb == 0:
                    for i in range(KB):
                        k = uses["T%d" % i]
                        pe.wait_ge(freed[k % 2], before(k, turn) + 1)
                k = uses["X%d" % eb]
                use(k, turn)
                for i in range(KB):
                    last = t_.matmul(bank(k)[:, :], wT[:, i, eb * P:(eb + 1) * P], ctxT[:, i, :], start=(i == 0), stop=(i == KB - 1))
                last.then_inc(filled[k % 2], 1)

            def x_proj(b, uses, turn):
                k = uses["XP"]
                use(k, turn)
                hold(pe, u_ready, b + 1)
                for eb in range(EB):
                    last = t_.matmul(bank(k)[0:DR + 2 * DS, :], xpT[:, eb, :], cols(u, b, eb * L, L), start=(eb == 0), stop=(eb == EB - 1))
                last.then_inc(filled[k % 2], 1)

            def dt_proj(uses, turn, eb):
                if eb == 0:
                    k = uses["XP"]
                    pe.wait_ge(freed[k % 2], before(k, turn) + 1)
                k = uses["DT%d" % eb]
                use(k, turn)
                t_.matmul(bank(k)[:, :], dtT[:, eb * P:(eb + 1) * P], xdbl[0:DR, :], start=True, stop=True).then_inc(filled[k % 2], 1)

            def y_T(b, h, uses, turn):
                pe.wait_ge(y_gated, b * 2 + h + 1)
                for e in range(2):
                    k = uses["FE"[h] + str(e)]
                    use(k, turn)
                    for t in range(LB):
                        last = t_.transpose(bank(k)[:, t * P:(t + 1) * P], g[:, e * L + t * P:e * L + (t + 1) * P], ident[:, :])
                    last.then_inc(filled[k % 2], 1)

            def gate_T(b, uses, turn, i):
                pe.wait_ge(xln_done, b * LB + i + 1)
                k = uses["G%d" % i]
                use(k, turn)
                for d in range(DI // P):
                    last = t_.transpose(bank(k)[:, d * P:(d + 1) * P], xlnb[:, i, d * P:(d + 1) * P], ident[:, :])
                last.then_inc(filled[k % 2], 1)

            def logits_of(uses, turn):
                for i in (LB - 2, LB - 1):
                    k = uses["G%d" % i]
                    pe.wait_ge(freed[k % 2], before(k, turn) + 1)
                k = uses["LG"]
                use(k, turn)
                for i in range(LB):
                    for d in range(DI // P):
                        last = t_.matmul(bank(k)[:, i * 8:(i + 1) * 8], gT[:, i, d * P:(d + 1) * P], gate[:, d, :], start=(d == 0), stop=(d == DI // P - 1))
                last.then_inc(filled[k % 2], 1)

            def half(b, h, tasks):
                for n in range(UPH):
                    if n > 0:
                        acc(b, h, n - 1)
                    for f in tasks.get(n, []):
                        f()
                acc(b, h, UPH - 1)

            def turn(b, uses, k, nxt=True, rest=True):
                tasks = {n: [] for n in range(2 * UPH)}
                if nxt:
                    tasks[0] += [lambda: ctx_T(b + 1, uses, k)]
                if rest:
                    tasks[1] += [lambda: y_T(b - 1, 1, uses, k)]
                if nxt:
                    tasks[4] += [lambda: in_proj(uses, k, 0), lambda: in_proj(uses, k, 1)]
                    tasks[9] += [lambda: in_proj(uses, k, 2), lambda: in_proj(uses, k, 3)]
                if rest:
                    tasks[14 if nxt else 9] += [lambda: gate_T(b - 1, uses, k, 0), lambda: gate_T(b - 1, uses, k, 1)]
                if nxt:
                    tasks[16] += [lambda: x_proj(b + 1, uses, k)]
                tasks[18] += [lambda: y_T(b, 0, uses, k)]
                if nxt:
                    tasks[20] += [lambda: dt_proj(uses, k, 0), lambda: dt_proj(uses, k, 1)]
                    tasks[24] += [lambda: dt_proj(uses, k, 2), lambda: dt_proj(uses, k, 3)]
                if rest:
                    tasks[27 if nxt else 12] += [lambda: gate_T(b - 1, uses, k, 2), lambda: gate_T(b - 1, uses, k, 3)]
                    tasks[29 if nxt else 15] += [lambda: logits_of(uses, k)]
                for h in range(2):
                    half(b, h, {n: tasks[h * UPH + n] for n in range(UPH)})

            pe.wait_ge(ident_ok, 2)
            pe.wait_ge(small_in, 16 * 9)
            for i in range(KB):
                k = CONST["W%d" % i]
                for eb in range(EB):
                    last = t_.transpose(bank(k)[:, eb * P:(eb + 1) * P], w_rows[:, eb, i * P:(i + 1) * P], ident[:, :])
                last.then_inc(filled[k % 2], 1)
            k, w = CONST["XPT"], DR + 2 * DS
            use(k, 0)
            for eb in range(EB):
                last = t_.transpose(bank(k)[:, eb * w:(eb + 1) * w], xp_rows[:, eb * P:(eb + 1) * P], ident[0:w, 0:w])
            last.then_inc(filled[k % 2], 1)
            k = CONST["DTT"]
            use(k, 0)
            for eb in range(EB):
                last = t_.transpose(bank(k)[0:DR, eb * P:(eb + 1) * P], dt_rows[:, eb, :], ident[:, :])
            last.then_inc(filled[k % 2], 1)

            ctx_T(0, FIRST, 0)
            for eb in range(EB):
                in_proj(FIRST, 0, eb)
            x_proj(0, FIRST, 0)
            for eb in range(EB):
                dt_proj(FIRST, 0, eb)
            turn(0, TURN0, 0, rest=False)
            with pe.Fori(1, NB - 1) as b:
                turn(b, LOOP, b - 1)
            turn(NB - 1, LAST, 0, nxt=False)
            y_T(NB - 1, 1, TAIL, 0)
            for i in range(LB):
                gate_T(NB - 1, TAIL, 0, i)
            logits_of(TAIL, 0)


NE, FF, TOPK = 8, 1024, 2
TOK = NB * L
KD = DI // P
KF = FF // P
SLOT_TILES = TOK * TOPK // P + NE - 1
ST = SLOT_TILES + 3
f32r, i32, u32 = mybir.dt.float32r, mybir.dt.int32, mybir.dt.uint32
AX = mybir.AxisListType


def ffn_block(nc, logits, xln_dram, w0, w1, wo, out):
    ctx = ExitStack()
    with ctx:
        def sb(name, shape, dt=fp32):
            return ctx.enter_context(nc.sbuf_tensor(name, shape, dt))

        def sem(name):
            return ctx.enter_context(nc.semaphore(name))

        NC = 6
        stage = [sb(f"stage{c}", [P, 4, 512]) for c in range(NC)]
        w_hi = [sb(f"w_hi{c}", [P, 4, 512], f32r) for c in range(NC)]
        w_lo = [sb(f"w_lo{c}", [P, 4, 512], f32r) for c in range(NC)]

        identf = sb("identf", [P, P])
        io8 = sb("io8", [P, NE])
        io_st = sb("io_st", [P, ST])
        io_cap = sb("io_cap", [P, NT])
        tokid = sb("tokid", [P, NT])
        first = sb("first", [P, NT])
        top = sb("top", [P, TOPK, NT])
        wgt = sb("wgt", [P, TOPK, NT])
        gap = sb("gap", [P, NT])
        expd = sb("expd", [P, NT])
        ntile = sb("ntile", [P, NE])
        tend = sb("tend", [P, NE])
        slotf = sb("slotf", [P, TOPK, NT])
        sloti = sb("sloti", [P, TOPK, NT], i32)
        quo_i = sb("quo_i", [P, TOPK * NT], i32)
        rem_i = sb("rem_i", [P, TOPK * NT], i32)
        texp_i = sb("texp_i", [P, ST], i32)
        nxt_i = sb("nxt_i", [P, ST], i32)
        flag_i = sb("flag_i", [P, ST], i32)
        tiles_i = sb("tiles_i", [P, 1], i32)
        odd_i = sb("odd_i", [P, 1], i32)
        tok_tab = sb("tok_tab", [P, ST], u32)
        index = [sb(f"index{i}", [P, 1], u32) for i in range(2)]
        acc_index = sb("acc_index", [P, 1], u32)
        out_index = sb("out_index", [P, 1], u32)
        out_tab = sb("out_tab", [P, ST], u32)
        wtab = sb("wtab", [P, ST])
        wgt_hi = sb("wgt_hi", [P, TOPK, NT], f32r)
        wgt_lo = sb("wgt_lo", [P, TOPK, NT])

        work = sb("work", [P, 8, 512])
        xg = [work[:, i, :] for i in range(2)]
        gated, inter = work[:, 2:4, :], work[:, 4:6, :]
        acc = [work[:, 6 + i, :] for i in range(2)]
        R = [sb(f"R{k}", [P, NT, P], f32r) for k in range(TOPK)]
        S_tok = sb("S_tok", [P, TOPK * NT, ST], f32r)
        S_w = sb("S_w", [P, TOPK * NT, 2 * ST], f32r)
        S_hi, S_lo = S_w[:, :, 0:ST], S_w[:, :, ST:2 * ST]
        flat = work[:, :, :].rearrange("p a n -> p (a n)")
        carved = [0]

        def carve(*shape):
            n = 1
            for d in shape:
                n *= d
            part = flat[:, carved[0]:carved[0] + n]
            carved[0] += n
            names = "abc"[:len(shape)]
            return part.rearrange("p (" + " ".join(names) + ") -> p " + " ".join(names), **dict(zip(names, shape)))

        ltri = carve(P)
        ones = carve(P)
        io128 = carve(P)
        segment, total, incl, over, base = (carve(NE, NT) for _ in range(5))
        cand, rest, ohs, pos = (carve(NT, NE) for _ in range(4))
        oh = carve(TOPK * NT, NE).rearrange("p (k t) e -> p k t e", k=TOPK)
        table8 = carve(ST, NE)
        quo, rem = carve(TOPK * NT), carve(TOPK * NT)
        tend_of, nxt, texp, flag = (carve(ST) for _ in range(4))
        tok1, none = carve(ST), carve(ST)
        xT_hi, xT_lo = (sb(n, [P, KD, P], f32r) for n in ("xT_hi", "xT_lo"))
        iT_hi, iT_lo = (sb(n, [P, KF, P], f32r) for n in ("iT_hi", "iT_lo"))

        hp = [ctx.enter_context(nc.psum_tensor(f"hp{i}", [P, 512], fp32)) for i in range(4)]
        xp = ctx.enter_context(nc.psum_tensor("xp", [P, 512], fp32))
        yp = ctx.enter_context(nc.psum_tensor("yp", [P, 512], fp32))
        tp = [ctx.enter_context(nc.psum_tensor(f"tp{i}", [P, 512], fp32)) for i in range(2)]

        consts, routed, gap_exp, counted, tabled = (sem(n) for n in ("consts", "routed", "gap_exp", "counted", "tabled"))
        gap_ok, ohs_ok, RS_ok, tables_ok = (sem(n) for n in ("gap_ok", "ohs_ok", "RS_ok", "tables_ok"))
        stage_in = [sem(f"stage_in{c}") for c in range(NC)]
        hi_done, lo_done = sem("hi_done"), sem("lo_done")
        h_done, xT_done, y_done, iT_done = (sem(n) for n in ("h_done", "xT_done", "y_done", "iT_done"))
        silu_done, x_hi, x_lo, i_hi, i_lo, inter_done, summed = (sem(n) for n in
            ("silu_done", "x_hi", "x_lo", "i_hi", "i_lo", "inter_done", "summed"))
        index_ok, acc_index_ok, out_index_ok = sem("index_ok"), sem("acc_index_ok"), sem("out_index_ok")
        xg_in = [sem(f"xg_in{i}") for i in range(2)]
        acc_in, scattered = sem("acc_in"), sem("scattered")

        block = ctx.enter_context(nc.Block())
        LAST = SLOT_TILES - 1
        TURNS = LAST // 2
        assert LAST == 2 * TURNS
        MIN_TILES = TOK * TOPK // P

        def hold(eng, sem, value, least=1):
            if not isinstance(value, int):
                value = eng.to_reg(value)
                eng.wait_ge(sem, least)
            eng.wait_ge(sem, value)

        def weights_of(c, e):
            if c < 4:
                src = (w0, w1)[c // 2]
                return src[bass.ds(e, 1), :, (c % 2) * 512:(c % 2 + 1) * 512].rearrange("e (k p) f -> p (e k) f", p=P)
            return wo[bass.ds(e, 1), (c - 4) * 512:(c - 3) * 512, :].rearrange("e (k p) d -> p (e k) d", p=P)

        def splits(s, c):
            return 4 + NC * s + c + 1

        def loads_of(c, s):
            return 2 + s + (1 if c < 4 else 0)

        out_rows = out.rearrange("b l d -> (b l) d")

        @block.sync
        def _(sp):
            for c in range(NC):
                sp.dma_start(stage[c][:, :, :], weights_of(c, 0)).then_inc(stage_in[c], 16)
            sp.wait_ge(tables_ok, 1)
            e0 = sp.value_load(texp_i[0:1, 0:1], min_val=0, max_val=NE - 1)
            for c in range(NC):
                sp.wait_ge(stage_in[c], 16)
                sp.dma_start(stage[c][:, :, :], weights_of(c, e0), cond=e0 > 0).then_inc(stage_in[c], 16)
            n0 = sp.value_load(nxt_i[0:1, 0:1], min_val=0, max_val=NE - 1)
            for c in range(4):
                sp.wait_ge(hi_done, c + 1)
                sp.wait_ge(lo_done, c + 1)
                sp.dma_start(stage[c][:, :, :], weights_of(c, n0)).then_inc(stage_in[c], 16)

            def reload(s, c, f, e):
                sp.wait_ge(hi_done, splits(s, c))
                sp.wait_ge(lo_done, splits(s, c))
                sp.dma_start(stage[c][:, :, :], weights_of(c, e), cond=f > 0).then_inc(stage_in[c], 16)

            def step(s):
                f = sp.value_load(flag_i[0:1, bass.ds(s + 1, 1)], min_val=0, max_val=1)
                e = sp.value_load(nxt_i[0:1, bass.ds(s + 1, 1)], min_val=0, max_val=NE - 1)
                for c in range(4):
                    reload(s, c, f, e)
                f = sp.value_load(flag_i[0:1, bass.ds(s, 1)], min_val=0, max_val=1)
                e = sp.value_load(nxt_i[0:1, bass.ds(s, 1)], min_val=0, max_val=NE - 1)
                for c in range(4, NC):
                    reload(s, c, f, e)

            step(0)
            tiles = sp.value_load(tiles_i[0:1, 0:1], min_val=MIN_TILES, max_val=SLOT_TILES)
            with sp.Fori(0, TURNS) as t:
                for j in range(1, 3):
                    with sp.If(tiles > 2 * t + j):
                        step(2 * t + j)
            for c in range(NC):
                hold(sp, stage_in[c], 16 * loads_of(c, tiles), 16)

        @block.gpsimd
        def _(pool):
            g_ = nc.gpsimd
            g_.iota(io8[:, :], [[1, NE]], base=0, channel_multiplier=0, allow_small_or_imprecise_dtypes=True).then_inc(consts, 1)
            g_.memset(identf[:, :], 0.0).then_inc(consts, 1)
            g_.memset(ltri[:, :], 1.0).then_inc(consts, 1)
            g_.memset(ones[:, :], 1.0).then_inc(consts, 1)
            g_.memset(segment[:, :, :], 1.0).then_inc(consts, 1)
            g_.iota(io128[:, :], [[1, P]], base=0, channel_multiplier=0, allow_small_or_imprecise_dtypes=True).then_inc(consts, 1)
            g_.iota(io_st[:, :], [[1, ST]], base=0, channel_multiplier=0, allow_small_or_imprecise_dtypes=True).then_inc(consts, 1)
            g_.iota(io_cap[:, :], [[P, NT]], base=0, channel_multiplier=0, allow_small_or_imprecise_dtypes=True).then_inc(consts, 1)
            g_.iota(tokid[:, :], [[P, NT]], base=1, channel_multiplier=1, allow_small_or_imprecise_dtypes=True).then_inc(consts, 1)
            pool.wait_ge(consts, 9)
            g_.memset(segment[:, :, 0:1], 0.0).then_inc(consts, 1)
            g_.affine_select(out=identf[:, :], in_=identf[:, :], compare_op=ALU.not_equal, fill=1.0, base=0,
                             pattern=[[-1, P]], channel_multiplier=1).then_inc(consts, 1)
            g_.affine_select(out=ltri[:, :], in_=ltri[:, :], compare_op=ALU.is_gt, fill=0.0, base=0,
                             pattern=[[1, P]], channel_multiplier=-1).then_inc(consts, 1)

            def gather(half, parity):
                s = 2 * half + parity
                start = isinstance(s, int) and s < 2
                if not start:
                    hold(pool, xg_in[parity], 16 * half, 16)
                g_.tensor_copy(index[parity][:, :], tok_tab[:, bass.ds(s, 1)]).then_inc(index_ok, 1)
                hold(pool, index_ok, s + 1)
                if not start:
                    hold(pool, xT_done, s - 1)
                g_.indirect_dma_start(out=xg[parity][:, :], out_offset=None, in_=xln_dram,
                                      in_offset=bass.IndirectOffsetOnAxis(ap=index[parity][:, 0:1], axis=0)).then_inc(xg_in[parity], 16)

            def gather_acc(s, parity):
                g_.tensor_copy(acc_index[:, :], tok_tab[:, bass.ds(s, 1)]).then_inc(acc_index_ok, 1)
                hold(pool, acc_index_ok, s + 1)
                if not (isinstance(s, int) and s == 0):
                    hold(pool, scattered, 16 * s, 16)
                g_.indirect_dma_start(out=acc[parity], out_offset=None, in_=out_rows,
                                      in_offset=bass.IndirectOffsetOnAxis(ap=acc_index[:, 0:1], axis=0)).then_inc(acc_in, 16)

            def scatter(s, parity):
                hold(pool, summed, s + 2)
                g_.tensor_copy(out_index[:, :], out_tab[:, bass.ds(s, 1)]).then_inc(out_index_ok, 1)
                hold(pool, out_index_ok, s + 1)
                g_.indirect_dma_start(out=out_rows, out_offset=bass.IndirectOffsetOnAxis(ap=out_index[:, 0:1], axis=0),
                                      in_=acc[parity], in_offset=None, bounds_check=TOK - 1, oob_is_err=False).then_inc(scattered, 16)

            pool.wait_ge(tabled, 1)
            gather(0, 0)
            gather(0, 1)
            gather_acc(0, 0)
            gather(1, 0)
            tiles = pool.value_load(tiles_i[0:1, 0:1], min_val=MIN_TILES, max_val=SLOT_TILES)
            with pool.Fori(0, TURNS) as t:
                for j in range(2):
                    with pool.If(tiles > 2 * t + 1 + j):
                        gather(t + 1 + j, 1 - j)
                        scatter(2 * t + j, j)
                        gather_acc(2 * t + 1 + j, 1 - j)

            odd = pool.value_load(odd_i[0:1, 0:1], min_val=0, max_val=1)
            with pool.If(odd > 0):
                scatter(tiles - 1, 0)
                hold(pool, xg_in[0], 8 * tiles + 24, 16)
                hold(pool, xg_in[1], 8 * tiles + 8, 16)
            with pool.Else():
                scatter(tiles - 1, 1)
                hold(pool, xg_in[0], 8 * tiles + 16, 16)
                hold(pool, xg_in[1], 8 * tiles + 16, 16)
            hold(pool, scattered, 16 * tiles, 16)

        @block.scalar
        def _(act):
            s_ = nc.scalar
            act.wait_ge(gap_ok, 1)
            s_.activation(expd[:, :], gap[:, :], ACT.Exp).then_inc(gap_exp, 1)

            def split(c, loads):
                hold(act, stage_in[c], 16 * loads, 16)
                s_.copy(w_hi[c][:, :, :], stage[c][:, :, :]).then_inc(hi_done, 1)

            def split_if(f, s, c):
                with act.If(f > 0):
                    split(c, loads_of(c, s))
                with act.Else():
                    hold(act, hi_done, splits(s, c) - 1)
                    act.sem_inc(hi_done, 1)

            def x_part(s):
                hold(act, xT_done, s + 1)
                s_.copy(xT_hi[:, :, :], xp[:, :].rearrange("p (k t) -> p k t", t=P)).then_inc(x_hi, 1)

            def step(s, y=True):
                f = act.value_load(flag_i[0:1, bass.ds(s + 1, 1)], min_val=0, max_val=1)
                for h in range(2):
                    hold(act, h_done, 4 * s + h + 1)
                    if h == 0 and y:
                        hold(act, inter_done, 2 * s)
                    s_.activation(gated[:, h, :], hp[h][:, :], ACT.Silu).then_inc(silu_done, 1)
                    split_if(f, s, h)
                hold(act, h_done, 4 * s + 3)
                split_if(f, s, 2)
                x_part(s + 1)
                hold(act, h_done, 4 * s + 4)
                split_if(f, s, 3)
                if y:
                    hold(act, y_done, s)
                f = act.value_load(flag_i[0:1, bass.ds(s, 1)], min_val=0, max_val=1)
                for h in range(2):
                    hold(act, iT_done, 2 * s + h + 1)
                    s_.copy(iT_hi[:, 4 * h:4 * h + 4, :], tp[h][:, :].rearrange("p (k t) -> p k t", t=P)).then_inc(i_hi, 1)
                for c in range(4, NC):
                    split_if(f, s, c)

            act.wait_ge(tables_ok, 1)
            for c in range(4):
                split(c, 2)
            x_part(0)
            step(0, y=False)
            tiles = act.value_load(tiles_i[0:1, 0:1], min_val=MIN_TILES, max_val=SLOT_TILES)
            with act.Fori(0, TURNS) as t:
                for j in range(1, 3):
                    with act.If(tiles > 2 * t + j):
                        step(2 * t + j)


        @block.vector
        def _(dve):
            v = nc.vector

            def over_e(a, n=NT):
                return a.unsqueeze(2).to_broadcast([P, n, NE])

            def over_t(a, n=NT):
                return a.unsqueeze(1).to_broadcast([P, n, NE])

            dve.wait_ge(consts, 1)
            source = logits
            for k in range(TOPK):
                n = 6 * k
                if k:
                    dve.wait_ge(routed, 6)
                v.tensor_reduce(top[:, k, :], source[:, :, :], axis=AX.X, op=ALU.max).then_inc(routed, 1)
                dve.wait_ge(routed, n + 1)
                v.tensor_tensor(cand[:, :, :], source[:, :, :], over_e(top[:, k, :]), ALU.is_equal).then_inc(routed, 1)
                dve.wait_ge(routed, n + 2)
                v.scalar_tensor_tensor(cand[:, :, :], cand[:, :, :], -float(NE), over_t(io8[:, :]), ALU.mult, ALU.add).then_inc(routed, 1)
                dve.wait_ge(routed, n + 3)
                v.tensor_reduce(first[:, :], cand[:, :, :], axis=AX.X, op=ALU.min).then_inc(routed, 1)
                dve.wait_ge(routed, n + 4)
                v.tensor_tensor(oh[:, k, :, :], cand[:, :, :], over_e(first[:, :]), ALU.is_equal).then_inc(routed, 1)
                if k == 0:
                    dve.wait_ge(routed, 5)
                    v.scalar_tensor_tensor(rest[:, :, :], oh[:, 0, :, :], -3e38, logits[:, :, :], ALU.mult, ALU.add).then_inc(routed, 1)
                    source = rest
            dve.wait_ge(routed, 11)
            v.tensor_tensor(gap[:, :], top[:, 1, :], top[:, 0, :], ALU.subtract).then_inc(gap_ok, 1)
            v.tensor_tensor(ohs[:, :, :], oh[:, 0, :, :], oh[:, 1, :, :], ALU.add).then_inc(ohs_ok, 1)

            dve.wait_ge(gap_exp, 1)
            v.tensor_scalar(wgt[:, 1, :], expd[:, :], 1.0, None, ALU.add).then_inc(routed, 1)
            dve.wait_ge(routed, 12)
            v.reciprocal(wgt[:, 0, :], wgt[:, 1, :]).then_inc(routed, 1)
            dve.wait_ge(routed, 13)
            v.tensor_tensor(wgt[:, 1, :], wgt[:, 0, :], expd[:, :], ALU.mult).then_inc(routed, 1)

            dve.wait_ge(consts, 12)
            dve.wait_ge(counted, 2)
            v.tensor_copy(total[:, :, :].rearrange("p e t -> p t e"), hp[1][:, 0:P].rearrange("p (t e) -> p t e", e=NE)).then_inc(routed, 1)
            dve.wait_ge(routed, 15)
            v.tensor_tensor_scan(incl[:, :, :].rearrange("p e t -> p (e t)"), segment[:, :, :].rearrange("p e t -> p (e t)"),
                                 total[:, :, :].rearrange("p e t -> p (e t)"), 0.0, ALU.mult, ALU.add).then_inc(routed, 1)
            dve.wait_ge(routed, 16)
            v.tensor_tensor(over[:, :, :], incl[:, :, NT - 1:NT].to_broadcast([P, NE, NT]),
                            io_cap[:, :].unsqueeze(1).to_broadcast([P, NE, NT]), ALU.is_gt).then_inc(routed, 1)
            dve.wait_ge(routed, 17)
            v.tensor_reduce(ntile[:, :], over[:, :, :], axis=AX.X, op=ALU.add).then_inc(routed, 1)
            dve.wait_ge(routed, 18)
            v.tensor_tensor_scan(tend[:, :], ones[:, 0:NE], ntile[:, :], 0.0, ALU.mult, ALU.add).then_inc(routed, 1)
            dve.wait_ge(routed, 19)
            v.tensor_tensor(ntile[:, :], tend[:, :], ntile[:, :], ALU.subtract).then_inc(routed, 1)
            v.tensor_tensor(incl[:, :, :], incl[:, :, :], total[:, :, :], ALU.subtract).then_inc(routed, 1)
            dve.wait_ge(routed, 21)
            v.scalar_tensor_tensor(base[:, :, :], ntile[:, :].unsqueeze(2).to_broadcast([P, NE, NT]), float(P), incl[:, :, :], ALU.mult, ALU.add).then_inc(routed, 1)
            dve.wait_ge(routed, 22)
            v.tensor_tensor(pos[:, :, :], hp[0][:, 0:P].rearrange("p (t e) -> p t e", e=NE),
                            base[:, :, :].rearrange("p e t -> p t e"), ALU.add).then_inc(routed, 1)
            dve.wait_ge(routed, 23)
            for k in range(TOPK):
                v.tensor_tensor(oh[:, k, :, :], oh[:, k, :, :], pos[:, :, :], ALU.mult).then_inc(routed, 1)
            dve.wait_ge(routed, 25)
            v.tensor_reduce(slotf[:, :, :].rearrange("p k t -> p (k t)"), oh[:, :, :, :].rearrange("p k t e -> p (k t) e"), axis=AX.X, op=ALU.add).then_inc(routed, 1)
            dve.wait_ge(routed, 26)
            v.tensor_copy(sloti[:, :, :], slotf[:, :, :]).then_inc(routed, 1)
            dve.wait_ge(routed, 27)
            slots = sloti[:, :, :].rearrange("p k t -> p (k t)")
            v.tensor_scalar(quo_i[:, :], slots, 7, None, ALU.logical_shift_right).then_inc(routed, 1)
            v.tensor_scalar(rem_i[:, :], slots, P - 1, None, ALU.bitwise_and).then_inc(routed, 1)
            dve.wait_ge(routed, 29)
            v.tensor_copy(quo[:, :], quo_i[:, :]).then_inc(routed, 1)
            v.tensor_copy(rem[:, :], rem_i[:, :]).then_inc(routed, 1)
            dve.wait_ge(routed, 31)
            tend_b = over_t(tend[:, :], ST)
            v.tensor_tensor(table8[:, :, :], tend_b, over_e(io_st[:, :], ST), ALU.is_le).then_inc(routed, 1)
            dve.wait_ge(routed, 32)
            v.tensor_reduce(texp[:, :], table8[:, :, :], axis=AX.X, op=ALU.add).then_inc(routed, 1)
            dve.wait_ge(routed, 33)
            v.tensor_scalar(texp[:, :], texp[:, :], float(NE - 1), None, ALU.min).then_inc(routed, 1)
            dve.wait_ge(routed, 34)
            v.memset(flag[:, 0:1], 1.0).then_inc(routed, 1)
            v.tensor_tensor(flag[:, 1:ST], texp[:, 1:ST], texp[:, 0:ST - 1], ALU.not_equal).then_inc(routed, 1)
            v.tensor_tensor(table8[:, :, :], over_t(io8[:, :], ST), over_e(texp[:, :], ST), ALU.is_equal).then_inc(routed, 1)
            dve.wait_ge(routed, 37)
            v.tensor_tensor(table8[:, :, :], table8[:, :, :], tend_b, ALU.mult).then_inc(routed, 1)
            dve.wait_ge(routed, 38)
            v.tensor_reduce(tend_of[:, :], table8[:, :, :], axis=AX.X, op=ALU.add).then_inc(routed, 1)
            dve.wait_ge(routed, 39)
            v.tensor_tensor(table8[:, :, :], tend_b, over_e(tend_of[:, :], ST), ALU.is_le).then_inc(routed, 1)
            dve.wait_ge(routed, 40)
            v.tensor_reduce(nxt[:, :], table8[:, :, :], axis=AX.X, op=ALU.add).then_inc(routed, 1)
            dve.wait_ge(routed, 41)
            v.tensor_scalar(nxt[:, :], nxt[:, :], float(NE - 1), None, ALU.min).then_inc(routed, 1)
            dve.wait_ge(routed, 42)
            v.tensor_copy(texp_i[:, :], texp[:, :]).then_inc(routed, 1)
            v.tensor_copy(nxt_i[:, :], nxt[:, :]).then_inc(routed, 1)
            v.tensor_copy(flag_i[:, :], flag[:, :]).then_inc(routed, 1)
            v.tensor_copy(tiles_i[:, :], tend[:, NE - 1:NE]).then_inc(routed, 1)
            dve.wait_ge(routed, 46)
            v.tensor_scalar(odd_i[:, :], tiles_i[:, :], 1, None, ALU.bitwise_and).then_inc(routed, 1)
            dve.wait_ge(routed, 47)
            dve.sem_inc(tables_ok, 1)
            v.tensor_tensor(S_lo, quo[:, :].unsqueeze(2).to_broadcast([P, TOPK * NT, ST]),
                            io_st[:, :].unsqueeze(1).to_broadcast([P, TOPK * NT, ST]), ALU.is_equal).then_inc(routed, 1)
            dve.wait_ge(routed, 48)
            for k in range(TOPK):
                part = slice(k * NT, (k + 1) * NT)
                v.tensor_tensor(S_tok[:, part, :], S_lo[:, part, :].bitcast(fp32), tokid[:, :].unsqueeze(2).to_broadcast([P, NT, ST]), ALU.mult).then_inc(routed, 1)
            dve.wait_ge(routed, 50)
            for k in range(TOPK):
                v.tensor_tensor(R[k][:, :, :], rem[:, k * NT:(k + 1) * NT].unsqueeze(2).to_broadcast([P, NT, P]),
                                io128[:, :].unsqueeze(1).to_broadcast([P, NT, P]), ALU.is_equal).then_inc(RS_ok, 1)

            def split(c, done):
                hold(dve, hi_done, done)
                v.tensor_tensor(w_lo[c][:, :, :], stage[c][:, :, :], w_hi[c][:, :, :].bitcast(fp32), ALU.subtract).then_inc(lo_done, 1)

            split(0, 1)
            dve.wait_ge(counted, 2 + TOPK)
            v.tensor_scalar(tok1[:, :], hp[2][:, 0:ST], -1.0, None, ALU.add).then_inc(routed, 1)
            dve.wait_ge(routed, 51)
            v.tensor_scalar(tok_tab[:, :], tok1[:, :], 0.0, None, ALU.max).then_inc(routed, 1)
            v.tensor_scalar(none[:, :], tok1[:, :], 0.0, float(2 * TOK), ALU.is_lt, ALU.mult).then_inc(routed, 1)
            dve.wait_ge(routed, 53)
            v.tensor_tensor(out_tab[:, :], tok1[:, :], none[:, :], ALU.add).then_inc(tabled, 1)

            def split_if(f, s, c):
                with dve.If(f > 0):
                    split(c, splits(s, c))
                with dve.Else():
                    hold(dve, lo_done, splits(s, c) - 1)
                    dve.sem_inc(lo_done, 1)

            def x_part(s):
                hold(dve, x_hi, s + 1)
                v.tensor_tensor(xT_lo[:, :, :], xp[:, :].rearrange("p (k t) -> p k t", t=P), xT_hi[:, :, :].bitcast(fp32), ALU.subtract).then_inc(x_lo, 1)

            def sum_rows(s, parity):
                hold(dve, y_done, s + 1)
                hold(dve, acc_in, 16 * s + 16, 16)
                v.scalar_tensor_tensor(acc[parity], yp[:, :], wtab[:, bass.ds(s, 1)], acc[parity], ALU.mult, ALU.add).then_inc(summed, 1)

            def step(s, parity, y=True):
                f = dve.value_load(flag_i[0:1, bass.ds(s + 1, 1)], min_val=0, max_val=1)
                split_if(f, s, 0)
                split_if(f, s, 1)
                for h in range(2):
                    hold(dve, h_done, 4 * s + 3 + h)
                    hold(dve, silu_done, 2 * s + h + 1)
                    if not (isinstance(s, int) and s == 0):
                        hold(dve, iT_done, 2 * s - 1 + h)
                    v.tensor_tensor(inter[:, h, :], hp[2 + h][:, :], gated[:, h, :], ALU.mult).then_inc(inter_done, 1)
                    if h == 0:
                        split_if(f, s, 2)
                x_part(s + 1)
                split_if(f, s, 3)
                if y:
                    sum_rows(s - 1, 1 - parity)
                f = dve.value_load(flag_i[0:1, bass.ds(s, 1)], min_val=0, max_val=1)
                for h in range(2):
                    hold(dve, i_hi, 2 * s + h + 1)
                    v.tensor_tensor(iT_lo[:, 4 * h:4 * h + 4, :], tp[h][:, :].rearrange("p (k t) -> p k t", t=P),
                                    iT_hi[:, 4 * h:4 * h + 4, :].bitcast(fp32), ALU.subtract).then_inc(i_lo, 1)
                for c in range(4, NC):
                    split_if(f, s, c)

            split(1, 2)
            def over_s(a):
                return a.rearrange("p k t -> p (k t)").unsqueeze(2).to_broadcast([P, TOPK * NT, ST])

            v.tensor_copy(wgt_hi[:, :, :], wgt[:, :, :]).then_inc(routed, 1)
            dve.wait_ge(routed, 54)
            v.tensor_tensor(wgt_lo[:, :, :], wgt[:, :, :], wgt_hi[:, :, :].bitcast(fp32), ALU.subtract).then_inc(routed, 1)
            v.tensor_tensor(S_hi, S_lo.bitcast(fp32), over_s(wgt_hi[:, :, :].bitcast(fp32)), ALU.mult).then_inc(routed, 1)
            dve.wait_ge(routed, 56)
            v.tensor_tensor(S_lo, S_lo.bitcast(fp32), over_s(wgt_lo[:, :, :]), ALU.mult).then_inc(routed, 1)
            dve.wait_ge(routed, 57)
            dve.sem_inc(RS_ok, 1)
            x_part(0)
            split(2, 3)
            split(3, 4)
            step(0, 0, y=False)
            dve.wait_ge(counted, 3 + TOPK)
            v.tensor_copy(wtab[:, :], yp[:, 0:ST]).then_inc(routed, 1)
            dve.wait_ge(routed, 58)
            v.tensor_tensor(wtab[:, :], wtab[:, :], yp[:, ST:2 * ST], ALU.add).then_inc(routed, 1)
            dve.wait_ge(routed, 59)
            dve.sem_inc(summed, 1)
            tiles = dve.value_load(tiles_i[0:1, 0:1], min_val=MIN_TILES, max_val=SLOT_TILES)
            with dve.Fori(0, TURNS) as t:
                for j in range(1, 3):
                    with dve.If(tiles > 2 * t + j):
                        step(2 * t + j, j % 2)
            odd = dve.value_load(odd_i[0:1, 0:1], min_val=0, max_val=1)
            with dve.If(odd > 0):
                sum_rows(tiles - 1, 0)
            with dve.Else():
                sum_rows(tiles - 1, 1)

        @block.tensor
        def _(pe):
            t_ = nc.tensor
            pe.wait_ge(consts, 12)
            pe.wait_ge(ohs_ok, 1)
            both = ohs[:, :, :].rearrange("p t e -> p (t e)")
            t_.matmul(hp[0][:, 0:P], ltri[:, :], both, start=True, stop=True).then_inc(counted, 1)
            t_.matmul(hp[1][:, 0:P], ones[:, :], both, start=True, stop=True).then_inc(counted, 1)
            for k in range(TOPK):
                pe.wait_ge(RS_ok, k + 1)
                for t in range(NT):
                    last = t_.matmul(hp[2][:, 0:ST], R[k][:, t, :], S_tok[:, k * NT + t, :], start=(k + t == 0), stop=(k * NT + t == TOPK * NT - 1))
                last.then_inc(counted, 1)
            def x_T(half, parity):
                s = 2 * half + parity
                pe.wait_ge(xg_in[parity], 16 * half + 16)
                if not (isinstance(s, int) and s == 0):
                    pe.wait_ge(x_lo, s)
                for k in range(KD):
                    last = t_.transpose(xp[:, k * P:(k + 1) * P], xg[parity][:, k * P:(k + 1) * P], identf[:, :])
                last.then_inc(xT_done, 1)

            def product(bank, a_hi, a_lo, ks, b_hi, b_lo, start, stop):
                for k in ks:
                    b = k % 4
                    t_.matmul(bank[:, :], a_hi[:, k, :], b_hi[:, b, :], start=(start and k == ks[0]), stop=False)
                    t_.matmul(bank[:, :], a_hi[:, k, :], b_lo[:, b, :], start=False, stop=False)
                    last = t_.matmul(bank[:, :], a_lo[:, k, :], b_hi[:, b, :], start=False, stop=(stop and k == ks[-1]))
                return last

            def inner(s):
                for c in range(4):
                    if c == 0:
                        pe.wait_ge(x_lo, s + 1)
                    ready = c + 1 if isinstance(s, int) and s == 0 else splits(s - 1, c)
                    pe.wait_ge(lo_done, ready)
                    if not (isinstance(s, int) and s == 0):
                        if c < 2:
                            pe.wait_ge(silu_done, 2 * s - 1 + c)
                        else:
                            pe.wait_ge(inter_done, 2 * s - 3 + c)
                    product(hp[c], xT_hi, xT_lo, range(4), w_hi[c], w_lo[c], True, True).then_inc(h_done, 1)

            def outer(s):
                pe.wait_ge(i_lo, 2 * s + 2)
                pe.wait_ge(summed, s + 1)
                pe.wait_ge(lo_done, splits(s, 4))
                product(yp, iT_hi, iT_lo, range(4), w_hi[4], w_lo[4], True, False)
                pe.wait_ge(lo_done, splits(s, 5))
                product(yp, iT_hi, iT_lo, range(4, 8), w_hi[5], w_lo[5], False, True).then_inc(y_done, 1)

            def inter_T(s):
                for h in range(2):
                    pe.wait_ge(inter_done, 2 * s + h + 1)
                    if not (isinstance(s, int) and s == 0):
                        pe.wait_ge(i_lo, 2 * s - 1 + h)
                    for k in range(4):
                        last = t_.transpose(tp[h][:, k * P:(k + 1) * P], inter[:, h, k * P:(k + 1) * P], identf[:, :])
                    last.then_inc(iT_done, 1)

            x_T(0, 0)
            pe.wait_ge(RS_ok, TOPK + 1)
            for k in range(TOPK):
                for t in range(NT):
                    last = t_.matmul(yp[:, 0:2 * ST], R[k][:, t, :], S_w[:, k * NT + t, :], start=(k + t == 0), stop=(k * NT + t == TOPK * NT - 1))
            last.then_inc(counted, 1)
            inner(0)
            x_T(0, 1)
            inter_T(0)
            pe.wait_ge(tables_ok, 1)
            tiles = pe.value_load(tiles_i[0:1, 0:1], min_val=MIN_TILES, max_val=SLOT_TILES)
            with pe.Fori(0, TURNS) as t:
                for j in range(2):
                    s = 2 * t + 1 + j
                    with pe.If(tiles > s):
                        inner(s)
                        x_T(t + 1, j)
                        outer(s - 1)
                        inter_T(s)
            outer(tiles - 1)


def model(nc, x, ctx_in, in_proj_w, conv_w, conv_b, x_proj_w, dt_proj_w, dt_proj_b, A_log, D, gate_w, w0, w1, wo, out):
    ctx = ExitStack()
    with ctx:
        logits = ctx.enter_context(nc.sbuf_tensor("logits", [P, NT, 8], fp32))
        bcs = nc.dram_tensor("bcs", [NB, 2 * DS, L], fp32).ap()
        xln_dram = nc.dram_tensor("xln_dram", [TOK, DI], fp32).ap()
        with nc.sbuf_tensor("xall", [P, NT, DI], fp32) as xall:
            mamba_block(nc, x, ctx_in, in_proj_w, conv_w, conv_b, x_proj_w, dt_proj_w, dt_proj_b, A_log, D, gate_w, xall, logits, bcs, xln_dram, out)
        ffn_block(nc, logits, xln_dram, w0, w1, wo, out)


_INS = (['x', 'ctx_1024'] + ['L0_xattn_' + n for n in ('in_proj_w', 'conv_w', 'conv_b', 'x_proj_w', 'dt_proj_w', 'dt_proj_b', 'A_log', 'D')]
        + ['L0_ffn_' + n for n in ('gate_kernel', 'w0_kernel', 'w1_kernel', 'wo_kernel')])


def kernel(**inputs):
    import numpy as _np
    import concourse.bacc as _bacc
    from concourse import mybir as _mybir
    from concourse.bass_utils import run_bass_kernel_spmd as _run
    nc = _bacc.Bacc("TRN2", target_bir_lowering=False, num_devices=1)
    arrays, args = {}, []
    for name in _INS:
        a = _np.ascontiguousarray(inputs[name])
        arrays[f"in_{name}_dram"] = a
        args.append(nc.dram_tensor(f"in_{name}_dram", a.shape, _mybir.dt.from_np(a.dtype), kind="ExternalInput").ap())
    args.append(nc.dram_tensor("out_0_dram", (4, 512, 512), _mybir.dt.float32, kind="ExternalOutput").ap())
    model(nc, *args)
    r = _run(nc, [arrays], core_ids=[0])
    return r.results[0]["out_0_dram"]
```
